# Optimizing a Trainium2 kernel written in Bass

```python
import numpy as np
import jax
import jax.numpy as jnp

def _softmax(x, axis=-1):
    return jax.nn.softmax(x, axis=axis)

def _gelu(x):
    return jax.nn.gelu(x, approximate=True)

def _silu(x):
    return jax.nn.silu(x)

def _sigmoid(x):
    return jax.nn.sigmoid(x)

def _layernorm(x, axis=-1, eps=1e-05):
    m = jnp.mean(x, axis=axis, keepdims=True)
    v = jnp.var(x, axis=axis, keepdims=True)
    return (x - m) / jnp.sqrt(v + eps)

def _scatter_add(tgt, idx, src, axis=0):
    return tgt.at[idx].add(src)

def _segment_sum(src, seg, n):
    return jax.ops.segment_sum(src, seg, n)
kernel_name = 'mk_vit_tower_d1_tok_img768_r4_589bff'

def setup_inputs(seed: int=0):
    np.random.seed(seed)
    _w = jnp.asarray

    def _rec_inputs():
        import jax
        import jax.numpy as jnp
        _rk = jax.random.key(seed)
        x = -0.000356955 + 1 * jax.random.normal(jax.random.fold_in(_rk, 1), (64, 3, 224, 224), jnp.float32)
        return x
    x = _rec_inputs()

    def _L0_tok_setup():
        import jax, jax.numpy as jnp
        import numpy as np
        N_PATCHES = 14
        HIDDEN_D = 192
        N_HEADS = 12
        D_HEAD = HIDDEN_D // N_HEADS
        SEQ = N_PATCHES ** 2 + 1
        INPUT_D = 3 * 16 * 16
        LN_EPS = 1e-05

        def positional_embeddings(seq_len, d):
            i = jnp.arange(seq_len, dtype=jnp.float32)[:, None]
            j = jnp.arange(d, dtype=jnp.float32)[None, :]
            even = (jnp.arange(d) % 2 == 0)[None, :]
            denom_even = jnp.power(10000.0, j / d)
            denom_odd = jnp.power(10000.0, (j - 1.0) / d)
            return jnp.where(even, jnp.sin(i / denom_even), jnp.cos(i / denom_odd))

        def _forward(images, W_map, b_map, class_token, ln_w, ln_b, Wq, bq, Wk, bk, Wv, bv):
            n = images.shape[0]
            patches = images.reshape(n, N_PATCHES ** 2, INPUT_D)
            tokens = jnp.einsum('npi,di->npd', patches, W_map) + b_map
            cls = jnp.broadcast_to(class_token[None], (n, 1, HIDDEN_D))
            tokens = jnp.concatenate([cls, tokens], axis=1)
            tokens = tokens + positional_embeddings(SEQ, HIDDEN_D)[None]
            mean = jnp.mean(tokens, axis=(-2, -1), keepdims=True)
            var = jnp.var(tokens, axis=(-2, -1), keepdims=True)
            x = (tokens - mean) / jnp.sqrt(var + LN_EPS) * ln_w + ln_b
            xh = x.reshape(n, SEQ, N_HEADS, D_HEAD)
            q = jnp.einsum('bshd,hed->bshe', xh, Wq) + bq[None, None]
            k = jnp.einsum('bshd,hed->bshe', xh, Wk) + bk[None, None]
            v = jnp.einsum('bshd,hed->bshe', xh, Wv) + bv[None, None]
            att = jax.nn.softmax(jnp.einsum('bshd,bthd->bhst', q, k) / jnp.sqrt(jnp.float32(D_HEAD)), axis=-1)
            msa = jnp.einsum('bhst,bthd->bshd', att, v).reshape(n, SEQ, HIDDEN_D)
            return tokens + msa
        key = jax.random.key(seed)
        ks = jax.random.split(key, 12)
        s = 0.02
        return {'images': jax.random.normal(ks[0], (128, 3, 224, 224), dtype=jnp.float32), 'W_map': jax.random.normal(ks[1], (HIDDEN_D, INPUT_D), dtype=jnp.float32) * s, 'b_map': jax.random.normal(ks[2], (HIDDEN_D,), dtype=jnp.float32) * s, 'class_token': jax.random.uniform(ks[3], (1, HIDDEN_D), dtype=jnp.float32), 'ln_w': jnp.ones((SEQ, HIDDEN_D), dtype=jnp.float32), 'ln_b': jnp.zeros((SEQ, HIDDEN_D), dtype=jnp.float32), 'Wq': jax.random.normal(ks[4], (N_HEADS, D_HEAD, D_HEAD), dtype=jnp.float32) * s, 'bq': jax.random.normal(ks[5], (N_HEADS, D_HEAD), dtype=jnp.float32) * s, 'Wk': jax.random.normal(ks[6], (N_HEADS, D_HEAD, D_HEAD), dtype=jnp.float32) * s, 'bk': jax.random.normal(ks[7], (N_HEADS, D_HEAD), dtype=jnp.float32) * s, 'Wv': jax.random.normal(ks[8], (N_HEADS, D_HEAD, D_HEAD), dtype=jnp.float32) * s, 'bv': jax.random.normal(ks[9], (N_HEADS, D_HEAD), dtype=jnp.float32) * s}
    _L0_tok_all = _L0_tok_setup()
    _L0_tok_in = {k: v for k, v in _L0_tok_all.items() if k in ('W_map', 'b_map', 'class_token', 'ln_w', 'ln_b', 'Wq', 'bq', 'Wk', 'bk', 'Wv', 'bv')}
    del _L0_tok_all

    def _L0_attn_setup():
        import jax, jax.numpy as jnp
        import numpy as np
        B, S, D, H = (64, 577, 192, 12)
        DH = D // H
        key = jax.random.key(seed)
        ks = jax.random.split(key, 9)
        sc = 0.02
        return {'x': jax.random.normal(ks[0], (B, S, D), jnp.float32), 'Wq': jax.random.normal(ks[1], (H, D, DH), jnp.float32) * sc, 'bq': jnp.zeros((H, DH), jnp.float32), 'Wk': jax.random.normal(ks[2], (H, D, DH), jnp.float32) * sc, 'bk': jnp.zeros((H, DH), jnp.float32), 'Wv': jax.random.normal(ks[3], (H, D, DH), jnp.float32) * sc, 'bv': jnp.zeros((H, DH), jnp.float32), 'Wo': jax.random.normal(ks[4], (D, D), jnp.float32) * sc, 'bo': jnp.zeros((D,), jnp.float32)}
    _L0_attn_all = _L0_attn_setup()
    _L0_attn_in = {k: v for k, v in _L0_attn_all.items() if k in ('Wq', 'bq', 'Wk', 'bk', 'Wv', 'bv', 'Wo', 'bo')}
    del _L0_attn_all

    def _L0_ffn_setup():
        import jax, jax.numpy as jnp
        import numpy as np
        DECAY = 0.9
        EPS = 0.01
        TOP_K = 2
        key = jax.random.key(seed)
        k1, k2, k3, k4 = jax.random.split(key, 4)
        B, S, H, I, E = (4, 512, 192, 512, 8)
        return {'hidden_states': jax.random.normal(k1, (B, S, H), jnp.float32), 'router_w': jax.random.normal(k2, (E, H), jnp.float32) * 0.02, 'w1': jax.random.normal(k3, (E, I, H), jnp.float32) * 0.02, 'w2': jax.random.normal(k4, (E, H, I), jnp.float32) * 0.02}
    _L0_ffn_all = _L0_ffn_setup()
    _L0_ffn_in = {k: v for k, v in _L0_ffn_all.items() if k in ('router_w', 'w1', 'w2')}
    del _L0_ffn_all
    return {'x': x, 'L0_tok_W_map': _L0_tok_in['W_map'], 'L0_tok_b_map': _L0_tok_in['b_map'], 'L0_tok_class_token': _L0_tok_in['class_token'], 'L0_tok_ln_w': _L0_tok_in['ln_w'], 'L0_tok_ln_b': _L0_tok_in['ln_b'], 'L0_tok_Wq': _L0_tok_in['Wq'], 'L0_tok_bq': _L0_tok_in['bq'], 'L0_tok_Wk': _L0_tok_in['Wk'], 'L0_tok_bk': _L0_tok_in['bk'], 'L0_tok_Wv': _L0_tok_in['Wv'], 'L0_tok_bv': _L0_tok_in['bv'], 'L0_attn_Wq': _L0_attn_in['Wq'], 'L0_attn_bq': _L0_attn_in['bq'], 'L0_attn_Wk': _L0_attn_in['Wk'], 'L0_attn_bk': _L0_attn_in['bk'], 'L0_attn_Wv': _L0_attn_in['Wv'], 'L0_attn_bv': _L0_attn_in['bv'], 'L0_attn_Wo': _L0_attn_in['Wo'], 'L0_attn_bo': _L0_attn_in['bo'], 'L0_ffn_router_w': _L0_ffn_in['router_w'], 'L0_ffn_w1': _L0_ffn_in['w1'], 'L0_ffn_w2': _L0_ffn_in['w2']}

def reference(x, L0_tok_W_map, L0_tok_b_map, L0_tok_class_token, L0_tok_ln_w, L0_tok_ln_b, L0_tok_Wq, L0_tok_bq, L0_tok_Wk, L0_tok_bk, L0_tok_Wv, L0_tok_bv, L0_attn_Wq, L0_attn_bq, L0_attn_Wk, L0_attn_bk, L0_attn_Wv, L0_attn_bv, L0_attn_Wo, L0_attn_bo, L0_ffn_router_w, L0_ffn_w1, L0_ffn_w2):
    import jax
    import jax.numpy as jnp

    def _L0_tok_ref(images, W_map, b_map, class_token, ln_w, ln_b, Wq, bq, Wk, bk, Wv, bv):
        import jax, jax.numpy as jnp
        import numpy as np
        N_PATCHES = 14
        HIDDEN_D = 192
        N_HEADS = 12
        D_HEAD = HIDDEN_D // N_HEADS
        SEQ = N_PATCHES ** 2 + 1
        INPUT_D = 3 * 16 * 16
        LN_EPS = 1e-05

        def positional_embeddings(seq_len, d):
            i = jnp.arange(seq_len, dtype=jnp.float32)[:, None]
            j = jnp.arange(d, dtype=jnp.float32)[None, :]
            even = (jnp.arange(d) % 2 == 0)[None, :]
            denom_even = jnp.power(10000.0, j / d)
            denom_odd = jnp.power(10000.0, (j - 1.0) / d)
            return jnp.where(even, jnp.sin(i / denom_even), jnp.cos(i / denom_odd))

        def _forward(images, W_map, b_map, class_token, ln_w, ln_b, Wq, bq, Wk, bk, Wv, bv):
            n = images.shape[0]
            patches = images.reshape(n, N_PATCHES ** 2, INPUT_D)
            tokens = jnp.einsum('npi,di->npd', patches, W_map) + b_map
            cls = jnp.broadcast_to(class_token[None], (n, 1, HIDDEN_D))
            tokens = jnp.concatenate([cls, tokens], axis=1)
            tokens = tokens + positional_embeddings(SEQ, HIDDEN_D)[None]
            mean = jnp.mean(tokens, axis=(-2, -1), keepdims=True)
            var = jnp.var(tokens, axis=(-2, -1), keepdims=True)
            x = (tokens - mean) / jnp.sqrt(var + LN_EPS) * ln_w + ln_b
            xh = x.reshape(n, SEQ, N_HEADS, D_HEAD)
            q = jnp.einsum('bshd,hed->bshe', xh, Wq) + bq[None, None]
            k = jnp.einsum('bshd,hed->bshe', xh, Wk) + bk[None, None]
            v = jnp.einsum('bshd,hed->bshe', xh, Wv) + bv[None, None]
            att = jax.nn.softmax(jnp.einsum('bshd,bthd->bhst', q, k) / jnp.sqrt(jnp.float32(D_HEAD)), axis=-1)
            msa = jnp.einsum('bhst,bthd->bshd', att, v).reshape(n, SEQ, HIDDEN_D)
            return tokens + msa
        return _forward(images, W_map, b_map, class_token, ln_w, ln_b, Wq, bq, Wk, bk, Wv, bv)

    def _L0_attn_ref(x, Wq, bq, Wk, bk, Wv, bv, Wo, bo):
        import jax, jax.numpy as jnp
        import numpy as np
        B, S, D, H = (64, 577, 192, 12)
        DH = D // H
        q = jnp.einsum('bsd,hde->bhse', x, Wq) + bq[None, :, None, :]
        k = jnp.einsum('bsd,hde->bhse', x, Wk) + bk[None, :, None, :]
        v = jnp.einsum('bsd,hde->bhse', x, Wv) + bv[None, :, None, :]
        scale = np.float32(1.0 / np.sqrt(DH))
        scores = jnp.einsum('bhqe,bhke->bhqk', q, k) * scale
        probs = jax.nn.softmax(scores, axis=2)
        ctx = jnp.einsum('bhqk,bhke->bhqe', probs, v)
        ctx = ctx.transpose(0, 2, 1, 3).reshape(x.shape[0], x.shape[1], H * DH)
        return ctx @ Wo + bo

    def _L0_ffn_ref(hidden_states, router_w, w1, w2):
        import jax, jax.numpy as jnp
        import numpy as np
        DECAY = 0.9
        EPS = 0.01
        TOP_K = 2
        B, S, H = hidden_states.shape
        E = router_w.shape[0]
        flat = hidden_states.reshape(B * S, H)
        logits = flat @ router_w.T
        probs = jax.nn.softmax(logits, axis=-1)
        topk_probs, topk_idx = jax.lax.top_k(probs, TOP_K)
        importance = jax.lax.stop_gradient(probs).sum(axis=0)
        running = jnp.ones((E,), dtype=flat.dtype)
        blended = running + (1.0 - DECAY) * (importance - running)
        running = blended + EPS
        balance = running[topk_idx]
        balanced = topk_probs / balance
        balanced = balanced / balanced.sum(axis=-1, keepdims=True)
        h = jnp.einsum('th,eih->tei', flat, w1)
        h = jax.nn.silu(h)
        outs = jnp.einsum('tei,ehi->teh', h, w2)
        sel = jnp.take_along_axis(outs, topk_idx[:, :, None], axis=1)
        combined = (sel * balanced[..., None]).sum(axis=1)
        return combined.reshape(B, S, H)
    h = _L0_tok_ref(x, L0_tok_W_map, L0_tok_b_map, L0_tok_class_token, L0_tok_ln_w, L0_tok_ln_b, L0_tok_Wq, L0_tok_bq, L0_tok_Wk, L0_tok_bk, L0_tok_Wv, L0_tok_bv)
    h = h + _L0_attn_ref(_layernorm(h, axis=-1), L0_attn_Wq, L0_attn_bq, L0_attn_Wk, L0_attn_bk, L0_attn_Wv, L0_attn_bv, L0_attn_Wo, L0_attn_bo)
    h = h + _L0_ffn_ref(_layernorm(h, axis=-1), L0_ffn_router_w, L0_ffn_w1, L0_ffn_w2)
    return h

_drawn_inputs = setup_inputs


def setup_inputs(seed=0):
    import zlib

    import numpy as np

    out = dict(_drawn_inputs(seed))
    spreads = {'L0_tok_ln_w': (1.0, 0.6),
     'L0_tok_ln_b': (0.0, 0.8),
     'L0_attn_bq': (0.0, 2.0),
     'L0_attn_bk': (0.0, 0.8),
     'L0_attn_bv': (0.0, 0.1),
     'L0_attn_bo': (0.0, 0.1)}
    factors = {'L0_tok_Wq': 8.0,
     'L0_tok_bq': 29.401,
     'L0_tok_Wk': 8.0,
     'L0_tok_bk': 64.0,
     'L0_attn_Wq': 8.0,
     'L0_attn_Wk': 8.0}
    for name, (base, spread) in spreads.items():
        noise = np.random.default_rng([zlib.crc32(name.encode()), seed]).standard_normal(out[name].shape)
        drawn = base * np.exp(spread * noise) if base else spread * noise
        out[name] = jnp.asarray(drawn.astype(out[name].dtype))
    for name, factor in factors.items():
        out[name] = (out[name] * factor).astype(out[name].dtype)
    return out
```

```python
from contextlib import ExitStack

import numpy as np

import concourse.bass as bass
from concourse import mybir

F32 = mybir.dt.float32
F32R = mybir.dt.float32r
BF16 = mybir.dt.bfloat16
I32 = mybir.dt.int32
U32 = mybir.dt.uint32
ALU = mybir.AluOpType
ACT = mybir.ActivationFunctionType
AX = mybir.AxisListType

P = 128
IMAGES = 64
PATCHES = 196
SEQ = PATCHES + 1
DIM = 192
HEADS = 12
DH = 16
IN_DIM = 768
KCH = IN_DIM // P
ROWS = (P, SEQ - P)
START = (0, P)
GROUPS = 3
PAIRS = HEADS // 2
EXPERTS = 8
FFN = 512
FCH = FFN // P
TOKENS = IMAGES * SEQ
TILES = 2 * TOKENS // P + EXPERTS - 1
TILES += TILES % 2
CAP = -(-(TOKENS + P) // P) * P
SPARE = TILES - 2 * TOKENS // P
SLOTS = EXPERTS * CAP + SPARE * P
EPS = 1e-5
SCALE = 0.25
REC = 10


class Steps:

    def __init__(self, sem, names):
        self.sem, self.names, self.seen = sem, names.split(), 0

    def step(self, name):
        assert self.names[self.seen % len(self.names)] == name, (self.names[self.seen % len(self.names)], name)
        self.seen += 1
        return 1

    def at(self, turn, name, before=0):
        return turn * len(self.names) + (1 - before) * len(self.names) + self.names.index(name) + 1


def units(prefix):
    return [f"{prefix}{u}" for u in range(2 * PAIRS)]


def group_of(pair):
    return pair // 2


def build(nc, ins, out):
    top = ExitStack()
    with top:
        def sb(name, shape, dt=F32, ctx=top):
            return ctx.enter_context(nc.sbuf_tensor(name, shape, dt))

        def sem(name):
            return top.enter_context(nc.semaphore(name))

        ps = top.enter_context(nc.psum_tensor("ps", [P, 8, 512], F32))
        xs = nc.dram_tensor("xs", [SLOTS, DIM], F32).ap()
        ys = nc.dram_tensor("ys", [TILES * P, DIM], F32).ap()
        h2d = nc.dram_tensor("h2d", [TOKENS, DIM], F32).ap()
        out_rows = out.rearrange("b s d -> (b s) d")

        rec_all = sb("rec_all", [P, IMAGES, REC])
        base = sb("slot_end", [P, EXPERTS])
        prob_sum = sb("prob_sum", [P, 2, EXPERTS])
        valid = sb("valid", [P, 2, EXPERTS])
        ones = sb("ones", [P, P])

        phase1(nc, ins, ps, xs, h2d, sb, sem, rec_all, base, prob_sum, valid, ones)
        phase234(nc, ins, ps, xs, ys, h2d, out_rows, sb, sem, rec_all, base, prob_sum, valid, ones)


def phase1(nc, ins, ps, xs, h2d, sb_top, sem, rec_all, base, prob_sum, valid, ones):
    ctx = ExitStack()
    with ctx:
        def sb(name, shape, dt=F32):
            return sb_top(name, shape, dt, ctx)

        ident = sb("ident", [P, P])
        ident_b = sb("ident_b", [P, P], BF16)
        wm = sb("wm", [P, KCH, DIM])
        addend = sb("addend", [P, 2, DIM])
        pos_emb = sb("pos_emb", [P, 2, DIM])
        ln_w = sb("ln_w", [P, 2, DIM])
        ln_b = sb("ln_b", [P, 2, DIM])
        wq1 = sb("wq1", [P, GROUPS, P])
        wk1 = sb("wk1", [P, GROUPS, P])
        wv1a = sb("wv1a", [P, DIM])
        wv1b = sb("wv1b", [DIM - P + 1, DIM])
        wq2a = sb("wq2a", [P, GROUPS, P])
        wq2b = sb("wq2b", [DIM - P, GROUPS, P])
        wk2a = sb("wk2a", [P, GROUPS, P])
        wk2b = sb("wk2b", [DIM - P, GROUPS, P])
        wv2a = sb("wv2a", [P, DIM])
        wv2b = sb("wv2b", [DIM - P + 1, DIM])
        bias = sb("bias", [P, 4, GROUPS])
        bias_q = sb("bias_q", [P, GROUPS])
        wo = sb("wo", [P, GROUPS, DIM])
        bo = sb("bo", [P, DIM])
        rw_a = sb("rw_a", [P, EXPERTS])
        rw_b = sb("rw_b", [DIM - P, EXPERTS])
        head_mask = sb("head_mask", [P, 4])
        hi_mask = sb("hi_mask", [P, 4])
        neg_lo = sb("neg_lo", [P, 1])
        mean_mat = sb("mean_mat", [P, P])
        neg_half = sb("neg_half", [P, 2])
        sel = sb("sel", [P, HEADS, P], BF16)
        iota_e = sb("iota_e", [P, 2, EXPERTS])
        tri = sb("tri", [P, P], BF16)
        ones_b = sb("ones_b", [P, P], BF16)
        sel_f = sb("sel_f", [P, HEADS, P])
        tri_f = sb("tri_f", [P, P])
        X = sb("X", [P, 2, IN_DIM])
        XT = sb("XT", [P, KCH, SEQ])
        tok = sb("tok", [P, 2, DIM])
        tok_sum = sb("tok_sum", [P, 2])
        sq = sb("sq", [P, 2])
        junk_sq = sb("junk_sq", [P, 2, DIM])
        neg_mean = sb("neg_mean", [P, 1])
        var_eps = sb("var_eps", [P, 1])
        junk2 = sb("junk2", [P, 2])
        rstd = sb("rstd", [P, 1])
        shift = sb("shift", [P, 1])
        xh = sb("xh", [P, 2, DIM])
        xTa = sb("xTa", [P, SEQ])
        xTb = sb("xTb", [DIM - P + 1, SEQ])
        q_full = sb("q_full", [P, GROUPS, SEQ])
        k_full = sb("k_full", [P, GROUPS, SEQ])
        q_hi = sb("q_hi", [P, GROUPS, SEQ], F32R)
        q_lo = sb("q_lo", [P, GROUPS, SEQ])
        k_hi = sb("k_hi", [P, GROUPS, SEQ])
        k_st = sb("k_st", [P, GROUPS, SEQ], F32R)
        k_msk = sb("k_msk", [P, HEADS, SEQ], F32R)
        qm_hi = sb("qm_hi", [P, HEADS, SEQ], F32R)
        qm_lo = sb("qm_lo", [P, HEADS, SEQ], F32R)
        va = sb("va", [P, HEADS, 2, 32])
        nmax = sb("nmax", [P, 2, HEADS])
        nm = sb("nm", [P, 2, 2 * HEADS], BF16)
        nmT = sb("nmT", [P, SEQ], BF16)
        PA = sb("PA", [P, 2, 2, 4, SEQ])
        OT = sb("OT", [P, GROUPS, SEQ])
        rzA = sb("rzA", [P, 2, HEADS])
        on = sb("on", [P, 2, DIM])
        h1 = sb("h1", [P, 2, DIM])
        h1b = sb("h1b", [P, 2, DIM])
        st2 = sb("st2", [P, 2, 6])
        mv2 = sb("mv2", [P, 2, 2])
        ve2 = sb("ve2", [P, 2])
        rstd2 = sb("rstd2", [P, 2])
        shift2 = sb("shift2", [P, 2])
        x2 = sb("x2", [P, 2, DIM])
        x2Ta = sb("x2Ta", [P, SEQ])
        x2Tb = sb("x2Tb", [DIM - P + 1, SEQ])
        q2_full = sb("q2_full", [P, GROUPS, SEQ])
        k2_full = sb("k2_full", [P, GROUPS, SEQ])
        q2_hi = sb("q2_hi", [P, GROUPS, SEQ])
        q2_lo = sb("q2_lo", [P, GROUPS, SEQ])
        k2_hi = sb("k2_hi", [P, GROUPS, SEQ])
        k2_st = sb("k2_st", [P, GROUPS, SEQ], F32R)
        q2m_hi = sb("q2m_hi", [P, HEADS, SEQ], F32R)
        q2m_lo = sb("q2m_lo", [P, HEADS, SEQ], F32R)
        v2 = sb("v2", [P, HEADS, 2, DH])
        v2s = sb("v2s", [P, HEADS, 2, 32])
        nmax2 = sb("nmax2", [P, 2, HEADS])
        Z2 = sb("Z2", [P, HEADS, 2])
        rz2 = sb("rz2", [P, HEADS, 2])
        PB = sb("PB", [P, 2, 2, 4, SEQ])
        CT = sb("CT", [P, GROUPS, SEQ])
        h2 = sb("h2", [P, 2, DIM])
        st3 = sb("st3", [P, 2, 6])
        mv3 = sb("mv3", [P, 2, 2])
        ve3 = sb("ve3", [P, 2])
        rstd3 = sb("rstd3", [P, 2])
        shift3 = sb("shift3", [P, 2])
        x3 = sb("x3", [P, 2, DIM])
        x3Ta = sb("x3Ta", [P, SEQ])
        x3Tb = sb("x3Tb", [DIM - P, SEQ])
        lg = sb("lg", [P, 2, EXPERTS])
        top8 = sb("top8", [P, 2, 8])
        top_i = sb("top_i", [P, 2, 8], U32)
        top_f = sb("top_f", [P, 2, 2])
        hot = sb("hot", [P, 2, 2, EXPERTS])
        hots = sb("hots", [P, 2, EXPERTS], BF16)
        slot = sb("slot", [P, 2, EXPERTS])
        picked = sb("picked", [P, 2, 2, EXPERTS])
        rec = sb("rec", [P, REC])
        slot_u = sb("slot_u", [P, 4], U32)
        lgm = sb("lgm", [P, 2, EXPERTS])
        ex = sb("ex", [P, 2, EXPERTS])
        exs = sb("exs", [P, 2])
        exr = sb("exr", [P, 2])
        prob = sb("prob", [P, 2, EXPERTS])
        held = sb("held", [P, 1])
        held_p = sb("held_p", [P, 1])
        nothing = sb("nothing", [P, DIM])

        loads = sem("loads")
        zeroed = sem("zeroed")
        set_up = sem("set_up")
        x_in = sem("x_in")
        h2_out = sem("h2_out")
        rows_out = sem("rows_out")

        A_PE = Steps(sem("a_pe"), "xt0 xt1 xt2 tok mean var xT qk0 qk1 qk2 v0 v1 "
                     + " ".join(units("sa")) + " nmT " + " ".join(units("sb")[:8])
                     + " o0 " + " ".join(units("sb")[8:]) + " o1 o2 oT0 oT1")
        A_ACT = Steps(sem("a_act"), "xt0 xt2 sq0 sq1 xn xTa xTb q0 q1 q2 k0 k1 k2 v0 v1 "
                      + " ".join(units("exp")[:8]) + " ot0 " + " ".join(units("exp")[8:]) + " ot1 ot2")
        A_DVE = Steps(sem("a_dve"), "xt1 tok0 tok1 nmean var shift lnw lnb q_hi q_lo k_hi k_st "
                      + " ".join(units("max")) + " nmh nml nmT rz0 on0 h0 rz1 on1 h1")
        A_POOL = Steps(sem("a_pool"), "rstd km0 km1 km2 qh0 ql0 qh1 ql1 qh2 ql2")
        B_PE = Steps(sem("b_pe"), "xT qk0 qk1 qk2 v " + " ".join(units("s")[:8]) + " c0 "
                     + " ".join(units("s")[8:]) + " c1 c2 wo x3T logits rank")
        B_ACT = Steps(sem("b_act"), "xTa xTb q0 q1 q2 k0 k1 k2 v0 v1 "
                      + " ".join(units("exp")[:8]) + " ct0 " + " ".join(units("exp")[8:])
                      + " ct1 ct2 x3Ta x3Tb ex")
        B_DVE = Steps(sem("b_dve"), "bs0 bs1 ba0 ba1 ve shift x20 x21 q_hi q_lo k_hi k_st "
                      + " ".join(units("max")[:4]) + " rz0 vs0 " + " ".join(units("max")[4:8]) + " rz1 vs1 "
                      + " ".join(units("max")[8:]) + " rz2 vs2 h20 h21 bs30 bs31 ba30 ba31 ve3 shift3 x30 x31 "
                      "lg0 lg1 top0 top1 ti0 ti1 topf diff hot0 hot1 hots lgm slot pick0 pos0 pick1 pos1 base "
                      "slotu recf rec exs exr prob sum")
        B_POOL = Steps(sem("b_pool"), "h1b rstd qh0 ql0 qh1 ql1 qh2 ql2 rstd3")

        def tA(n):
            return ps[:, 2 + n % 2, :]

        def tB(n):
            return ps[:, 6 + n % 2, :]

        A_EMPTY = [(A_ACT, "xt0"), (A_DVE, "xt1"), (A_ACT, "xt2"), (A_DVE, "tok1"), (A_DVE, "nmean"), (A_DVE, "var"),
                   (A_ACT, "xTb"), (A_ACT, "q1"), (A_ACT, "k0"), (A_ACT, "k2"), (A_ACT, "v0"), (A_ACT, "v1"),
                   (A_DVE, "nmT"), (A_ACT, "ot0"), (A_ACT, "ot1"), (A_ACT, "ot2"), (A_DVE, "on0"), (A_DVE, "on1")]
        B_EMPTY = [(B_ACT, "xTb"), (B_ACT, "q1"), (B_ACT, "k0"), (B_ACT, "k2"), (B_ACT, "v1"), (B_ACT, "ct0"),
                   (B_ACT, "ct1"), (B_ACT, "ct2"), (B_DVE, "h21"), (B_ACT, "x3Tb"), (B_DVE, "lg1"), (B_DVE, "base")]

        def empty(eng, table, n, i):
            steps, name = table[(n - 2) % len(table)]
            eng.wait_ge(steps.sem, steps.at(i, name, before=1 if n < 2 else 0))

        block = ctx.enter_context(nc.Block())
        W = ins
        n_loads = []

        @block.sync
        def _(sp):
            def load(dst, src):
                sp.dma_start(dst, src).then_inc(loads, 16)
                n_loads.append(1)

            sp.wait_ge(zeroed, 1)
            for dst, name in ((ident, "ident"), (wm, "wm"), (wq1, "wq1"), (wk1, "wk1"),
                              (wv1a, "wv1a"), (wv1b, "wv1b"), (wq2a, "wq2a"), (wq2b, "wq2b"), (wk2a, "wk2a"),
                              (wk2b, "wk2b"), (wv2a, "wv2a"), (wv2b, "wv2b"), (bias, "bias"), (wo, "wo"),
                              (rw_a, "rw_a"), (rw_b, "rw_b"), (head_mask, "head_mask"), (hi_mask, "hi_mask"),
                              (neg_lo, "neg_lo"), (sel_f, "sel"), (iota_e, "iota_e"), (tri_f, "tri"),
                              (valid, "valid"), (base, "first_slot")):
                load(dst[:], W[name][:])
            load(bo[:, :], W["bo"].to_broadcast([P, DIM]))
            for c in range(2):
                s0, n = START[c], ROWS[c]
                load(pos_emb[0:n, c, :], W["pos_emb"][s0:s0 + n, :])
                load(ln_w[0:n, c, :], W["ln_w"][s0:s0 + n, :])
                load(ln_b[0:n, c, :], W["ln_b"][s0:s0 + n, :])
                load(addend[:, c, :], W["b_map"].to_broadcast([P, DIM]))
            sp.wait_ge(loads, 16 * len(n_loads))
            load(addend[0:1, 0, :], W["cls"][:, :])

            def load_x(i):
                sp.wait_ge(A_PE.sem, A_PE.at(i, "xt2", before=1))
                img = W["x"][bass.ds(i, 1)].rearrange("b p k -> (b p) k")
                sp.dma_start(X[1:P, 0, :], img[0:P - 1, :]).then_inc(x_in, 16)
                sp.dma_start(X[0:ROWS[1], 1, :], img[P - 1:PATCHES, :]).then_inc(x_in, 16)

            def store_h2(i):
                sp.wait_ge(B_DVE.sem, B_DVE.at(i, "h21"))
                for c in range(2):
                    sp.dma_start(h2d[bass.ds(i * SEQ + START[c], ROWS[c]), :], h2[0:ROWS[c], c, :])\
                        .then_inc(h2_out, 16)

            load_x(0)
            load_x(1)
            with sp.Fori(1, IMAGES - 1) as i:
                load_x(i + 1)
                store_h2(i - 1)
            store_h2(IMAGES - 2)
            store_h2(IMAGES - 1)
            sp.wait_ge(h2_out, 32 * IMAGES + 32)

        @block.gpsimd
        def _(pool):
            pool.sem_inc(A_POOL.sem, len(A_POOL.names))
            pool.sem_inc(B_POOL.sem, len(B_POOL.names))
            for t in (nothing, X, tok, tok_sum, sq, ln_w, ln_b, pos_emb, xTb, x2Tb, nmax, nmT, PA, PB, h1, h2, mv2, mv3,
                      v2, v2s, va, lg, prob_sum):
                pool.memset(t[:], 0.0)
            pool.memset(Z2[:], 1.0)
            pool.memset(ones[:], 1.0)
            pool.memset(ones_b[:], 1.0)
            pool.memset(neg_half[:], -0.5)
            pool.memset(mean_mat[:], 1.0 / (SEQ * DIM)).then_inc(zeroed, 1)
            pool.wait_ge(set_up, 9)
            for t in range(SPARE):
                pool.dma_start(xs[EXPERTS * CAP + t * P:EXPERTS * CAP + (t + 1) * P, :], nothing[:, :])\
                    .then_inc(rows_out, 16)

            def mask_head(dst, src, mask, g):
                return pool.tensor_tensor(dst[:, 4 * g:4 * g + 4, :],
                                          src[:, g, :].unsqueeze(1).to_broadcast([P, 4, SEQ]),
                                          mask[:, :].unsqueeze(2).to_broadcast([P, 4, SEQ]), ALU.mult)

            def a_rstd(i):
                pool.wait_ge(A_DVE.sem, A_DVE.at(i, "var"))
                pool.tensor_tensor(rstd[:, :], var_eps[:, :], neg_half[:, 0:1], ALU.pow)\
                    .then_inc(A_POOL.sem, A_POOL.step("rstd"))

            def a_masks(i):
                pool.wait_ge(A_DVE.sem, A_DVE.at(i, "k_st"))
                pool.wait_ge(A_PE.sem, A_PE.at(i, "sb11", before=1))
                for g in range(GROUPS):
                    mask_head(k_msk, k_hi, hi_mask, g).then_inc(A_POOL.sem, A_POOL.step(f"km{g}"))
                for g in range(GROUPS):
                    mask_head(qm_hi, q_hi[:, :, :].bitcast(F32), head_mask, g).then_inc(A_POOL.sem, A_POOL.step(f"qh{g}"))
                    mask_head(qm_lo, q_lo, hi_mask, g).then_inc(A_POOL.sem, A_POOL.step(f"ql{g}"))

            def b_residual(i):
                pool.wait_ge(A_DVE.sem, A_DVE.at(i, "h1"))
                pool.wait_ge(B_DVE.sem, B_DVE.at(i, "h21", before=1))
                pool.tensor_tensor(h1b[:, :, :], h1[:, :, :], bo[:, :].unsqueeze(1).to_broadcast([P, 2, DIM]),
                                   ALU.add).then_inc(B_POOL.sem, B_POOL.step("h1b"))

            def b_rstd(i):
                pool.wait_ge(B_DVE.sem, B_DVE.at(i, "ve"))
                pool.tensor_tensor(rstd2[:, :], ve2[:, :], neg_half[:, :], ALU.pow)\
                    .then_inc(B_POOL.sem, B_POOL.step("rstd"))

            def b_masks(i):
                pool.wait_ge(B_DVE.sem, B_DVE.at(i, "q_lo"))
                pool.wait_ge(B_PE.sem, B_PE.at(i, "s11", before=1))
                for g in range(GROUPS):
                    mask_head(q2m_hi, q2_hi, head_mask, g).then_inc(B_POOL.sem, B_POOL.step(f"qh{g}"))
                    mask_head(q2m_lo, q2_lo, hi_mask, g).then_inc(B_POOL.sem, B_POOL.step(f"ql{g}"))

            def b_rstd3(i):
                pool.wait_ge(B_DVE.sem, B_DVE.at(i, "ve3"))
                pool.tensor_tensor(rstd3[:, :], ve3[:, :], neg_half[:, :], ALU.pow)\
                    .then_inc(B_POOL.sem, B_POOL.step("rstd3"))

            def b_scatter(i):
                pool.wait_ge(B_DVE.sem, B_DVE.at(i, "slotu"))
                pool.tensor_tensor(held_p[:, :], neg_half[:, 0:1], neg_half[:, 0:1], ALU.add)
                for k in range(2):
                    for c in range(2):
                        n = ROWS[c]
                        pool.indirect_dma_start(
                            out=xs[:, :],
                            out_offset=bass.IndirectOffsetOnAxis(ap=slot_u[0:n, 2 * k + c:2 * k + c + 1], axis=0),
                            in_=x3[0:n, c, :], in_offset=None).then_inc(rows_out, 16)

            a_rstd(0)
            a_masks(0)
            with pool.Fori(1, IMAGES) as i:
                b_residual(i - 1)
                b_rstd(i - 1)
                b_masks(i - 1)
                a_rstd(i)
                a_masks(i)
                b_rstd3(i - 1)
                b_scatter(i - 1)
            for step in (b_residual, b_rstd, b_masks, b_rstd3, b_scatter):
                step(IMAGES - 1)
            pool.wait_ge(rows_out, 64 * IMAGES + 16 * SPARE)

        @block.tensor
        def _(pe):
            pe.sem_inc(A_PE.sem, len(A_PE.names))
            pe.sem_inc(B_PE.sem, len(B_PE.names))
            pe.wait_ge(set_up, 9)

            def a_embed(i):
                pe.wait_ge(x_in, i * 32 + 32)
                for n in range(3):
                    empty(pe, A_EMPTY, n, i)
                    for kk in range(2):
                        k = 2 * n + kk
                        for c in range(2):
                            r, o = ROWS[c], kk * SEQ + START[c]
                            mm = pe.transpose(tA(n)[:, o:o + r], X[0:r, c, k * P:(k + 1) * P], ident[0:r, 0:r])
                    mm.then_inc(A_PE.sem, A_PE.step(f"xt{n}"))
                empty(pe, A_EMPTY, 3, i)
                pe.wait_ge(A_ACT.sem, A_ACT.at(i, "xt2"))
                for c in range(2):
                    for k in range(KCH):
                        mm = pe.matmul(tA(3)[0:ROWS[c], c * DIM:(c + 1) * DIM], XT[:, k, START[c]:START[c] + ROWS[c]],
                                       wm[:, k, :], start=(k == 0), stop=(k == KCH - 1))
                mm.then_inc(A_PE.sem, A_PE.step("tok"))

            def a_mean(i):
                empty(pe, A_EMPTY, 4, i)
                pe.wait_ge(A_DVE.sem, A_DVE.at(i, "tok1"))
                pe.matmul(tA(4)[:, 0:2], mean_mat[:, :], tok_sum[:, :], start=True, stop=True)\
                    .then_inc(A_PE.sem, A_PE.step("mean"))

            def a_var(i):
                empty(pe, A_EMPTY, 5, i)
                pe.wait_ge(A_ACT.sem, A_ACT.at(i, "sq1"))
                pe.matmul(tA(5)[:, 0:2], mean_mat[:, :], sq[:, :], start=True, stop=True)\
                    .then_inc(A_PE.sem, A_PE.step("var"))

            def turn(t, src):
                for f, (lo, hi) in enumerate(((0, P), (P, DIM))):
                    for c in range(2):
                        r, o = ROWS[c], f * SEQ + START[c]
                        mm = pe.transpose(t[0:hi - lo, o:o + r], src[0:r, c, lo:hi], ident[0:r, 0:r])
                return mm

            def a_project(i):
                empty(pe, A_EMPTY, 6, i)
                pe.wait_ge(A_DVE.sem, A_DVE.at(i, "lnb"))
                turn(tA(6), xh).then_inc(A_PE.sem, A_PE.step("xT"))
                pe.wait_ge(A_ACT.sem, A_ACT.at(i, "xTb"))
                for n in range(3):
                    empty(pe, A_EMPTY, 7 + n, i)
                    for kk in range(2):
                        m = 2 * n + kk
                        w, g = (wq1, m) if m < GROUPS else (wk1, m - GROUPS)
                        o = tA(7 + n)[:, kk * SEQ:(kk + 1) * SEQ]
                        if g < 2:
                            mm = pe.matmul(o, w[:, g, :], xTa[:, :], start=True, stop=True)
                        else:
                            mm = pe.matmul(o, w[0:DIM - P, g, :], xTb[0:DIM - P, :], start=True, stop=True)
                    mm.then_inc(A_PE.sem, A_PE.step(f"qk{n}"))
                for c in range(2):
                    empty(pe, A_EMPTY, 10 + c, i)
                    s = slice(START[c], START[c] + ROWS[c])
                    pe.matmul(tA(10 + c)[0:ROWS[c], 0:DIM], xTa[:, s], wv1a[:, :], start=True, stop=False)
                    pe.matmul(tA(10 + c)[0:ROWS[c], 0:DIM], xTb[:, s], wv1b[:, :], start=False, stop=True)\
                        .then_inc(A_PE.sem, A_PE.step(f"v{c}"))

            def a_rough(i, u):
                p, c = divmod(u, 2)
                g = group_of(p)
                if u == 0:
                    pe.wait_ge(A_POOL.sem, A_POOL.at(i, "km2"))
                    pe.wait_ge(A_DVE.sem, A_DVE.at(i, "k_st"))
                if u < 2:
                    pe.wait_ge(A_ACT.sem, A_ACT.at(i, f"exp{10 + c}", before=1))
                else:
                    pe.wait_ge(A_DVE.sem, A_DVE.at(i, f"max{u - 2}"))
                pe.matmul(ps[0:ROWS[c], c, 0:2 * SEQ], q_hi[:, g, START[c]:START[c] + ROWS[c]],
                          k_msk[:, 2 * p:2 * p + 2, :].rearrange("p a b -> p (a b)"), start=True, stop=True)\
                    .then_inc(A_PE.sem, A_PE.step(f"sa{u}"))

            def a_max_rows(i):
                empty(pe, A_EMPTY, 12, i)
                pe.wait_ge(A_DVE.sem, A_DVE.at(i, "nml"))
                tb = tA(12).bitcast(BF16)
                for c in range(2):
                    mm = pe.transpose(tb[0:2 * HEADS, START[c]:START[c] + ROWS[c]], nm[0:ROWS[c], c, :],
                                      ident_b[0:ROWS[c], 0:ROWS[c]])
                mm.then_inc(A_PE.sem, A_PE.step("nmT"))

            def a_scores(i, u):
                p, c = divmod(u, 2)
                g = group_of(p)
                if u == 0:
                    pe.wait_ge(A_DVE.sem, A_DVE.at(i, "nmT"))
                    pe.wait_ge(A_POOL.sem, A_POOL.at(i, "ql2"))
                if u < 2:
                    pe.wait_ge(A_DVE.sem, A_DVE.at(i, f"max{10 + c}"))
                else:
                    pe.wait_ge(A_ACT.sem, A_ACT.at(i, f"exp{u - 2}"))
                r = ROWS[c]
                o = ps[0:r, c, 0:2 * SEQ]
                k = k_st[:, g, START[c]:START[c] + r]
                for a in range(2):
                    pe.matmul(ps[0:r, c, a * SEQ:(a + 1) * SEQ], sel[:, 2 * p + a, 0:r], nmT[:, :],
                              start=(a == 0), stop=False, skip_group_check=True)
                pe.matmul(o, k, qm_hi[:, 2 * p:2 * p + 2, :].rearrange("p a b -> p (a b)"), start=False, stop=False,
                          skip_group_check=True)
                mm = pe.matmul(o, k, qm_lo[:, 2 * p:2 * p + 2, :].rearrange("p a b -> p (a b)"), start=False, stop=True,
                               skip_group_check=True)
                mm.then_inc(A_PE.sem, A_PE.step(f"sb{u}"))

            def a_values(i, g):
                n = 13 + g
                empty(pe, A_EMPTY, n, i)
                pe.wait_ge(A_ACT.sem, A_ACT.at(i, f"exp{4 * g + 3}"))
                for c in range(2):
                    for j in range(4):
                        mm = pe.matmul(tA(n)[32 * j:32 * j + 32, 0:SEQ], va[:, 4 * g + j, c, :], PA[:, g % 2, c, j, :],
                                       start=(c == 0), stop=(c == 1), tile_position=(0, 32 * j))
                mm.then_inc(A_PE.sem, A_PE.step(f"o{g}"))

            def a_turn_back(i):
                pe.wait_ge(A_ACT.sem, A_ACT.at(i, "ot2"))
                for c in range(2):
                    empty(pe, A_EMPTY, 16 + c, i)
                    for g in range(GROUPS):
                        mm = pe.transpose(tA(16 + c)[0:ROWS[c], g * P:(g + 1) * P],
                                          OT[:, g, START[c]:START[c] + ROWS[c]], ident[:, :])
                    mm.then_inc(A_PE.sem, A_PE.step(f"oT{c}"))

            def b_project(i):
                empty(pe, B_EMPTY, 0, i)
                pe.wait_ge(B_DVE.sem, B_DVE.at(i, "x21"))
                turn(tB(0), x2).then_inc(B_PE.sem, B_PE.step("xT"))
                pe.wait_ge(B_ACT.sem, B_ACT.at(i, "xTb"))
                for n in range(3):
                    empty(pe, B_EMPTY, 1 + n, i)
                    for kk in range(2):
                        m = 2 * n + kk
                        wa, wb, g = (wq2a, wq2b, m) if m < GROUPS else (wk2a, wk2b, m - GROUPS)
                        o = tB(1 + n)[:, kk * SEQ:(kk + 1) * SEQ]
                        pe.matmul(o, wa[:, g, :], x2Ta[:, :], start=True, stop=False)
                        mm = pe.matmul(o, wb[:, g, :], x2Tb[0:DIM - P, :], start=False, stop=True)
                    mm.then_inc(B_PE.sem, B_PE.step(f"qk{n}"))
                empty(pe, B_EMPTY, 4, i)
                for c in range(2):
                    s = slice(START[c], START[c] + ROWS[c])
                    o = tB(4)[0:ROWS[c], c * DIM:(c + 1) * DIM]
                    pe.matmul(o, x2Ta[:, s], wv2a[:, :], start=True, stop=False)
                    mm = pe.matmul(o, x2Tb[:, s], wv2b[:, :], start=False, stop=True)
                mm.then_inc(B_PE.sem, B_PE.step("v"))

            def b_scores(i, u):
                p, c = divmod(u, 2)
                g = group_of(p)
                if u == 0:
                    pe.wait_ge(B_DVE.sem, B_DVE.at(i, "k_st"))
                if u % 4 == 0:
                    pe.wait_ge(B_POOL.sem, B_POOL.at(i, f"ql{g}"))
                if u < 2:
                    pe.wait_ge(B_ACT.sem, B_ACT.at(i, f"exp{10 + c}", before=1))
                else:
                    pe.wait_ge(B_ACT.sem, B_ACT.at(i, f"exp{u - 2}"))
                o = ps[0:ROWS[c], 4 + c, 0:2 * SEQ]
                k = k2_st[:, g, START[c]:START[c] + ROWS[c]]
                pe.matmul(o, k, q2m_hi[:, 2 * p:2 * p + 2, :].rearrange("p a b -> p (a b)"), start=True, stop=False)
                pe.matmul(o, k, q2m_lo[:, 2 * p:2 * p + 2, :].rearrange("p a b -> p (a b)"), start=False, stop=True)\
                    .then_inc(B_PE.sem, B_PE.step(f"s{u}"))

            def b_values(i, g):
                n = 5 + g
                empty(pe, B_EMPTY, n, i)
                pe.wait_ge(B_ACT.sem, B_ACT.at(i, f"exp{4 * g + 3}"))
                pe.wait_ge(B_DVE.sem, B_DVE.at(i, f"vs{g}"))
                for c in range(2):
                    for j in range(4):
                        mm = pe.matmul(tB(n)[32 * j:32 * j + 32, 0:SEQ], v2s[:, 4 * g + j, c, :], PB[:, g % 2, c, j, :],
                                       start=(c == 0), stop=(c == 1), tile_position=(0, 32 * j))
                mm.then_inc(B_PE.sem, B_PE.step(f"c{g}"))

            def b_out(i):
                empty(pe, B_EMPTY, 8, i)
                pe.wait_ge(B_ACT.sem, B_ACT.at(i, "ct2"))
                for c in range(2):
                    for g in range(GROUPS):
                        mm = pe.matmul(tB(8)[0:ROWS[c], c * DIM:(c + 1) * DIM], CT[:, g, START[c]:START[c] + ROWS[c]],
                                       wo[:, g, :], start=(g == 0), stop=(g == GROUPS - 1))
                mm.then_inc(B_PE.sem, B_PE.step("wo"))

            def b_logits(i):
                empty(pe, B_EMPTY, 9, i)
                pe.wait_ge(B_DVE.sem, B_DVE.at(i, "x31"))
                turn(tB(9), x3).then_inc(B_PE.sem, B_PE.step("x3T"))
                empty(pe, B_EMPTY, 10, i)
                pe.wait_ge(B_ACT.sem, B_ACT.at(i, "x3Tb"))
                for c in range(2):
                    s = slice(START[c], START[c] + ROWS[c])
                    o = tB(10)[0:ROWS[c], c * EXPERTS:(c + 1) * EXPERTS]
                    pe.matmul(o, x3Ta[:, s], rw_a[:, :], start=True, stop=False)
                    mm = pe.matmul(o, x3Tb[:, s], rw_b[:, :], start=False, stop=True)
                mm.then_inc(B_PE.sem, B_PE.step("logits"))

            def b_rank(i):
                empty(pe, B_EMPTY, 11, i)
                pe.wait_ge(B_DVE.sem, B_DVE.at(i, "hots"))
                t, E = tB(11), EXPERTS
                pe.matmul(t[:, 0:E], tri[:, :], hots[:, 0, :], start=True, stop=True)
                pe.matmul(t[:, E:2 * E], tri[:, :], hots[:, 1, :], start=True, stop=False)
                pe.matmul(t[:, E:2 * E], ones_b[:, :], hots[:, 0, :], start=False, stop=True)
                pe.matmul(t[:, 2 * E:3 * E], ones_b[:, :], hots[:, 0, :], start=True, stop=False)
                pe.matmul(t[:, 2 * E:3 * E], ones_b[:, :], hots[:, 1, :], start=False, stop=True)\
                    .then_inc(B_PE.sem, B_PE.step("rank"))

            def stage_a(i):
                a_embed(i)
                a_mean(i)
                a_var(i)
                a_project(i)
                for u in range(12):
                    a_rough(i, u)
                a_max_rows(i)
                for u in range(12):
                    a_scores(i, u)
                    if u == 7:
                        a_values(i, 0)
                a_values(i, 1)
                a_values(i, 2)
                a_turn_back(i)

            def stage_b(i):
                b_project(i)
                for u in range(12):
                    b_scores(i, u)
                    if u == 7:
                        b_values(i, 0)
                b_values(i, 1)
                b_values(i, 2)
                b_out(i)
                b_logits(i)
                b_rank(i)

            stage_a(0)
            with pe.Fori(1, IMAGES) as i:
                b = i - 1
                a_embed(i)
                b_project(b)
                a_mean(i)
                b_scores(b, 0)
                b_scores(b, 1)
                a_var(i)
                for u in range(2, 6):
                    b_scores(b, u)
                a_project(i)
                b_scores(b, 6)
                b_scores(b, 7)
                b_values(b, 0)
                for u in range(8, 12):
                    a_rough(i, 2 * (u - 8))
                    b_scores(b, u)
                    a_rough(i, 2 * (u - 8) + 1)
                b_values(b, 1)
                a_rough(i, 8)
                a_rough(i, 9)
                b_values(b, 2)
                a_rough(i, 10)
                a_rough(i, 11)
                b_out(b)
                a_max_rows(i)
                for u in range(12):
                    a_scores(i, u)
                    if u == 5:
                        b_logits(b)
                    if u == 7:
                        a_values(i, 0)
                    if u == 10:
                        b_rank(b)
                a_values(i, 1)
                a_values(i, 2)
                a_turn_back(i)
            stage_b(IMAGES - 1)

        @block.scalar
        def _(act):
            act.sem_inc(A_ACT.sem, len(A_ACT.names))
            act.sem_inc(B_ACT.sem, len(B_ACT.names))
            act.wait_ge(set_up, 9)

            def a_xt(i, n):
                act.wait_ge(A_PE.sem, A_PE.at(i, f"xt{n}"))
                act.copy(XT[:, 2 * n:2 * n + 2, :], tA(n)[:, 0:2 * SEQ].rearrange("p (a b) -> p a b", a=2))\
                    .then_inc(A_ACT.sem, A_ACT.step(f"xt{n}"))

            def a_squares(i):
                act.wait_ge(A_DVE.sem, A_DVE.at(i, "nmean"))
                for c in range(2):
                    r = ROWS[c]
                    act.activation(junk_sq[0:r, c, :], tok[0:r, c, :], ACT.Square, bias=neg_mean[0:r, :],
                                   accum_out=sq[0:r, c:c + 1]).then_inc(A_ACT.sem, A_ACT.step(f"sq{c}"))

            def a_normal(i):
                act.wait_ge(A_DVE.sem, A_DVE.at(i, "shift"))
                act.activation(xh[:, :, :], tok[:, :, :], ACT.Identity, bias=shift[:, :], scale=rstd[:, :])\
                    .then_inc(A_ACT.sem, A_ACT.step("xn"))

            def columns(steps, t, a, b, names):
                act.copy(a, t[:, 0:SEQ]).then_inc(steps.sem, steps.step(names[0]))
                act.copy(b, t[0:DIM - P, SEQ:2 * SEQ]).then_inc(steps.sem, steps.step(names[1]))

            def a_operands(i):
                act.wait_ge(A_PE.sem, A_PE.at(i, "xT"))
                columns(A_ACT, tA(6), xTa[:, :], xTb[0:DIM - P, :], ("xTa", "xTb"))
                for m in range(2 * GROUPS):
                    n = m // 2
                    dst, j, g, name = (q_full, 0, m, f"q{m}") if m < GROUPS else (k_full, 1, m - GROUPS, f"k{m - GROUPS}")
                    if m % 2 == 0:
                        act.wait_ge(A_PE.sem, A_PE.at(i, f"qk{n}"))
                    act.activation(dst[:, g, :], tA(7 + n)[:, (m % 2) * SEQ:(m % 2 + 1) * SEQ], ACT.Identity,
                                   bias=bias[:, j, g:g + 1]).then_inc(A_ACT.sem, A_ACT.step(name))
                for c in range(2):
                    r = ROWS[c]
                    act.wait_ge(A_PE.sem, A_PE.at(i, f"v{c}"))
                    act.copy(va[0:r, :, c, 0:DH], tA(10 + c)[0:r, 0:DIM].rearrange("p (h d) -> p h d", h=HEADS))\
                        .then_inc(A_ACT.sem, A_ACT.step(f"v{c}"))

            def a_exp(i, u):
                p, c = divmod(u, 2)
                g, r = group_of(p), ROWS[c]
                act.wait_ge(A_PE.sem, A_PE.at(i, f"sb{u}"))
                if u == 8:
                    act.wait_ge(A_PE.sem, A_PE.at(i, "o0"))
                act.activation(PA[0:r, g % 2, c, 2 * (p % 2):2 * (p % 2) + 2, :],
                               ps[0:r, c, 0:2 * SEQ].rearrange("p (a b) -> p a b", a=2), ACT.Exp, scale=SCALE)\
                    .then_inc(A_ACT.sem, A_ACT.step(f"exp{u}"))

            def a_ot(i, g):
                act.wait_ge(A_PE.sem, A_PE.at(i, f"o{g}"))
                act.copy(OT[:, g, :], tA(13 + g)[:, 0:SEQ]).then_inc(A_ACT.sem, A_ACT.step(f"ot{g}"))

            def b_operands(i):
                act.wait_ge(B_PE.sem, B_PE.at(i, "xT"))
                columns(B_ACT, tB(0), x2Ta[:, :], x2Tb[0:DIM - P, :], ("xTa", "xTb"))
                for m in range(2 * GROUPS):
                    n = m // 2
                    if m % 2 == 0:
                        act.wait_ge(B_PE.sem, B_PE.at(i, f"qk{n}"))
                    src = tB(1 + n)[:, (m % 2) * SEQ:(m % 2 + 1) * SEQ]
                    if m < GROUPS:
                        act.activation(q2_full[:, m, :], src, ACT.Identity, bias=bias_q[:, m:m + 1], scale=SCALE)\
                            .then_inc(B_ACT.sem, B_ACT.step(f"q{m}"))
                    else:
                        g = m - GROUPS
                        act.activation(k2_full[:, g, :], src, ACT.Identity, bias=bias[:, 3, g:g + 1])\
                            .then_inc(B_ACT.sem, B_ACT.step(f"k{g}"))
                act.wait_ge(B_PE.sem, B_PE.at(i, "v"))
                for c in range(2):
                    r = ROWS[c]
                    act.copy(v2[0:r, :, c, :], tB(4)[0:r, c * DIM:(c + 1) * DIM].rearrange("p (h d) -> p h d", h=HEADS))\
                        .then_inc(B_ACT.sem, B_ACT.step(f"v{c}"))

            def b_exp(i, u):
                p, c = divmod(u, 2)
                g, r = group_of(p), ROWS[c]
                act.wait_ge(B_DVE.sem, B_DVE.at(i, f"max{u}"))
                if u == 8:
                    act.wait_ge(B_PE.sem, B_PE.at(i, "c0"))
                for a in range(2):
                    h = 2 * p + a
                    e = act.activation(PB[0:r, g % 2, c, h % 4, :], ps[0:r, 4 + c, a * SEQ:(a + 1) * SEQ], ACT.Exp,
                                       bias=nmax2[0:r, c, h:h + 1], accum_out=Z2[0:r, h, c:c + 1])
                e.then_inc(B_ACT.sem, B_ACT.step(f"exp{u}"))

            def b_ct(i, g):
                act.wait_ge(B_PE.sem, B_PE.at(i, f"c{g}"))
                act.copy(CT[:, g, :], tB(5 + g)[:, 0:SEQ]).then_inc(B_ACT.sem, B_ACT.step(f"ct{g}"))

            def b_x3(i):
                act.wait_ge(B_PE.sem, B_PE.at(i, "x3T"))
                columns(B_ACT, tB(9), x3Ta[:, :], x3Tb[:, :], ("x3Ta", "x3Tb"))

            def b_router(i):
                act.wait_ge(B_DVE.sem, B_DVE.at(i, "lgm"))
                act.activation(ex[:, :, :], lgm[:, :, :], ACT.Exp).then_inc(B_ACT.sem, B_ACT.step("ex"))

            def stage_a(i):
                a_xt(i, 0)
                a_xt(i, 2)
                a_squares(i)
                a_normal(i)
                a_operands(i)
                for u in range(12):
                    a_exp(i, u)
                    if u == 7:
                        a_ot(i, 0)
                a_ot(i, 1)
                a_ot(i, 2)

            def stage_b(i):
                b_operands(i)
                for u in range(12):
                    b_exp(i, u)
                    if u == 7:
                        b_ct(i, 0)
                b_ct(i, 1)
                b_ct(i, 2)
                b_x3(i)
                b_router(i)

            stage_a(0)
            with act.Fori(1, IMAGES) as i:
                b = i - 1
                a_xt(i, 0)
                a_xt(i, 2)
                b_operands(b)
                a_squares(i)
                b_exp(b, 0)
                b_exp(b, 1)
                a_normal(i)
                for u in range(2, 6):
                    b_exp(b, u)
                a_operands(i)
                b_exp(b, 6)
                b_exp(b, 7)
                b_ct(b, 0)
                for u in range(8, 12):
                    b_exp(b, u)
                b_ct(b, 1)
                b_ct(b, 2)
                for u in range(12):
                    a_exp(i, u)
                    if u == 5:
                        b_x3(b)
                    if u == 7:
                        a_ot(i, 0)
                    if u == 10:
                        b_router(b)
                a_ot(i, 1)
                a_ot(i, 2)
            stage_b(IMAGES - 1)

        @block.vector
        def _(dve):
            dve.sem_inc(A_DVE.sem, len(A_DVE.names))
            dve.sem_inc(B_DVE.sem, len(B_DVE.names))
            dve.sem_inc(h2_out, 32)
            dve.wait_ge(zeroed, 1)
            dve.memset(xTb[DIM - P:, :], 1.0).then_inc(set_up, 1)
            dve.memset(x2Tb[DIM - P:, :], 1.0).then_inc(set_up, 1)
            for c in range(2):
                dve.memset(va[0:ROWS[c], :, c, DH:DH + 1], 1.0).then_inc(set_up, 1)
            dve.wait_ge(loads, 16 * len(n_loads))
            dve.tensor_tensor(addend[:, :, :], addend[:, :, :], pos_emb[:, :, :], ALU.add).then_inc(set_up, 1)
            dve.tensor_copy(ident_b[:, :], ident[:, :]).then_inc(set_up, 1)
            dve.tensor_copy(tri[:, :], tri_f[:, :]).then_inc(set_up, 1)
            dve.tensor_copy(sel[:, :, :], sel_f[:, :, :]).then_inc(set_up, 1)
            dve.tensor_scalar(bias_q[:, :], bias[:, 2, :], SCALE, None, ALU.mult).then_inc(set_up, 1)
            dve.wait_ge(set_up, 9)

            def after(steps, i, name):
                dve.wait_ge(steps.sem, steps.at(i, name))

            def hold():
                dve.memset(held[:, :], 0.0)

            def a_tokens(i):
                dve.wait_ge(A_PE.sem, A_PE.at(i, "xt1"))
                dve.tensor_copy(XT[:, 2:4, :], tA(1)[:, 0:2 * SEQ].rearrange("p (a b) -> p a b", a=2))\
                    .then_inc(A_DVE.sem, A_DVE.step("xt1"))
                dve.wait_ge(A_PE.sem, A_PE.at(i, "tok"))
                for c in range(2):
                    r = ROWS[c]
                    dve.scalar_tensor_tensor(tok[0:r, c, :], tA(3)[0:r, c * DIM:(c + 1) * DIM], 1.0, addend[0:r, c, :],
                                             ALU.mult, ALU.add, accum_out=tok_sum[0:r, c:c + 1])\
                        .then_inc(A_DVE.sem, A_DVE.step(f"tok{c}"))

            def a_mean(i):
                dve.wait_ge(A_PE.sem, A_PE.at(i, "mean"))
                dve.tensor_reduce(neg_mean[:, :], tA(4)[:, 0:2], AX.X, ALU.add, negate=True)\
                    .then_inc(A_DVE.sem, A_DVE.step("nmean"))

            def a_var(i):
                dve.wait_ge(A_PE.sem, A_PE.at(i, "var"))
                dve.tensor_scalar(junk2[:, :], tA(5)[:, 0:2], 1.0, EPS, ALU.mult, ALU.add, accum_out=var_eps[:, :])\
                    .then_inc(A_DVE.sem, A_DVE.step("var"))

            def a_normal(i):
                dve.wait_ge(A_POOL.sem, A_POOL.at(i, "rstd"))
                dve.tensor_tensor(shift[:, :], neg_mean[:, :], rstd[:, :], ALU.mult)\
                    .then_inc(A_DVE.sem, A_DVE.step("shift"))
                dve.wait_ge(A_ACT.sem, A_ACT.at(i, "xn"))
                dve.tensor_tensor(xh[:, :, :], xh[:, :, :], ln_w[:, :, :], ALU.mult)\
                    .then_inc(A_DVE.sem, A_DVE.step("lnw"))
                after(A_DVE, i, "lnw")
                dve.tensor_tensor(xh[:, :, :], xh[:, :, :], ln_b[:, :, :], ALU.add)\
                    .then_inc(A_DVE.sem, A_DVE.step("lnb"))

            def split(steps, i, act_steps, q, qh, qh_f, ql, k, kh, kst):
                dve.wait_ge(act_steps.sem, act_steps.at(i, "q2"))
                dve.tensor_copy(qh, q).then_inc(steps.sem, steps.step("q_hi"))
                after(steps, i, "q_hi")
                dve.tensor_tensor(ql, q, qh_f, ALU.subtract).then_inc(steps.sem, steps.step("q_lo"))
                dve.wait_ge(act_steps.sem, act_steps.at(i, "k2"))
                dve.tensor_copy(kh.bitcast(F32R), k).then_inc(steps.sem, steps.step("k_hi"))
                after(steps, i, "k_hi")
                dve.scalar_tensor_tensor(kst, kh, neg_lo[:, 0:1], k, ALU.mult, ALU.add)\
                    .then_inc(steps.sem, steps.step("k_st"))

            def a_split(i):
                split(A_DVE, i, A_ACT, q_full[:, :, :], q_hi[:, :, :], q_hi[:, :, :].bitcast(F32), q_lo[:, :, :],
                      k_full[:, :, :], k_hi[:, :, :], k_st[:, :, :])

            def a_max(i, u):
                p, c = divmod(u, 2)
                dve.wait_ge(A_PE.sem, A_PE.at(i, f"sa{u}"))
                dve.tensor_reduce(nmax[0:ROWS[c], c, 2 * p:2 * p + 2],
                                  ps[0:ROWS[c], c, 0:2 * SEQ].rearrange("p (a b) -> p a b", a=2), AX.X, ALU.max,
                                  negate=True).then_inc(A_DVE.sem, A_DVE.step(f"max{u}"))

            def a_max_rows(i):
                after(A_DVE, i, "max11")
                dve.tensor_copy(nm[:, :, 0:HEADS], nmax[:, :, :]).then_inc(A_DVE.sem, A_DVE.step("nmh"))
                after(A_DVE, i, "nmh")
                dve.tensor_tensor(nm[:, :, HEADS:], nmax[:, :, :], nm[:, :, 0:HEADS], ALU.subtract)\
                    .then_inc(A_DVE.sem, A_DVE.step("nml"))
                dve.wait_ge(A_PE.sem, A_PE.at(i, "nmT"))
                dve.tensor_copy(nmT[0:2 * HEADS, :], tA(12).bitcast(BF16)[0:2 * HEADS, 0:SEQ])\
                    .then_inc(A_DVE.sem, A_DVE.step("nmT"))

            def a_finish(i):
                dve.wait_ge(B_POOL.sem, B_POOL.at(i, "h1b", before=1))
                for c in range(2):
                    r = ROWS[c]
                    dve.wait_ge(A_PE.sem, A_PE.at(i, f"oT{c}"))
                    o = tA(16 + c)[0:r, 0:GROUPS * P].rearrange("p (h d) -> p h d", h=HEADS)
                    dve.reciprocal(rzA[0:r, c, :], o[:, :, DH]).then_inc(A_DVE.sem, A_DVE.step(f"rz{c}"))
                    after(A_DVE, i, f"rz{c}")
                    dve.tensor_tensor(on[0:r, c, :].rearrange("p (h d) -> p h d", h=HEADS), o[:, :, 0:DH],
                                      rzA[0:r, c, :].unsqueeze(2).to_broadcast([r, HEADS, DH]), ALU.mult)\
                        .then_inc(A_DVE.sem, A_DVE.step(f"on{c}"))
                    after(A_DVE, i, f"on{c}")
                    dve.tensor_tensor(h1[0:r, c, :], on[0:r, c, :], tok[0:r, c, :], ALU.add)\
                        .then_inc(A_DVE.sem, A_DVE.step(("h0", "h1")[c]))

            def layer_norm(i, src, dst, st, mv, ve, rs, sh, names):
                bs, ba, v, rstd_step, s, x = names
                for c in range(2):
                    dve.bn_stats(st[0:ROWS[c], c, :], src[0:ROWS[c], c, :]).then_inc(B_DVE.sem, B_DVE.step(f"{bs}{c}"))
                after(B_DVE, i, f"{bs}1")
                hold()
                for c in range(2):
                    dve.bn_aggr(mv[0:ROWS[c], c, :], st[0:ROWS[c], c, :]).then_inc(B_DVE.sem, B_DVE.step(f"{ba}{c}"))
                after(B_DVE, i, f"{ba}1")
                dve.tensor_scalar(ve[:, :], mv[:, :, 1], EPS, None, ALU.add).then_inc(B_DVE.sem, B_DVE.step(v))
                dve.wait_ge(B_POOL.sem, B_POOL.at(i, rstd_step))
                dve.scalar_tensor_tensor(sh[:, :], mv[:, :, 0], -1.0, rs[:, :], ALU.mult, ALU.mult)\
                    .then_inc(B_DVE.sem, B_DVE.step(s))
                after(B_DVE, i, s)
                for c in range(2):
                    dve.tensor_scalar(dst[:, c, :], src[:, c, :], rs[:, c:c + 1], sh[:, c:c + 1], ALU.mult, ALU.add)\
                        .then_inc(B_DVE.sem, B_DVE.step(f"{x}{c}"))

            def b_normal(i):
                after(A_DVE, i, "h1")
                layer_norm(i, h1, x2, st2, mv2, ve2, rstd2, shift2, ("bs", "ba", "ve", "rstd", "shift", "x2"))

            def b_split(i):
                split(B_DVE, i, B_ACT, q2_full[:, :, :], q2_hi[:, :, :].bitcast(F32R), q2_hi[:, :, :], q2_lo[:, :, :],
                      k2_full[:, :, :], k2_hi[:, :, :], k2_st[:, :, :])

            def b_max(i, u):
                p, c = divmod(u, 2)
                dve.wait_ge(B_PE.sem, B_PE.at(i, f"s{u}"))
                dve.tensor_reduce(nmax2[0:ROWS[c], c, 2 * p:2 * p + 2],
                                  ps[0:ROWS[c], 4 + c, 0:2 * SEQ].rearrange("p (a b) -> p a b", a=2), AX.X, ALU.max,
                                  negate=True).then_inc(B_DVE.sem, B_DVE.step(f"max{u}"))

            def b_values(i, g):
                dve.wait_ge(B_ACT.sem, B_ACT.at(i, f"exp{4 * g + 3}"))
                h = slice(4 * g, 4 * g + 4)
                dve.reciprocal(rz2[:, h, :], Z2[:, h, :]).then_inc(B_DVE.sem, B_DVE.step(f"rz{g}"))
                after(B_DVE, i, f"rz{g}")
                dve.tensor_tensor(v2s[:, h, :, 0:DH], v2[:, h, :, :],
                                  rz2[:, h, :].unsqueeze(3).to_broadcast([P, 4, 2, DH]), ALU.mult)\
                    .then_inc(B_DVE.sem, B_DVE.step(f"vs{g}"))

            def b_residual(i):
                dve.wait_ge(B_PE.sem, B_PE.at(i, "wo"))
                dve.wait_ge(B_POOL.sem, B_POOL.at(i, "h1b"))
                dve.wait_ge(h2_out, i * 32 + 32)
                for c in range(2):
                    r = ROWS[c]
                    dve.tensor_tensor(h2[0:r, c, :], tB(8)[0:r, c * DIM:(c + 1) * DIM], h1b[0:r, c, :], ALU.add)\
                        .then_inc(B_DVE.sem, B_DVE.step(f"h2{c}"))
                after(B_DVE, i, "h21")
                dve.wait_ge(rows_out, i * 64 + 16 * SPARE)
                layer_norm(i, h2, x3, st3, mv3, ve3, rstd3, shift3, ("bs3", "ba3", "ve3", "rstd3", "shift3", "x3"))

            def b_choose(i):
                dve.wait_ge(B_PE.sem, B_PE.at(i, "logits"))
                for c in range(2):
                    dve.tensor_copy(lg[0:ROWS[c], c, :], tB(10)[0:ROWS[c], c * EXPERTS:(c + 1) * EXPERTS])\
                        .then_inc(B_DVE.sem, B_DVE.step(f"lg{c}"))
                after(B_DVE, i, "lg1")
                hold()
                for c in range(2):
                    dve.max(top8[:, c, :], lg[:, c, :]).then_inc(B_DVE.sem, B_DVE.step(f"top{c}"))
                after(B_DVE, i, "top1")
                hold()
                for c in range(2):
                    dve.max_index(top_i[:, c, :], top8[:, c, :], lg[:, c, :]).then_inc(B_DVE.sem, B_DVE.step(f"ti{c}"))
                after(B_DVE, i, "ti1")
                dve.tensor_copy(top_f[:, :, :], top_i[:, :, 0:2]).then_inc(B_DVE.sem, B_DVE.step("topf"))
                dve.tensor_tensor(rec[:, 8:10], top8[:, :, 1], top8[:, :, 0], ALU.subtract)\
                    .then_inc(B_DVE.sem, B_DVE.step("diff"))
                after(B_DVE, i, "topf")
                for k in range(2):
                    dve.tensor_tensor(hot[:, k, :, :], iota_e[:, :, :],
                                      top_f[:, :, k].unsqueeze(2).to_broadcast([P, 2, EXPERTS]), ALU.is_equal)\
                        .then_inc(B_DVE.sem, B_DVE.step(f"hot{k}"))
                after(B_DVE, i, "hot1")
                dve.tensor_tensor(hots[:, :, :], hot[:, 0, :, :], hot[:, 1, :, :], ALU.add)\
                    .then_inc(B_DVE.sem, B_DVE.step("hots"))
                dve.tensor_tensor(lgm[:, :, :], lg[:, :, :], top8[:, :, 0:1].to_broadcast([P, 2, EXPERTS]),
                                  ALU.subtract).then_inc(B_DVE.sem, B_DVE.step("lgm"))

            def b_slots(i):
                dve.wait_ge(B_PE.sem, B_PE.at(i, "rank"))
                t = tB(11)
                dve.tensor_tensor(slot[:, :, :], t[:, 0:2 * EXPERTS].rearrange("p (a b) -> p a b", a=2),
                                  base[:, :].unsqueeze(1).to_broadcast([P, 2, EXPERTS]), ALU.add)\
                    .then_inc(B_DVE.sem, B_DVE.step("slot"))
                after(B_DVE, i, "slot")
                for k in range(2):
                    dve.tensor_tensor(picked[:, k, :, :], hot[:, k, :, :], slot[:, :, :], ALU.mult)\
                        .then_inc(B_DVE.sem, B_DVE.step(f"pick{k}"))
                    after(B_DVE, i, f"pick{k}")
                    dve.tensor_reduce(rec[:, 2 * k:2 * k + 2], picked[:, k, :, :], AX.X, ALU.add)\
                        .then_inc(B_DVE.sem, B_DVE.step(f"pos{k}"))
                dve.tensor_tensor(base[:, :], base[:, :], t[:, 2 * EXPERTS:3 * EXPERTS], ALU.add)\
                    .then_inc(B_DVE.sem, B_DVE.step("base"))
                after(B_DVE, i, "pos1")
                dve.tensor_copy(slot_u[:, :], rec[:, 0:4]).then_inc(B_DVE.sem, B_DVE.step("slotu"))
                dve.tensor_copy(rec[:, 4:8].rearrange("p (k c) -> p c k", k=2), top_f[:, :, :])\
                    .then_inc(B_DVE.sem, B_DVE.step("recf"))
                after(B_DVE, i, "recf")
                dve.tensor_copy(rec_all[:, bass.ds(i, 1), :].rearrange("p a r -> p (a r)"), rec[:, :])\
                    .then_inc(B_DVE.sem, B_DVE.step("rec"))
                dve.wait_ge(B_ACT.sem, B_ACT.at(i, "ex"))
                dve.tensor_reduce(exs[:, :], ex[:, :, :], AX.X, ALU.add).then_inc(B_DVE.sem, B_DVE.step("exs"))
                after(B_DVE, i, "exs")
                dve.reciprocal(exr[:, :], exs[:, :]).then_inc(B_DVE.sem, B_DVE.step("exr"))
                after(B_DVE, i, "exr")
                dve.tensor_tensor(prob[:, :, :], ex[:, :, :], exr[:, :].unsqueeze(2).to_broadcast([P, 2, EXPERTS]),
                                  ALU.mult).then_inc(B_DVE.sem, B_DVE.step("prob"))
                after(B_DVE, i, "prob")
                dve.tensor_tensor(prob_sum[:, :, :], prob_sum[:, :, :], prob[:, :, :], ALU.add)\
                    .then_inc(B_DVE.sem, B_DVE.step("sum"))

            def stage_a(i):
                a_tokens(i)
                a_mean(i)
                a_var(i)
                a_normal(i)
                a_split(i)
                for u in range(12):
                    a_max(i, u)
                a_max_rows(i)
                a_finish(i)

            def stage_b(i):
                b_normal(i)
                b_split(i)
                for u in range(12):
                    b_max(i, u)
                    if u % 4 == 3:
                        b_values(i, u // 4)
                b_residual(i)
                b_choose(i)
                b_slots(i)

            stage_a(0)
            with dve.Fori(1, IMAGES) as i:
                b = i - 1
                b_normal(b)
                a_tokens(i)
                b_split(b)
                a_mean(i)
                b_max(b, 0)
                b_max(b, 1)
                a_var(i)
                b_max(b, 2)
                b_max(b, 3)
                a_normal(i)
                b_values(b, 0)
                b_max(b, 4)
                b_max(b, 5)
                a_split(i)
                b_max(b, 6)
                b_max(b, 7)
                b_values(b, 1)
                for u in range(8, 12):
                    a_max(i, 2 * (u - 8))
                    b_max(b, u)
                    a_max(i, 2 * (u - 8) + 1)
                a_max(i, 8)
                a_max(i, 9)
                b_values(b, 2)
                a_max(i, 10)
                a_max(i, 11)
                a_max_rows(i)
                b_residual(b)
                b_choose(b)
                b_slots(b)
                a_finish(i)
            stage_b(IMAGES - 1)


def phase234(nc, ins, ps, xs, ys, h2d, out_rows, sb_top, sem, rec_all, base, prob_sum, valid, ones):
    ctx = ExitStack()
    with ctx:
        def sb(name, shape, dt=F32):
            return sb_top(name, shape, dt, ctx)

        w1_hi = sb("w1_hi", [P, EXPERTS, FFN], F32R)
        w1_lo = sb("w1_lo", [P, EXPERTS, FFN], F32R)
        w1_st = sb("w1_st", [P, EXPERTS, FFN], F32R)
        w2_hi = sb("w2_hi", [P, EXPERTS, FCH * DIM], F32R)
        w2_lo = sb("w2_lo", [P, EXPERTS, FCH * DIM], F32R)
        tile_expert = sb("tile_expert", [1, TILES], I32)
        tile_start = sb("tile_start", [1, TILES], I32)
        gate = sb("gate", [P, 2, IMAGES, 2])
        ident = sb("ident2", [P, P])

        phase2(nc, ins, ps, xs, sb_top, sem, rec_all, base, prob_sum, valid, ones, w1_hi, w1_lo, w1_st, w2_hi, w2_lo,
               tile_expert, tile_start, gate, ident)
        phase3(nc, ps, xs, ys, sb_top, sem, w1_hi, w1_lo, w1_st, w2_hi, w2_lo, tile_expert, tile_start, ident)
        phase4(nc, ys, h2d, out_rows, sb_top, sem, rec_all, gate)


def phase2(nc, ins, ps, xs, sb_top, sem, rec_all, base, prob_sum, valid, ones, w1_hi, w1_lo, w1_st, w2_hi, w2_lo,
           tile_expert, tile_start, gate, ident):
    ctx = ExitStack()
    with ctx:
        def sb(name, shape, dt=F32):
            return sb_top(name, shape, dt, ctx)

        raw1 = sb("raw1", [P, 2, FFN])
        raw1s = sb("raw1s", [P, 2, FFN])
        raw1h = sb("raw1h", [P, 2, FFN])
        raw2 = sb("raw2", [P, 2, FCH * DIM])
        neg_low_half = sb("neg_low_half", [P, 1])
        first_slot = sb("first_slot2", [P, EXPERTS])
        row_of = sb("row_of", [P, EXPERTS])
        tile_i = sb("tile_i", [1, TILES])
        zeros = sb("zeros", [P, DIM])
        pad_slot = sb("pad_slot", [P, EXPERTS], U32)
        importance = sb("importance", [P, EXPERTS])
        inv = sb("inv", [P, EXPERTS])
        count_i = sb("count_i", [P, EXPERTS], I32)
        tiles_of = sb("tiles_of", [P, EXPERTS])
        tiles_to = sb("tiles_to", [P, EXPERTS])
        no_e = sb("no_e", [P, EXPERTS])
        past = sb("past", [1, TILES, EXPERTS])
        past_n = sb("past_n", [1, TILES, EXPERTS])
        te = sb("te", [1, TILES])
        tu = sb("tu", [1, TILES])
        share = sb("share", [P, 2, IMAGES, 2])
        to_row = sb("to_row", [P, EXPERTS])
        one_e = sb("one_e", [P, IMAGES, 2])
        e2 = sb("e2", [P, IMAGES, 2])
        total = sb("total", [P, IMAGES, 2])

        const_in = sem("const_in")
        raw_in = [sem("raw_in_even"), sem("raw_in_odd")]
        hi_done = sem("hi_done")
        lo_done = sem("lo_done")
        sums_ready = sem("sums_ready")
        probs_ready = sem("probs_ready")
        chain = sem("dve_chain")
        pads_known = sem("pads_known")
        exp_ready = sem("exp_ready")
        zero_ready = sem("zero_ready")
        pads_out = sem("pads_out")

        block = ctx.enter_context(nc.Block())

        @block.sync
        def _(sp):
            for dst, name in ((neg_low_half, "neg_low_half"), (first_slot, "first_slot"), (row_of, "row_of"),
                              (tile_i, "tile_i"), (ident, "ident")):
                sp.dma_start(dst[:], ins[name][:]).then_inc(const_in, 16)
            for e in range(EXPERTS):
                if e >= 2:
                    sp.wait_ge(lo_done, 3 * (e - 1))
                s = raw_in[e % 2]
                sp.dma_start(raw1[:, e % 2, :], ins["w1"][0:P, e, :]).then_inc(s, 16)
                for half in range(2):
                    sp.dma_start(raw1s[64 * half:64 * half + 64, e % 2, :], ins["w1"][P:DIM, e, :]).then_inc(s, 16)
                sp.dma_start(raw2[:, e % 2, :], ins["w2"][:, e, :]).then_inc(s, 16)
            sp.wait_ge(raw_in[1], 64 * (EXPERTS // 2))

        @block.gpsimd
        def _(pool):
            pool.memset(zeros[:], 0.0).then_inc(zero_ready, 1)
            pool.wait_ge(zero_ready, 1)
            pool.wait_ge(pads_known, 1)
            for e in range(EXPERTS):
                pool.indirect_dma_start(out=xs[:, :],
                                        out_offset=bass.IndirectOffsetOnAxis(ap=pad_slot[:, e:e + 1], axis=0),
                                        in_=zeros[:, :], in_offset=None).then_inc(pads_out, 16)
            pool.wait_ge(pads_out, 16 * EXPERTS)

        @block.tensor
        def _(pe):
            pe.wait_ge(probs_ready, 1)
            pe.matmul(ps[:, 0, 0:2 * EXPERTS], ones[:, :], prob_sum[:, :, :].rearrange("p a b -> p (a b)"),
                      start=True, stop=True).then_inc(sums_ready, 1)

        @block.scalar
        def _(act):
            for e in range(EXPERTS):
                act.wait_ge(raw_in[e % 2], 64 * (e // 2 + 1))
                if e >= 2:
                    act.wait_ge(lo_done, 3 * (e - 1))
                act.copy(w1_hi[:, e, :], raw1[:, e % 2, :]).then_inc(hi_done, 1)
                act.copy(raw1h[:, e % 2, :].bitcast(F32R), raw1s[:, e % 2, :]).then_inc(hi_done, 1)
                act.copy(w2_hi[:, e, :], raw2[:, e % 2, :]).then_inc(hi_done, 1)
            act.activation(e2[:, :, :], rec_all[:, :, 8:10], ACT.Exp).then_inc(exp_ready, 1)

        @block.vector
        def _(dve):
            links = [0]

            def link(instruction):
                links[0] += 1
                instruction.then_inc(chain, 1)
                dve.wait_ge(chain, links[0])

            dve.wait_ge(const_in, 16 * 5)
            dve.tensor_tensor(pad_slot[:, :], base[:, :], row_of[:, :], ALU.add).then_inc(pads_known, 1)
            link(dve.tensor_tensor(no_e[:, :], base[:, :], first_slot[:, :], ALU.subtract))
            link(dve.tensor_scalar(count_i[:, :], no_e[:, :], float(P - 1), None, ALU.add))
            link(dve.tensor_scalar(count_i[:, :], count_i[:, :], P.bit_length() - 1, None, ALU.logical_shift_right))
            link(dve.tensor_copy(tiles_of[:, :], count_i[:, :]))
            link(dve.memset(no_e[:, :], 0.0))
            link(dve.tensor_tensor_scan(tiles_to[:, :], tiles_of[:, :], no_e[:, :], 0.0, ALU.add, ALU.add))
            link(dve.tensor_tensor(past[:, :, :], tile_i[:, :].unsqueeze(2).to_broadcast([1, TILES, EXPERTS]),
                                   tiles_to[0:1, :].unsqueeze(1).to_broadcast([1, TILES, EXPERTS]), ALU.is_ge))
            link(dve.tensor_reduce(te[:, :], past[:, :, :], AX.X, ALU.add))
            link(dve.tensor_tensor(past_n[:, :, :], past[:, :, :],
                                   tiles_of[0:1, :].unsqueeze(1).to_broadcast([1, TILES, EXPERTS]), ALU.mult))
            link(dve.tensor_reduce(tu[:, :], past_n[:, :, :], AX.X, ALU.add))
            link(dve.tensor_tensor(tu[:, :], tile_i[:, :], tu[:, :], ALU.subtract))
            link(dve.tensor_scalar(tu[:, :], tu[:, :], float(P), None, ALU.mult))
            link(dve.scalar_tensor_tensor(tile_start[:, :], te[:, :], float(CAP), tu[:, :], ALU.mult, ALU.add))
            link(dve.tensor_scalar(tile_expert[:, :], te[:, :], float(EXPERTS - 1), None, ALU.min))
            link(dve.tensor_tensor(no_e[:, :], tiles_to[:, :], tiles_of[:, :], ALU.subtract))
            link(dve.scalar_tensor_tensor(to_row[:, :], no_e[:, :], float(P), first_slot[:, :], ALU.mult, ALU.subtract))
            dve.tensor_tensor(prob_sum[:, :, :], prob_sum[:, :, :], valid[:, :, :], ALU.mult).then_inc(probs_ready, 1)
            dve.wait_ge(sums_ready, 1)
            link(dve.tensor_copy(importance[:, :], ps[:, 0, 0:EXPERTS]))
            link(dve.tensor_tensor(importance[:, :], ps[:, 0, EXPERTS:2 * EXPERTS], importance[:, :], ALU.add))
            link(dve.tensor_scalar(importance[:, :], importance[:, :], -1.0, float(np.float32(1.0 - 0.9)),
                                   ALU.add, ALU.mult))
            link(dve.tensor_scalar(importance[:, :], importance[:, :], 1.0, 0.01, ALU.add, ALU.add))
            link(dve.reciprocal(inv[:, :], importance[:, :]))
            link(dve.memset(share[:, :, :, :], 0.0))
            for k in range(2):
                for e in range(EXPERTS):
                    link(dve.tensor_scalar(one_e[:, :, :], rec_all[:, :, 4 + 2 * k:6 + 2 * k], float(e),
                                           inv[:, e:e + 1], ALU.is_equal, ALU.mult))
                    link(dve.tensor_tensor(share[:, k, :, :], share[:, k, :, :], one_e[:, :, :], ALU.add))
                    link(dve.tensor_scalar(one_e[:, :, :], rec_all[:, :, 4 + 2 * k:6 + 2 * k], float(e),
                                           to_row[:, e:e + 1], ALU.is_equal, ALU.mult))
                    link(dve.tensor_tensor(rec_all[:, :, 2 * k:2 * k + 2], rec_all[:, :, 2 * k:2 * k + 2],
                                           one_e[:, :, :], ALU.add))
            for e in range(EXPERTS):
                h = raw1h[:, e % 2, :]
                dve.wait_ge(hi_done, 3 * e + 1)
                dve.tensor_tensor(w1_lo[:, e, :], raw1[:, e % 2, :], w1_hi[:, e, :].bitcast(F32), ALU.subtract)\
                    .then_inc(lo_done, 1)
                dve.wait_ge(hi_done, 3 * e + 2)
                dve.scalar_tensor_tensor(w1_st[:, e, :], h, neg_low_half[:, 0:1], raw1s[:, e % 2, :],
                                         ALU.mult, ALU.add).then_inc(lo_done, 1)
                dve.wait_ge(hi_done, 3 * e + 3)
                dve.tensor_tensor(w2_lo[:, e, :], raw2[:, e % 2, :], w2_hi[:, e, :].bitcast(F32), ALU.subtract)\
                    .then_inc(lo_done, 1)
            dve.wait_ge(exp_ready, 1)
            link(dve.tensor_tensor(share[:, 1, :, :], share[:, 1, :, :], e2[:, :, :], ALU.mult))
            link(dve.tensor_tensor(total[:, :, :], share[:, 0, :, :], share[:, 1, :, :], ALU.add))
            link(dve.reciprocal(total[:, :, :], total[:, :, :]))
            for k in range(2):
                link(dve.tensor_tensor(gate[:, k, :, :], share[:, k, :, :], total[:, :, :], ALU.mult))


def phase3(nc, ps, xs, ys, sb_top, sem, w1_hi, w1_lo, w1_st, w2_hi, w2_lo, tile_expert, tile_start, ident):
    ctx = ExitStack()
    with ctx:
        def sb(name, shape, dt=F32):
            return sb_top(name, shape, dt, ctx)

        xt = sb("xt", [P, 2, 2 * P])
        x_hi = sb("x_hi", [P, 2, 2 * P], F32R)
        x_lo = sb("x_lo", [P, 2, 2 * P], F32R)
        hid = sb("hid", [P, 2, FFN])
        h_hi = sb("h_hi", [P, 2, FFN], F32R)
        h_lo = sb("h_lo", [P, 2, FFN], F32R)
        yt = sb("yt", [P, 2, DIM])

        xt_in = [sem("xt_in_even"), sem("xt_in_odd")]
        y_out = [sem("y_out_even"), sem("y_out_odd")]
        x_turned, up_done, h_turned, down_done = (sem(s) for s in ("x_turned", "up_done", "h_turned", "down_done"))
        x_hi_done, silu_done, h_hi_done = (sem(s) for s in ("x_hi_done", "silu_done", "h_hi_done"))
        x_lo_done, y_done, h_lo_done = (sem(s) for s in ("x_lo_done", "y_done", "h_lo_done"))

        def through(tile):
            return tile + 2

        def bank(kind, par):
            return ps[:, 2 * kind + par, :]

        def tiles(eng, slot):
            for n in range(3):
                slot(n, n % 2, n // 2)
            with eng.Fori(1, (TILES - 2) // 2) as i:
                slot(2 * i + 1, 1, i)
                slot(2 * i + 2, 0, i + 1)
            slot(TILES - 1, 1, TILES // 2 - 1)

        def first(n):
            return isinstance(n, int) and n == 0

        def last(n):
            return isinstance(n, int) and n == TILES - 1

        block = ctx.enter_context(nc.Block())

        @block.sync
        def _(sp):
            def load(n, par, turned=None):
                r = sp.value_load(tile_start[0:1, bass.ds(n, 1)], min_val=0, max_val=SLOTS - P)
                if turned is not None:
                    sp.wait_ge(x_turned, through(turned))
                sp.dma_start(xt[:, par, 0:DIM], xs[bass.ds(r, P), :]).then_inc(xt_in[par], 16)
                sp.dma_start(xt[:, par, DIM:2 * P], xs[bass.ds(r, P), P:DIM]).then_inc(xt_in[par], 16)

            load(0, 0)
            load(1, 1)
            with sp.Fori(0, (TILES - 2) // 2) as i:
                for par in range(2):
                    load(2 * i + 2 + par, par, turned=2 * i + par)

        @block.gpsimd
        def _(pool):
            for s in (x_turned, up_done, h_turned, down_done, x_hi_done, silu_done, h_hi_done, x_lo_done, y_done,
                      h_lo_done):
                pool.sem_inc(s, 1)
            with pool.Fori(0, TILES // 2) as i:
                for par in range(2):
                    n = 2 * i + par
                    pool.wait_ge(y_done, through(n))
                    pool.dma_start(ys[bass.ds(n * P, P), :], yt[:, par, :]).then_inc(y_out[par], 16)
            for s in y_out:
                pool.wait_ge(s, 16 * (TILES // 2))

        @block.tensor
        def _(pe):
            def turn_x(n, par, loads):
                pe.wait_ge(xt_in[par], 32 * loads + 32)
                if not first(n):
                    pe.wait_ge(x_lo_done, through(n - 2))
                pe.transpose(bank(0, par)[:, 0:P], xt[:, par, 0:P], ident[:, :])
                pe.transpose(bank(0, par)[:, P:2 * P], xt[:, par, P:2 * P], ident[:, :]).then_inc(x_turned, 1)

            def up(n, par):
                e = pe.value_load(tile_expert[0:1, bass.ds(n, 1)], min_val=0, max_val=EXPERTS - 1)
                pe.wait_ge(x_lo_done, through(n))
                if not first(n):
                    pe.wait_ge(silu_done, through(n - 2))
                o = bank(1, par)[:, 0:FFN]

                def w(t, rows=P):
                    return t[0:rows, bass.ds(e, 1), :].rearrange("p a b -> p (a b)")

                pe.matmul(o, x_hi[:, par, 0:P], w(w1_hi), start=True, stop=False)
                pe.matmul(o, x_hi[:, par, 0:P], w(w1_lo), start=False, stop=False)
                pe.matmul(o, x_lo[:, par, 0:P], w(w1_hi), start=False, stop=False)
                pe.matmul(o, x_hi[:, par, P:2 * P], w(w1_st), start=False, stop=False)
                pe.matmul(o, x_lo[:, par, P:2 * P], w(w1_st), start=False, stop=True).then_inc(up_done, 1)

            def turn_h(n, par):
                pe.wait_ge(silu_done, through(n))
                if not first(n):
                    pe.wait_ge(h_lo_done, through(n - 2))
                for f in range(FCH):
                    mm = pe.transpose(bank(2, par)[:, f * P:(f + 1) * P], hid[:, par, f * P:(f + 1) * P], ident[:, :])
                mm.then_inc(h_turned, 1)

            def down(n, par):
                e = pe.value_load(tile_expert[0:1, bass.ds(n, 1)], min_val=0, max_val=EXPERTS - 1)
                pe.wait_ge(h_lo_done, through(n))
                if not first(n):
                    pe.wait_ge(y_done, through(n - 2))
                o = bank(3, par)[:, 0:DIM]
                parts = [(h, w, f) for f in range(FCH) for h, w in ((h_hi, w2_hi), (h_hi, w2_lo), (h_lo, w2_hi))]
                for m, (h, w, f) in enumerate(parts):
                    mm = pe.matmul(o, h[:, par, f * P:(f + 1) * P],
                                   w[:, bass.ds(e, 1), f * DIM:(f + 1) * DIM].rearrange("p a b -> p (a b)"),
                                   start=(m == 0), stop=(m == len(parts) - 1))
                mm.then_inc(down_done, 1)

            def slot(n, par, pair):
                up(n, par)
                if not last(n):
                    turn_x(n + 1, 1 - par, pair + 1 if par else pair)
                if not first(n):
                    down(n - 1, 1 - par)
                turn_h(n, par)

            turn_x(0, 0, 0)
            tiles(pe, slot)
            down(TILES - 1, 1)

        @block.scalar
        def _(act):
            def high_x(n, par):
                act.wait_ge(x_turned, through(n))
                if not first(n):
                    act.wait_ge(up_done, through(n - 2))
                act.copy(x_hi[:, par, :], bank(0, par)[:, 0:2 * P]).then_inc(x_hi_done, 1)

            def slot(n, par, pair):
                act.wait_ge(up_done, through(n))
                if not first(n):
                    act.wait_ge(h_turned, through(n - 2))
                act.activation(hid[:, par, :], bank(1, par)[:, 0:FFN], ACT.Silu).then_inc(silu_done, 1)
                if not last(n):
                    high_x(n + 1, 1 - par)
                act.wait_ge(h_turned, through(n))
                if not first(n):
                    act.wait_ge(down_done, through(n - 2))
                act.copy(h_hi[:, par, :], bank(2, par)[:, 0:FFN]).then_inc(h_hi_done, 1)

            high_x(0, 0)
            tiles(act, slot)

        @block.vector
        def _(dve):
            def low_x(n, par):
                dve.wait_ge(x_hi_done, through(n))
                if not first(n):
                    dve.wait_ge(up_done, through(n - 2))
                dve.tensor_tensor(x_lo[:, par, :], bank(0, par)[:, 0:2 * P], x_hi[:, par, :].bitcast(F32), ALU.subtract)\
                    .then_inc(x_lo_done, 1)

            def output(n, par, stores):
                dve.wait_ge(down_done, through(n))
                if not (isinstance(stores, int) and stores <= 0):
                    dve.wait_ge(y_out[par], 16 * stores)
                dve.tensor_copy(yt[:, par, :], bank(3, par)[:, 0:DIM]).then_inc(y_done, 1)

            def slot(n, par, pair):
                if not last(n):
                    low_x(n + 1, 1 - par)
                if not first(n):
                    output(n - 1, 1 - par, pair if par else pair - 1)
                dve.wait_ge(h_hi_done, through(n))
                if not first(n):
                    dve.wait_ge(down_done, through(n - 2))
                dve.tensor_tensor(h_lo[:, par, :], bank(2, par)[:, 0:FFN], h_hi[:, par, :].bitcast(F32), ALU.subtract)\
                    .then_inc(h_lo_done, 1)

            low_x(0, 0)
            tiles(dve, slot)
            output(TILES - 1, 1, TILES // 2 - 1)


def phase4(nc, ys, h2d, out_rows, sb_top, sem, rec_all, gate):
    ctx = ExitStack()
    with ctx:
        def sb(name, shape, dt=F32):
            return sb_top(name, shape, dt, ctx)

        BUFS = 2
        held = sb("held4", [P, 1])
        slot_u = sb("slot_u4", [P, BUFS, 4], U32)
        y = sb("y4", [P, BUFS, 4, DIM])
        res = sb("res4", [P, BUFS, 2, DIM])
        o = sb("o4", [P, BUFS, 2, DIM])
        rows_in = [sem("rows_in_even"), sem("rows_in_odd")]
        res_in = [sem("res_in_even"), sem("res_in_odd")]
        out_done = [sem("out_done_even"), sem("out_done_odd")]
        slots_ready = sem("slots_ready")
        mixed = sem("mixed")
        MIX = 4

        block = ctx.enter_context(nc.Block())
        PAIRS_OF = IMAGES // 2

        @block.sync
        def _(sp):
            for s in out_done:
                sp.sem_inc(s, 32)

            def load(i, par):
                for c in range(2):
                    sp.dma_start(res[0:ROWS[c], par, c, :], h2d[bass.ds(i * SEQ + START[c], ROWS[c]), :])\
                        .then_inc(res_in[par], 16)

            load(0, 0)
            load(1, 1)
            with sp.Fori(0, PAIRS_OF - 1) as i:
                for par in range(2):
                    sp.wait_ge(mixed, MIX * (2 * i + par) + 3 * MIX)
                    load(2 * i + 2 + par, par)

        @block.scalar
        def _(act):
            with act.Fori(0, PAIRS_OF) as i:
                for par in range(2):
                    n = 2 * i + par
                    act.wait_ge(mixed, MIX * n + 3 * MIX)
                    for c in range(2):
                        act.dma_start(out_rows[bass.ds(n * SEQ + START[c], ROWS[c]), :], o[0:ROWS[c], par, c, :])\
                            .then_inc(out_done[par], 16)
            for s in out_done:
                act.wait_ge(s, 32 + 32 * PAIRS_OF)

        @block.gpsimd
        def _(pool):
            pool.sem_inc(mixed, 2 * MIX)
            with pool.Fori(0, PAIRS_OF) as i:
                for par in range(2):
                    n = 2 * i + par
                    pool.wait_ge(mixed, MIX * n + MIX)
                    pool.tensor_copy(slot_u[:, par, :],
                                     rec_all[:, bass.ds(n, 1), 0:4].rearrange("p a r -> p (a r)"))\
                        .then_inc(slots_ready, 1)
                    pool.wait_ge(slots_ready, n + 1)
                    pool.tensor_tensor(held[:, :], rec_all[:, 0, 8:9], rec_all[:, 0, 8:9], ALU.add)
                    for k in range(2):
                        for c in range(2):
                            m, r = 2 * k + c, ROWS[c]
                            pool.indirect_dma_start(
                                out=y[0:r, par, m, :], out_offset=None, in_=ys[:, :],
                                in_offset=bass.IndirectOffsetOnAxis(ap=slot_u[0:r, par, m:m + 1], axis=0))\
                                .then_inc(rows_in[par], 16)

        @block.vector
        def _(dve):
            with dve.Fori(0, PAIRS_OF) as i:
                for par in range(2):
                    n = 2 * i + par
                    dve.wait_ge(rows_in[par], 64 * i + 64)
                    dve.wait_ge(res_in[par], 32 * i + 32)
                    dve.wait_ge(out_done[par], 32 * i + 32)
                    for k in range(2):
                        for c in range(2):
                            r = ROWS[c]
                            if k:
                                dve.wait_ge(mixed, MIX * n + 2 * MIX + 1 + c)
                            dve.scalar_tensor_tensor(
                                o[0:r, par, c, :], y[0:r, par, 2 * k + c, :],
                                gate[0:r, k, bass.ds(n, 1), c:c + 1].rearrange("p a b -> p (a b)"),
                                o[0:r, par, c, :] if k else res[0:r, par, c, :], ALU.mult, ALU.add)\
                                .then_inc(mixed, 1)




def _layout(x):
    a = {k.replace("L0_", ""): np.asarray(v) for k, v in x.items()}
    f = np.float32
    o = {}
    o["x"] = np.ascontiguousarray(a["x"]).reshape(IMAGES, PATCHES, IN_DIM)
    o["wm"] = a["tok_W_map"].T.reshape(KCH, P, DIM).transpose(1, 0, 2)
    o["b_map"] = a["tok_b_map"][None]
    o["cls"] = a["tok_class_token"]
    o["ln_w"], o["ln_b"] = a["tok_ln_w"], a["tok_ln_b"]

    def columns(w):
        full = np.zeros((DIM, GROUPS, P), f)
        for h in range(HEADS):
            rows = slice(None) if w.shape[1] == DIM else slice(h * DH, (h + 1) * DH)
            for twice in range(2):
                at = 32 * (h % 4) + twice * DH
                full[rows, h // 4, at:at + DH] = w[h]
        return full

    for n, w in (("wq1", a["tok_Wq"]), ("wk1", a["tok_Wk"])):
        full = columns(w.transpose(0, 2, 1))
        both = full[:P].copy()
        both[0:DIM - P, 2, :] = full[P:, 2, :]
        o[n] = both
    for n, w in (("wq2", a["attn_Wq"]), ("wk2", a["attn_Wk"])):
        full = columns(w)
        o[n + "a"], o[n + "b"] = full[:P], full[P:]
    bd = np.zeros((DIM + 1, DIM), f)
    for h in range(HEADS):
        bd[h * DH:(h + 1) * DH, h * DH:(h + 1) * DH] = a["tok_Wv"][h].T
    bd[DIM] = a["tok_bv"].reshape(DIM)
    o["wv1a"], o["wv1b"] = bd[:P], bd[P:]
    wv = np.zeros((DIM + 1, DIM), f)
    wv[:DIM] = a["attn_Wv"].transpose(1, 0, 2).reshape(DIM, DIM)
    wv[DIM] = a["attn_bv"].reshape(DIM)
    o["wv2a"], o["wv2b"] = wv[:P], wv[P:]
    bias = np.zeros((P, 4, GROUPS), f)
    for j, n in enumerate(("tok_bq", "tok_bk", "attn_bq", "attn_bk")):
        for h in range(HEADS):
            for twice in range(2):
                at = 32 * (h % 4) + twice * DH
                bias[at:at + DH, j, h // 4] = a[n][h]
    o["bias"] = bias
    wo = np.zeros((P, GROUPS, DIM), f)
    for h in range(HEADS):
        wo[32 * (h % 4):32 * (h % 4) + DH, h // 4] = a["attn_Wo"][h * DH:(h + 1) * DH]
    o["wo"] = wo
    o["bo"] = a["attn_bo"][None]
    o["rw_a"], o["rw_b"] = a["ffn_router_w"].T[:P], a["ffn_router_w"].T[P:]
    o["w1"] = a["ffn_w1"].transpose(2, 0, 1)
    o["w2"] = a["ffn_w2"].transpose(0, 2, 1).reshape(EXPERTS, FCH, P, DIM).transpose(2, 0, 1, 3)\
        .reshape(P, EXPERTS, FCH * DIM)

    part, row = np.arange(P), np.arange(SEQ, dtype=f)[:, None]
    col = np.arange(DIM, dtype=f)[None]
    even = np.arange(DIM) % 2 == 0
    o["pos_emb"] = np.where(even, np.sin(row / np.power(f(10000), col / f(DIM))),
                            np.cos(row / np.power(f(10000), (col - f(1)) / f(DIM)))).astype(f)
    o["ident"] = np.eye(P, dtype=f)
    o["tri"] = (part[:, None] < part[None]).astype(f)
    sel = np.zeros((P, HEADS, P), f)
    for h in range(HEADS):
        sel[[h, HEADS + h], h] = 1
    o["sel"] = sel
    o["head_mask"] = (part[:, None] // 32 == np.arange(4)).astype(f)
    o["hi_mask"] = o["head_mask"] * (part[:, None] % 32 < DH).astype(f)
    o["neg_lo"] = -(part[:, None] % 32 >= DH).astype(f)
    o["neg_low_half"] = -(part[:, None] >= DIM - P).astype(f)
    real = np.stack([part < ROWS[0], part < ROWS[1]], 1)[:, :, None]
    o["iota_e"] = np.where(real, np.arange(EXPERTS), -1).astype(f)
    o["valid"] = np.broadcast_to(real, (P, 2, EXPERTS)).astype(f)
    o["first_slot"] = np.broadcast_to(np.arange(EXPERTS) * CAP, (P, EXPERTS)).astype(f)
    o["row_of"] = np.broadcast_to(part[:, None], (P, EXPERTS)).astype(f)
    o["tile_i"] = np.arange(TILES, dtype=f)[None]
    return {k: np.ascontiguousarray(v) for k, v in o.items()}


def kernel(**inputs):
    import concourse.bacc as _bacc
    from concourse import mybir as _mybir
    from concourse.bass_utils import run_bass_kernel_spmd as _run

    nc = _bacc.Bacc("TRN2", target_bir_lowering=False, num_devices=1)
    arrays, ins = {}, {}
    for name, a in _layout(inputs).items():
        arrays[f"in_{name}"] = a
        ins[name] = nc.dram_tensor(f"in_{name}", a.shape, _mybir.dt.from_np(a.dtype), kind="ExternalInput").ap()
    out = nc.dram_tensor("out", (IMAGES, SEQ, DIM), F32, kind="ExternalOutput").ap()
    build(nc, ins, out)
    r = _run(nc, [arrays], core_ids=[0])
    return r.results[0]["out"]
```

```python
from contextlib import ExitStack

import numpy as np

import concourse.bass as bass
from concourse import mybir

F32 = mybir.dt.float32
F32R = mybir.dt.float32r
BF16 = mybir.dt.bfloat16
I32 = mybir.dt.int32
U32 = mybir.dt.uint32
ALU = mybir.AluOpType
ACT = mybir.ActivationFunctionType
AX = mybir.AxisListType

P = 128
IMAGES = 64
PATCHES = 196
SEQ = PATCHES + 1
DIM = 192
HEADS = 12
DH = 16
IN_DIM = 768
KCH = IN_DIM // P
ROWS = (P, SEQ - P)
START = (0, P)
GROUPS = 3
PAIRS = HEADS // 2
EXPERTS = 8
FFN = 512
FCH = FFN // P
TOKENS = IMAGES * SEQ
TILES = 2 * TOKENS // P + EXPERTS - 1
TILES += TILES % 2
CAP = -(-(TOKENS + P) // P) * P
SPARE = TILES - 2 * TOKENS // P
SLOTS = EXPERTS * CAP + SPARE * P
EPS = 1e-5
SCALE = 0.25
REC = 10


class Steps:

    def __init__(self, sem, names):
        self.sem, self.names, self.seen = sem, names.split(), 0

    def step(self, name):
        assert self.names[self.seen % len(self.names)] == name, (self.names[self.seen % len(self.names)], name)
        self.seen += 1
        return 1

    def at(self, turn, name, before=0):
        return turn * len(self.names) + (1 - before) * len(self.names) + self.names.index(name) + 1


def upto(prefix, *parts):
    out, u = [], 0
    for part in parts:
        if isinstance(part, str):
            out.append(part)
        else:
            out += [f"{prefix}{n}" for n in range(u, part)]
            u = part
    return " ".join(out)


def group_of(pair):
    return pair // 2


def build(nc, ins, out):
    top = ExitStack()
    with top:
        def sb(name, shape, dt=F32, ctx=top):
            return ctx.enter_context(nc.sbuf_tensor(name, shape, dt))

        def sem(name):
            return top.enter_context(nc.semaphore(name))

        ps = top.enter_context(nc.psum_tensor("ps", [P, 8, 512], F32))
        xs = nc.dram_tensor("xs", [SLOTS, DIM], F32).ap()
        ys = nc.dram_tensor("ys", [TILES * P, DIM], F32).ap()
        h2d = nc.dram_tensor("h2d", [TOKENS, DIM], F32).ap()
        out_rows = out.rearrange("b s d -> (b s) d")

        rec_all = sb("rec_all", [P, IMAGES, REC])
        base = sb("slot_end", [P, EXPERTS])
        prob_sum = sb("prob_sum", [P, 2, EXPERTS])
        valid = sb("valid", [P, 2, EXPERTS])
        ones = sb("ones", [P, P])

        phase1(nc, ins, ps, xs, h2d, sb, sem, rec_all, base, prob_sum, valid, ones)
        phase234(nc, ins, ps, xs, ys, h2d, out_rows, sb, sem, rec_all, base, prob_sum, valid, ones)


def phase1(nc, ins, ps, xs, h2d, sb_top, sem, rec_all, base, prob_sum, valid, ones):
    ctx = ExitStack()
    with ctx:
        def sb(name, shape, dt=F32):
            return sb_top(name, shape, dt, ctx)

        ident = sb("ident", [P, P])
        ident_b = sb("ident_b", [P, P], BF16)
        wm = sb("wm", [P, KCH, DIM])
        addend = sb("addend", [P, 2, DIM])
        pos_emb = sb("pos_emb", [P, 2, DIM])
        ln_w = sb("ln_w", [P, 2, DIM])
        ln_b = sb("ln_b", [P, 2, DIM])
        wq1 = sb("wq1", [P, GROUPS, P])
        wk1 = sb("wk1", [P, GROUPS, P])
        wv1a = sb("wv1a", [P, DIM])
        wv1b = sb("wv1b", [DIM - P + 1, DIM])
        wq2a = sb("wq2a", [P, GROUPS, P])
        wq2b = sb("wq2b", [DIM - P, GROUPS, P])
        wk2a = sb("wk2a", [P, GROUPS, P])
        wk2b = sb("wk2b", [DIM - P, GROUPS, P])
        wv2a = sb("wv2a", [P, DIM])
        wv2b = sb("wv2b", [DIM - P + 1, DIM])
        bias = sb("bias", [P, 4, GROUPS])
        bias_q = sb("bias_q", [P, GROUPS])
        wo = sb("wo", [P, GROUPS, DIM])
        bo = sb("bo", [P, DIM])
        rw_a = sb("rw_a", [P, EXPERTS])
        rw_b = sb("rw_b", [DIM - P, EXPERTS])
        neg_lo = sb("neg_lo", [P, 1])
        mean_mat = sb("mean_mat", [P, P])
        neg_half = sb("neg_half", [P, 2])
        zero = sb("zero", [P, 2])
        sel = sb("sel", [P, HEADS, P], BF16)
        iota_e = sb("iota_e", [P, 2, EXPERTS])
        tri = sb("tri", [P, P], BF16)
        ones_b = sb("ones_b", [P, P], BF16)
        sel_f = sb("sel_f", [P, HEADS, P])
        tri_f = sb("tri_f", [P, P])
        X = sb("X", [P, 2, IN_DIM])
        XT = sb("XT", [P, KCH, SEQ])
        tok = sb("tok", [P, 2, DIM])
        tok2 = sb("tok2", [P, 2, DIM])
        tok_sum = sb("tok_sum", [P, 2])
        sq = sb("sq", [P, 2])
        junk_sq = sb("junk_sq", [P, 2, DIM])
        neg_mean = sb("neg_mean", [P, 1])
        var_eps = sb("var_eps", [P, 1])
        junk2 = sb("junk2", [P, 2])
        rstd = sb("rstd", [P, 1])
        shift = sb("shift", [P, 1])
        xh = sb("xh", [P, 2, DIM])
        xTa = sb("xTa", [P, SEQ])
        xTb = sb("xTb", [DIM - P + 1, SEQ])
        k_full = sb("k_full", [P, GROUPS, SEQ])
        q_hi = sb("q_hi", [P, GROUPS, SEQ], F32R)
        q_lo = sb("q_lo", [P, GROUPS, SEQ], F32R)
        k_hi = sb("k_hi", [P, GROUPS, SEQ], F32R)
        k_st = sb("k_st", [P, GROUPS, SEQ], F32R)
        k_msk = sb("k_msk", [P, HEADS, SEQ], F32R)
        qm_hi = sb("qm_hi", [P, HEADS, SEQ], F32R)
        qm_lo = sb("qm_lo", [P, HEADS, SEQ], F32R)
        va = sb("va", [P, HEADS, 2, 32])
        nmax = sb("nmax", [P, 2, HEADS])
        nm = sb("nm", [P, 2, 2 * HEADS], BF16)
        nmT = sb("nmT", [P, SEQ], BF16)
        PA = sb("PA", [P, 2, 2, 4, SEQ])
        OT = sb("OT", [P, GROUPS, SEQ])
        rzA = sb("rzA", [P, 2, HEADS])
        on = sb("on", [P, 2, DIM])
        h1 = sb("h1", [P, 2, DIM])
        h1b = sb("h1b", [P, 2, DIM])
        st2 = sb("st2", [P, 2, 6])
        mv2 = sb("mv2", [P, 2, 2])
        ve2 = sb("ve2", [P, 2])
        rstd2 = sb("rstd2", [P, 2])
        shift2 = sb("shift2", [P, 2])
        x2 = sb("x2", [P, 2, DIM])
        x2Ta = sb("x2Ta", [P, SEQ])
        x2Tb = sb("x2Tb", [DIM - P + 1, SEQ])
        q2_full = sb("q2_full", [P, GROUPS, SEQ])
        k2_full = sb("k2_full", [P, GROUPS, SEQ])
        q2_hi = sb("q2_hi", [P, GROUPS, SEQ], F32R)
        q2_lo = sb("q2_lo", [P, GROUPS, SEQ], F32R)
        k2_hi = sb("k2_hi", [P, GROUPS, SEQ], F32R)
        k2_st = sb("k2_st", [P, GROUPS, SEQ], F32R)
        q2m_hi = sb("q2m_hi", [P, HEADS, SEQ], F32R)
        q2m_lo = sb("q2m_lo", [P, HEADS, SEQ], F32R)
        v2 = sb("v2", [P, HEADS, 2, DH])
        v2s = sb("v2s", [P, HEADS, 2, 32])
        nmax2 = sb("nmax2", [P, 2, HEADS])
        Z2 = sb("Z2", [P, HEADS, 2])
        rz2 = sb("rz2", [P, HEADS, 2])
        PB = sb("PB", [P, 2, 2, 4, SEQ])
        CT = sb("CT", [P, GROUPS, SEQ])
        h2 = sb("h2", [P, 2, DIM])
        st3 = sb("st3", [P, 2, 6])
        mv3 = sb("mv3", [P, 2, 2])
        ve3 = sb("ve3", [P, 2])
        rstd3 = sb("rstd3", [P, 2])
        shift3 = sb("shift3", [P, 2])
        x3 = sb("x3", [P, 2, DIM])
        x3Ta = sb("x3Ta", [P, SEQ])
        x3Tb = sb("x3Tb", [DIM - P, SEQ])
        lg = sb("lg", [P, 2, EXPERTS])
        top8 = sb("top8", [P, 2, 8])
        top_i = sb("top_i", [P, 2, 8], U32)
        top_f = sb("top_f", [P, 2, 2])
        hot = sb("hot", [P, 2, 2, EXPERTS])
        hots = sb("hots", [P, 2, EXPERTS], BF16)
        slot = sb("slot", [P, 2, EXPERTS])
        picked = sb("picked", [P, 2, 2, EXPERTS])
        rec = sb("rec", [P, REC])
        slot_u = sb("slot_u", [P, 4], U32)
        lgm = sb("lgm", [P, 2, EXPERTS])
        ex = sb("ex", [P, 2, EXPERTS])
        exs = sb("exs", [P, 2])
        exr = sb("exr", [P, 2])
        prob = sb("prob", [P, 2, EXPERTS])
        held = sb("held", [P, 1])
        held_p = sb("held_p", [P, 1])
        nothing = sb("nothing", [P, DIM])

        loads = sem("loads")
        zeroed = sem("zeroed")
        set_up = sem("set_up")
        x_in = sem("x_in")
        h2_out = sem("h2_out")
        rows_out = sem("rows_out")

        A1_PE = Steps(sem("a1_pe"), "xt0 xt1 xt2 tok0 tok1 mean var xT kq0 kq1 kq2 v")
        A1_ACT = Steps(sem("a1_act"), "xt0 xt2 sq0 sq1 xn xTa xTb k0 k1 k2 q_hi0 k_hi q_hi1 q_hi2 v0 v1")
        A1_DVE = Steps(sem("a1_dve"), "xt1 tok0 tok1 nmean var shift lnw lnb q_lo0 k_st q_lo1 q_lo2")
        A1_POOL = Steps(sem("a1_pool"), "rstd")
        A2_PE = Steps(sem("a2_pe"), upto("sa", 12) + " nmT " + upto("sb", 7, "o0", 12, "o1 o2 oT0 oT1"))
        A2_ACT = Steps(sem("a2_act"), upto("exp", 7, "ot0", 12, "ot1 ot2"))
        A2_DVE = Steps(sem("a2_dve"), upto("max", 12) + " nmh nml nmT rz0 on0 h0 rz1 on1 h1 "
                       "bs0 bs1 ba0 ba1 ve shift x0 x1")
        A2_POOL = Steps(sem("a2_pool"), "tok rstd")
        B1_PE = Steps(sem("b1_pe"), "xT qk0 qk1 qk2 " + upto("s", 2, "v", 8, "c0", 12, "c1 c2"))
        B1_ACT = Steps(sem("b1_act"), "xTa xTb q0 q1 q2 k0 k1 k2 " + upto("exp", 2, "v0 v1", 8, "ct0", 12, "ct1 ct2"))
        B1_DVE = Steps(sem("b1_dve"), "q_hi q_lo k_hi k_st "
                       + upto("max", 6, "rz0 vs0", 11, "rz1 vs1", 12, "rz2 vs2"))
        B1_POOL = Steps(sem("b1_pool"), "h1b")
        B2_PE = Steps(sem("b2_pe"), "wo x3T logits rank")
        B2_ACT = Steps(sem("b2_act"), "x3Ta x3Tb ex")
        B2_DVE = Steps(sem("b2_dve"), "h20 h21 bs0 bs1 ba0 ba1 ve shift x0 x1 lg0 lg1 top0 top1 ti0 ti1 topf diff "
                       "hot0 hot1 hots lgm slot pick0 pos0 pick1 pos1 base slotu recf rec exs exr prob sum")
        B2_POOL = Steps(sem("b2_pool"), "rstd")
        km_in, qh_in, ql_in, q2h_in, q2l_in = (sem(n) for n in ("km_in", "qh_in", "ql_in", "q2h_in", "q2l_in"))
        PLACED = 16 * 4

        tA1, tA2, tB1, tB2 = (ps[:, b, :] for b in (2, 3, 6, 7))

        A1_T = [("xt0", A1_ACT, "xt0"), ("xt1", A1_DVE, "xt1"), ("xt2", A1_ACT, "xt2"), ("tok0", A1_DVE, "tok1"),
                ("mean", A1_DVE, "nmean"), ("var", A1_DVE, "var"), ("xT", A1_ACT, "xTb"), ("kq0", A1_ACT, "k1"),
                ("kq2", A1_DVE, "q_lo2")]
        A2_T = [("nmT", A2_DVE, "nmT"), ("o0", A2_ACT, "ot0"), ("o1", A2_ACT, "ot1"), ("o2", A2_ACT, "ot2"),
                ("oT0", A2_DVE, "on0"), ("oT1", A2_DVE, "on1")]
        A1_KQ = (tA1, tA2, tA1)
        B1_T = [("xT", B1_ACT, "xTb"), ("qk0", B1_ACT, "q1"), ("qk1", B1_ACT, "k0"), ("qk2", B1_ACT, "k2"),
                ("v", B1_ACT, "v1"), ("c0", B1_ACT, "ct0"), ("c1", B1_ACT, "ct1"), ("c2", B1_ACT, "ct2")]
        B2_T = [("wo", B2_DVE, "h21"), ("x3T", B2_ACT, "x3Tb"), ("logits", B2_DVE, "lg1"), ("rank", B2_DVE, "base")]

        def empty(eng, table, name, i):
            n = [row[0] for row in table].index(name)
            _, steps, reader = table[n - 1]
            eng.wait_ge(steps.sem, steps.at(i, reader, before=1 if n == 0 else 0))

        def stages(i, a1, a2, b1, b2):
            return ((lambda f, *rest: f(i, *rest) if a1 else None), (lambda f, *rest: f(i - 1, *rest) if a2 else None),
                    (lambda f, *rest: f(i - 2, *rest) if b1 else None), (lambda f, *rest: f(i - 3, *rest) if b2 else None))

        def turns(eng, body):
            body(0, *stages(0, 1, 0, 0, 0))
            body(1, *stages(1, 1, 1, 0, 0))
            body(2, *stages(2, 1, 1, 1, 0))
            with eng.Fori(3, IMAGES) as i:
                body(i, *stages(i, 1, 1, 1, 1))
            body(IMAGES, *stages(IMAGES, 0, 1, 1, 1))
            body(IMAGES + 1, *stages(IMAGES + 1, 0, 0, 1, 1))
            body(IMAGES + 2, *stages(IMAGES + 2, 0, 0, 0, 1))

        block = ctx.enter_context(nc.Block())
        W = ins
        n_loads = []

        @block.sync
        def _(sp):
            def load(dst, src):
                sp.dma_start(dst, src).then_inc(loads, 16)
                n_loads.append(1)

            sp.wait_ge(zeroed, 1)
            for dst, name in ((ident, "ident"), (wm, "wm"), (wq1, "wq1"), (wk1, "wk1"),
                              (wv1a, "wv1a"), (wv1b, "wv1b"), (wq2a, "wq2a"), (wq2b, "wq2b"), (wk2a, "wk2a"),
                              (wk2b, "wk2b"), (wv2a, "wv2a"), (wv2b, "wv2b"), (bias, "bias"), (wo, "wo"),
                              (rw_a, "rw_a"), (rw_b, "rw_b"),
                              (neg_lo, "neg_lo"), (sel_f, "sel"), (iota_e, "iota_e"), (tri_f, "tri"),
                              (valid, "valid"), (base, "first_slot")):
                load(dst[:], W[name][:])
            load(bo[:, :], W["bo"].to_broadcast([P, DIM]))
            for c in range(2):
                s0, n = START[c], ROWS[c]
                load(pos_emb[0:n, c, :], W["pos_emb"][s0:s0 + n, :])
                load(ln_w[0:n, c, :], W["ln_w"][s0:s0 + n, :])
                load(ln_b[0:n, c, :], W["ln_b"][s0:s0 + n, :])
                load(addend[:, c, :], W["b_map"].to_broadcast([P, DIM]))
            sp.wait_ge(loads, 16 * len(n_loads))
            load(addend[0:1, 0, :], W["cls"][:, :])

            def load_x(i):
                sp.wait_ge(A1_PE.sem, A1_PE.at(i, "xt2", before=1))
                img = W["x"][bass.ds(i, 1)].rearrange("b p k -> (b p) k")
                sp.dma_start(X[1:P, 0, :], img[0:P - 1, :]).then_inc(x_in, 16)
                sp.dma_start(X[0:ROWS[1], 1, :], img[P - 1:PATCHES, :]).then_inc(x_in, 16)

            def place_heads(dst, src, rows, placed):
                for j in range(4):
                    at = slice(32 * j, 32 * j + rows)
                    sp.dma_start(dst[at, j::4, :].bitcast(F32), src[at, :, :].bitcast(F32)).then_inc(placed, 16)

            def a1_keys(i):
                sp.wait_ge(A1_ACT.sem, A1_ACT.at(i, "k_hi"))
                place_heads(k_msk, k_hi, DH, km_in)

            def a1_queries(i):
                sp.wait_ge(A1_ACT.sem, A1_ACT.at(i, "q_hi2"))
                place_heads(qm_hi, q_hi, 2 * DH, qh_in)
                sp.wait_ge(A1_DVE.sem, A1_DVE.at(i, "q_lo2"))
                place_heads(qm_lo, q_lo, DH, ql_in)

            def b1_queries(i):
                sp.wait_ge(B1_DVE.sem, B1_DVE.at(i, "q_hi"))
                place_heads(q2m_hi, q2_hi, 2 * DH, q2h_in)
                sp.wait_ge(B1_DVE.sem, B1_DVE.at(i, "q_lo"))
                place_heads(q2m_lo, q2_lo, DH, q2l_in)

            def store_h2(i):
                sp.wait_ge(B2_DVE.sem, B2_DVE.at(i, "h21"))
                for c in range(2):
                    sp.dma_start(h2d[bass.ds(i * SEQ + START[c], ROWS[c]), :], h2[0:ROWS[c], c, :])\
                        .then_inc(h2_out, 16)

            def body(j):
                steps = [(store_h2, 4), (b1_queries, 3), (load_x, 0), (a1_keys, 1), (a1_queries, 1)]
                for step, behind in steps:
                    if not isinstance(j, int) or 0 <= j - behind < IMAGES:
                        step(j - behind)

            for j in range(4):
                body(j)
            with sp.Fori(4, IMAGES) as j:
                body(j)
            for j in range(IMAGES, IMAGES + 4):
                body(j)
            sp.wait_ge(h2_out, 32 * IMAGES + 32)

        @block.gpsimd
        def _(pool):
            for steps in (A1_POOL, A2_POOL, B1_POOL, B2_POOL):
                pool.sem_inc(steps.sem, len(steps.names))
            for t in (nothing, X, tok, tok_sum, sq, ln_w, ln_b, pos_emb, xTb, x2Tb, nmax, nmT, PA, PB, h1, h2, mv2, mv3,
                      v2, v2s, va, lg, prob_sum):
                pool.memset(t[:], 0.0)
            pool.memset(Z2[:], 1.0)
            pool.memset(ones[:], 1.0)
            pool.memset(ones_b[:], 1.0)
            for t in (k_msk, qm_hi, qm_lo, q2m_hi, q2m_lo):
                pool.memset(t[:].bitcast(F32), 0.0)
            pool.memset(zero[:], 0.0)
            pool.memset(neg_half[:], -0.5)
            pool.memset(mean_mat[:], 1.0 / (SEQ * DIM)).then_inc(zeroed, 1)
            pool.wait_ge(set_up, 9)
            for t in range(SPARE):
                pool.dma_start(xs[EXPERTS * CAP + t * P:EXPERTS * CAP + (t + 1) * P, :], nothing[:, :])\
                    .then_inc(rows_out, 16)

            def a_rstd(i):
                pool.wait_ge(A1_DVE.sem, A1_DVE.at(i, "var"))
                pool.tensor_tensor(rstd[:, :], var_eps[:, :], neg_half[:, 0:1], ALU.pow)\
                    .then_inc(A1_POOL.sem, A1_POOL.step("rstd"))

            def a_keep(i):
                pool.wait_ge(A1_DVE.sem, A1_DVE.at(i, "tok1"))
                pool.wait_ge(A2_DVE.sem, A2_DVE.at(i, "h1", before=1))
                pool.tensor_tensor(tok2[:, :, :], tok[:, :, :], zero[:, :].unsqueeze(2).to_broadcast([P, 2, DIM]),
                                   ALU.add).then_inc(A2_POOL.sem, A2_POOL.step("tok"))

            def b_residual(i):
                pool.wait_ge(A2_DVE.sem, A2_DVE.at(i, "h1"))
                pool.wait_ge(B2_DVE.sem, B2_DVE.at(i, "h21", before=1))
                pool.tensor_tensor(h1b[:, :, :], h1[:, :, :], bo[:, :].unsqueeze(1).to_broadcast([P, 2, DIM]),
                                   ALU.add).then_inc(B1_POOL.sem, B1_POOL.step("h1b"))

            def a_rstd2(i):
                pool.wait_ge(A2_DVE.sem, A2_DVE.at(i, "ve"))
                pool.tensor_tensor(rstd2[:, :], ve2[:, :], neg_half[:, :], ALU.pow)\
                    .then_inc(A2_POOL.sem, A2_POOL.step("rstd"))

            def b_rstd3(i):
                pool.wait_ge(B2_DVE.sem, B2_DVE.at(i, "ve"))
                pool.tensor_tensor(rstd3[:, :], ve3[:, :], neg_half[:, :], ALU.pow)\
                    .then_inc(B2_POOL.sem, B2_POOL.step("rstd"))

            def b_scatter(i):
                pool.wait_ge(B2_DVE.sem, B2_DVE.at(i, "slotu"))
                pool.tensor_tensor(held_p[:, :], neg_half[:, 0:1], neg_half[:, 0:1], ALU.add)
                for k in range(2):
                    for c in range(2):
                        n = ROWS[c]
                        pool.indirect_dma_start(
                            out=xs[:, :],
                            out_offset=bass.IndirectOffsetOnAxis(ap=slot_u[0:n, 2 * k + c:2 * k + c + 1], axis=0),
                            in_=x3[0:n, c, :], in_offset=None).then_inc(rows_out, 16)

            def body(i, a1, a2, b1, b2):
                b2(b_rstd3)
                a2(a_keep)
                b1(b_residual)
                a1(a_rstd)
                b2(b_scatter)
                a2(a_rstd2)

            turns(pool, body)
            pool.wait_ge(rows_out, 64 * IMAGES + 16 * SPARE)

        @block.tensor
        def _(pe):
            for steps in (A1_PE, A2_PE, B1_PE, B2_PE):
                pe.sem_inc(steps.sem, len(steps.names))
            pe.wait_ge(set_up, 9)

            def a_columns(i, n):
                if n == 0:
                    pe.wait_ge(x_in, i * 32 + 32)
                empty(pe, A1_T, f"xt{n}", i)
                for kk in range(2):
                    k = 2 * n + kk
                    for c in range(2):
                        r, o = ROWS[c], kk * SEQ + START[c]
                        mm = pe.transpose(tA1[:, o:o + r], X[0:r, c, k * P:(k + 1) * P], ident[0:r, 0:r])
                mm.then_inc(A1_PE.sem, A1_PE.step(f"xt{n}"))

            def a_embed(i, c):
                if c == 0:
                    empty(pe, A1_T, "tok0", i)
                    pe.wait_ge(A1_ACT.sem, A1_ACT.at(i, "xt2"))
                for k in range(KCH):
                    mm = pe.matmul(tA1[0:ROWS[c], c * DIM:(c + 1) * DIM], XT[:, k, START[c]:START[c] + ROWS[c]],
                                   wm[:, k, :], start=(k == 0), stop=(k == KCH - 1))
                mm.then_inc(A1_PE.sem, A1_PE.step(f"tok{c}"))

            def a_mean(i):
                empty(pe, A1_T, "mean", i)
                pe.wait_ge(A1_DVE.sem, A1_DVE.at(i, "tok1"))
                pe.matmul(tA1[:, 0:2], mean_mat[:, :], tok_sum[:, :], start=True, stop=True)\
                    .then_inc(A1_PE.sem, A1_PE.step("mean"))

            def a_var(i):
                empty(pe, A1_T, "var", i)
                pe.wait_ge(A1_ACT.sem, A1_ACT.at(i, "sq1"))
                pe.matmul(tA1[:, 0:2], mean_mat[:, :], sq[:, :], start=True, stop=True)\
                    .then_inc(A1_PE.sem, A1_PE.step("var"))

            def turn_rows(t, src):
                for f, (lo, hi) in enumerate(((0, P), (P, DIM))):
                    for c in range(2):
                        r, o = ROWS[c], f * SEQ + START[c]
                        mm = pe.transpose(t[0:hi - lo, o:o + r], src[0:r, c, lo:hi], ident[0:r, 0:r])
                return mm

            def a_turn(i):
                empty(pe, A1_T, "xT", i)
                pe.wait_ge(A1_DVE.sem, A1_DVE.at(i, "lnb"))
                turn_rows(tA1, xh).then_inc(A1_PE.sem, A1_PE.step("xT"))

            def a_project(i, n):
                if n == 1:
                    pe.wait_ge(A2_DVE.sem, A2_DVE.at(i, "on1", before=1))
                else:
                    empty(pe, A1_T, f"kq{n}", i)
                for kk in range(2):
                    m = 2 * n + kk
                    w, g = (wk1, m) if m < GROUPS else (wq1, m - GROUPS)
                    o = A1_KQ[n][:, kk * SEQ:(kk + 1) * SEQ]
                    if g < 2:
                        mm = pe.matmul(o, w[:, g, :], xTa[:, :], start=True, stop=True)
                    else:
                        mm = pe.matmul(o, w[0:DIM - P, g, :], xTb[0:DIM - P, :], start=True, stop=True)
                mm.then_inc(A1_PE.sem, A1_PE.step(f"kq{n}"))

            def project_values(steps, t, xa, xb, wa, wb):
                for c in range(2):
                    s = slice(START[c], START[c] + ROWS[c])
                    o = t[0:ROWS[c], c * DIM:(c + 1) * DIM]
                    pe.matmul(o, xa[:, s], wa[:, :], start=True, stop=False)
                    mm = pe.matmul(o, xb[:, s], wb[:, :], start=False, stop=True)
                mm.then_inc(steps.sem, steps.step("v"))

            def a_project_values(i):
                pe.wait_ge(A1_DVE.sem, A1_DVE.at(i, "q_lo0"))
                project_values(A1_PE, tA2, xTa, xTb, wv1a, wv1b)

            def a_rough(i, u):
                p, c = divmod(u, 2)
                g = group_of(p)
                if u == 0:
                    pe.wait_ge(km_in, PLACED * i + PLACED)
                    pe.wait_ge(A1_ACT.sem, A1_ACT.at(i, "q_hi2"))
                if u < 2:
                    pe.wait_ge(A2_ACT.sem, A2_ACT.at(i, f"exp{10 + c}", before=1))
                else:
                    pe.wait_ge(A2_DVE.sem, A2_DVE.at(i, f"max{u - 2}"))
                pe.matmul(ps[0:ROWS[c], c, 0:2 * SEQ], q_hi[:, g, START[c]:START[c] + ROWS[c]],
                          k_msk[:, 2 * p:2 * p + 2, :].rearrange("p a b -> p (a b)"), start=True, stop=True)\
                    .then_inc(A2_PE.sem, A2_PE.step(f"sa{u}"))

            def a_max_rows(i):
                pe.wait_ge(A1_ACT.sem, A1_ACT.at(i, "v1"))
                pe.wait_ge(A2_DVE.sem, A2_DVE.at(i, "nml"))
                tb = tA2.bitcast(BF16)
                for c in range(2):
                    mm = pe.transpose(tb[0:2 * HEADS, START[c]:START[c] + ROWS[c]], nm[0:ROWS[c], c, :],
                                      ident_b[0:ROWS[c], 0:ROWS[c]])
                mm.then_inc(A2_PE.sem, A2_PE.step("nmT"))

            def a_scores(i, u):
                p, c = divmod(u, 2)
                g = group_of(p)
                if u == 0:
                    pe.wait_ge(A2_DVE.sem, A2_DVE.at(i, "nmT"))
                    pe.wait_ge(qh_in, PLACED * i + PLACED)
                    pe.wait_ge(ql_in, PLACED * i + PLACED)
                if u < 2:
                    pe.wait_ge(A2_DVE.sem, A2_DVE.at(i, f"max{10 + c}"))
                else:
                    pe.wait_ge(A2_ACT.sem, A2_ACT.at(i, f"exp{u - 2}"))
                r = ROWS[c]
                o = ps[0:r, c, 0:2 * SEQ]
                k = k_st[:, g, START[c]:START[c] + r]
                for a in range(2):
                    pe.matmul(ps[0:r, c, a * SEQ:(a + 1) * SEQ], sel[:, 2 * p + a, 0:r], nmT[:, :],
                              start=(a == 0), stop=False, skip_group_check=True)
                pe.matmul(o, k, qm_hi[:, 2 * p:2 * p + 2, :].rearrange("p a b -> p (a b)"), start=False, stop=False,
                          skip_group_check=True)
                mm = pe.matmul(o, k, qm_lo[:, 2 * p:2 * p + 2, :].rearrange("p a b -> p (a b)"), start=False, stop=True,
                               skip_group_check=True)
                mm.then_inc(A2_PE.sem, A2_PE.step(f"sb{u}"))

            def a_values(i, g):
                empty(pe, A2_T, f"o{g}", i)
                pe.wait_ge(A2_ACT.sem, A2_ACT.at(i, f"exp{4 * g + 3}"))
                for c in range(2):
                    for j in range(4):
                        mm = pe.matmul(tA2[32 * j:32 * j + 32, 0:SEQ], va[:, 4 * g + j, c, :], PA[:, g % 2, c, j, :],
                                       start=(c == 0), stop=(c == 1), tile_position=(0, 32 * j))
                mm.then_inc(A2_PE.sem, A2_PE.step(f"o{g}"))

            def a_turn_back(i, c):
                if c == 0:
                    pe.wait_ge(A2_ACT.sem, A2_ACT.at(i, "ot2"))
                empty(pe, A2_T, f"oT{c}", i)
                for g in range(GROUPS):
                    mm = pe.transpose(tA2[0:ROWS[c], g * P:(g + 1) * P],
                                      OT[:, g, START[c]:START[c] + ROWS[c]], ident[:, :])
                mm.then_inc(A2_PE.sem, A2_PE.step(f"oT{c}"))

            def b_turn(i):
                empty(pe, B1_T, "xT", i)
                pe.wait_ge(A2_DVE.sem, A2_DVE.at(i, "x1"))
                turn_rows(tB1, x2).then_inc(B1_PE.sem, B1_PE.step("xT"))

            def b_project(i, n):
                empty(pe, B1_T, f"qk{n}", i)
                for kk in range(2):
                    m = 2 * n + kk
                    wa, wb, g = (wq2a, wq2b, m) if m < GROUPS else (wk2a, wk2b, m - GROUPS)
                    o = tB1[:, kk * SEQ:(kk + 1) * SEQ]
                    pe.matmul(o, wa[:, g, :], x2Ta[:, :], start=True, stop=False)
                    mm = pe.matmul(o, wb[:, g, :], x2Tb[0:DIM - P, :], start=False, stop=True)
                mm.then_inc(B1_PE.sem, B1_PE.step(f"qk{n}"))

            def b_project_values(i):
                empty(pe, B1_T, "v", i)
                project_values(B1_PE, tB1, x2Ta, x2Tb, wv2a, wv2b)

            def b_scores(i, u):
                p, c = divmod(u, 2)
                g = group_of(p)
                if u == 0:
                    pe.wait_ge(B1_DVE.sem, B1_DVE.at(i, "k_st"))
                    pe.wait_ge(q2h_in, PLACED * i + PLACED)
                    pe.wait_ge(q2l_in, PLACED * i + PLACED)
                if u < 2:
                    pe.wait_ge(B1_ACT.sem, B1_ACT.at(i, f"exp{10 + c}", before=1))
                else:
                    pe.wait_ge(B1_ACT.sem, B1_ACT.at(i, f"exp{u - 2}"))
                o = ps[0:ROWS[c], 4 + c, 0:2 * SEQ]
                k = k2_st[:, g, START[c]:START[c] + ROWS[c]]
                pe.matmul(o, k, q2m_hi[:, 2 * p:2 * p + 2, :].rearrange("p a b -> p (a b)"), start=True, stop=False)
                pe.matmul(o, k, q2m_lo[:, 2 * p:2 * p + 2, :].rearrange("p a b -> p (a b)"), start=False, stop=True)\
                    .then_inc(B1_PE.sem, B1_PE.step(f"s{u}"))

            def b_values(i, g):
                empty(pe, B1_T, f"c{g}", i)
                pe.wait_ge(B1_ACT.sem, B1_ACT.at(i, f"exp{4 * g + 3}"))
                pe.wait_ge(B1_DVE.sem, B1_DVE.at(i, f"vs{g}"))
                for c in range(2):
                    for j in range(4):
                        mm = pe.matmul(tB1[32 * j:32 * j + 32, 0:SEQ], v2s[:, 4 * g + j, c, :], PB[:, g % 2, c, j, :],
                                       start=(c == 0), stop=(c == 1), tile_position=(0, 32 * j))
                mm.then_inc(B1_PE.sem, B1_PE.step(f"c{g}"))

            def b_out(i):
                empty(pe, B2_T, "wo", i)
                pe.wait_ge(B1_ACT.sem, B1_ACT.at(i, "ct2"))
                for c in range(2):
                    for g in range(GROUPS):
                        mm = pe.matmul(tB2[0:ROWS[c], c * DIM:(c + 1) * DIM], CT[:, g, START[c]:START[c] + ROWS[c]],
                                       wo[:, g, :], start=(g == 0), stop=(g == GROUPS - 1))
                mm.then_inc(B2_PE.sem, B2_PE.step("wo"))

            def b_turn_rows(i):
                empty(pe, B2_T, "x3T", i)
                pe.wait_ge(B2_DVE.sem, B2_DVE.at(i, "x1"))
                turn_rows(tB2, x3).then_inc(B2_PE.sem, B2_PE.step("x3T"))

            def b_logits(i):
                empty(pe, B2_T, "logits", i)
                for c in range(2):
                    s = slice(START[c], START[c] + ROWS[c])
                    o = tB2[0:ROWS[c], c * EXPERTS:(c + 1) * EXPERTS]
                    pe.matmul(o, x3Ta[:, s], rw_a[:, :], start=True, stop=False)
                    mm = pe.matmul(o, x3Tb[:, s], rw_b[:, :], start=False, stop=True)
                mm.then_inc(B2_PE.sem, B2_PE.step("logits"))

            def b_rank(i):
                empty(pe, B2_T, "rank", i)
                pe.wait_ge(B2_DVE.sem, B2_DVE.at(i, "hots"))
                t, E = tB2, EXPERTS
                pe.matmul(t[:, 0:E], tri[:, :], hots[:, 0, :], start=True, stop=True)
                pe.matmul(t[:, E:2 * E], tri[:, :], hots[:, 1, :], start=True, stop=False)
                pe.matmul(t[:, E:2 * E], ones_b[:, :], hots[:, 0, :], start=False, stop=True)
                pe.matmul(t[:, 2 * E:3 * E], ones_b[:, :], hots[:, 0, :], start=True, stop=False)
                pe.matmul(t[:, 2 * E:3 * E], ones_b[:, :], hots[:, 1, :], start=False, stop=True)\
                    .then_inc(B2_PE.sem, B2_PE.step("rank"))

            def body(i, a1, a2, b1, b2):
                a1(a_columns, 0)
                b2(b_out)
                a2(a_rough, 0)
                a2(a_rough, 1)
                b1(b_turn)
                a2(a_rough, 2)
                a2(a_rough, 3)
                b1(b_project, 0)
                a2(a_rough, 4)
                a2(a_rough, 5)
                a1(a_columns, 1)
                b1(b_project, 1)
                a2(a_rough, 6)
                a2(a_rough, 7)
                b1(b_project, 2)
                a2(a_rough, 8)
                a2(a_rough, 9)
                a1(a_columns, 2)
                a2(a_rough, 10)
                a2(a_rough, 11)
                b2(b_turn_rows)
                a1(a_embed, 0)
                a2(a_max_rows)
                a2(a_scores, 0)
                a2(a_scores, 1)
                a1(a_embed, 1)
                b1(b_scores, 0)
                b1(b_scores, 1)
                a2(a_scores, 2)
                b2(b_logits)
                b1(b_project_values)
                a2(a_scores, 3)
                a1(a_mean)
                a2(a_scores, 4)
                b1(b_scores, 2)
                a2(a_scores, 5)
                b1(b_scores, 3)
                a1(a_var)
                a2(a_scores, 6)
                a2(a_values, 0)
                a2(a_scores, 7)
                b1(b_scores, 4)
                a2(a_scores, 8)
                b1(b_scores, 5)
                b2(b_rank)
                a2(a_scores, 9)
                b1(b_scores, 6)
                a2(a_scores, 10)
                b1(b_scores, 7)
                a2(a_scores, 11)
                a2(a_values, 1)
                b1(b_values, 0)
                b1(b_scores, 8)
                a2(a_values, 2)
                a1(a_turn)
                b1(b_scores, 9)
                a2(a_turn_back, 0)
                b1(b_scores, 10)
                a1(a_project, 0)
                a2(a_turn_back, 1)
                b1(b_scores, 11)
                a1(a_project, 1)
                b1(b_values, 1)
                a1(a_project, 2)
                a1(a_project_values)
                b1(b_values, 2)

            turns(pe, body)

        @block.scalar
        def _(act):
            for steps in (A1_ACT, A2_ACT, B1_ACT, B2_ACT):
                act.sem_inc(steps.sem, len(steps.names))
            act.wait_ge(set_up, 9)

            def a_xt(i, n):
                act.wait_ge(A1_PE.sem, A1_PE.at(i, f"xt{n}"))
                act.copy(XT[:, 2 * n:2 * n + 2, :], tA1[:, 0:2 * SEQ].rearrange("p (a b) -> p a b", a=2))\
                    .then_inc(A1_ACT.sem, A1_ACT.step(f"xt{n}"))

            def a_squares(i):
                act.wait_ge(A1_DVE.sem, A1_DVE.at(i, "nmean"))
                for c in range(2):
                    r = ROWS[c]
                    act.activation(junk_sq[0:r, c, :], tok[0:r, c, :], ACT.Square, bias=neg_mean[0:r, :],
                                   accum_out=sq[0:r, c:c + 1]).then_inc(A1_ACT.sem, A1_ACT.step(f"sq{c}"))

            def a_normal(i):
                act.wait_ge(A1_DVE.sem, A1_DVE.at(i, "shift"))
                act.activation(xh[:, :, :], tok[:, :, :], ACT.Identity, bias=shift[:, :], scale=rstd[:, :])\
                    .then_inc(A1_ACT.sem, A1_ACT.step("xn"))

            def columns(steps, t, a, b, names):
                act.copy(a, t[:, 0:SEQ]).then_inc(steps.sem, steps.step(names[0]))
                act.copy(b, t[0:DIM - P, SEQ:2 * SEQ]).then_inc(steps.sem, steps.step(names[1]))

            def a_columns(i):
                act.wait_ge(A1_PE.sem, A1_PE.at(i, "xT"))
                columns(A1_ACT, tA1, xTa[:, :], xTb[0:DIM - P, :], ("xTa", "xTb"))

            def a_keys(i, n):
                act.wait_ge(A1_PE.sem, A1_PE.at(i, f"kq{n}"))
                if n == 0:
                    act.wait_ge(A1_DVE.sem, A1_DVE.at(i, "k_st", before=1))
                for g in ((0, 1), (2,))[n]:
                    act.activation(k_full[:, g, :], A1_KQ[n][:, (g % 2) * SEQ:(g % 2 + 1) * SEQ], ACT.Identity,
                                   bias=bias[:, 1, g:g + 1]).then_inc(A1_ACT.sem, A1_ACT.step(f"k{g}"))

            def a_query(i, g, at):
                act.activation(q_hi[:, g, :], A1_KQ[1 if g == 0 else 2][:, at * SEQ:(at + 1) * SEQ], ACT.Identity,
                               bias=bias[:, 0, g:g + 1]).then_inc(A1_ACT.sem, A1_ACT.step(f"q_hi{g}"))

            def a_key_parts(i):
                a_query(i, 0, 1)
                act.wait_ge(A1_ACT.sem, A1_ACT.at(i, "k2"))
                act.copy(k_hi[:, :, :], k_full[:, :, :]).then_inc(A1_ACT.sem, A1_ACT.step("k_hi"))

            def a_queries(i):
                act.wait_ge(A1_PE.sem, A1_PE.at(i, "kq2"))
                for g in (1, 2):
                    a_query(i, g, g - 1)

            def a_values(i):
                act.wait_ge(A1_PE.sem, A1_PE.at(i, "v"))
                act.wait_ge(A2_PE.sem, A2_PE.at(i, "o2", before=1))
                for c in range(2):
                    r = ROWS[c]
                    act.copy(va[0:r, :, c, 0:DH], tA2[0:r, c * DIM:(c + 1) * DIM].rearrange("p (h d) -> p h d", h=HEADS))\
                        .then_inc(A1_ACT.sem, A1_ACT.step(f"v{c}"))

            def a_exp(i, u):
                p, c = divmod(u, 2)
                g, r = group_of(p), ROWS[c]
                act.wait_ge(A2_PE.sem, A2_PE.at(i, f"sb{u}"))
                if u == 8:
                    act.wait_ge(A2_PE.sem, A2_PE.at(i, "o0"))
                act.activation(PA[0:r, g % 2, c, 2 * (p % 2):2 * (p % 2) + 2, :],
                               ps[0:r, c, 0:2 * SEQ].rearrange("p (a b) -> p a b", a=2), ACT.Exp, scale=SCALE)\
                    .then_inc(A2_ACT.sem, A2_ACT.step(f"exp{u}"))

            def a_ot(i, g):
                act.wait_ge(A2_PE.sem, A2_PE.at(i, f"o{g}"))
                act.copy(OT[:, g, :], tA2[:, 0:SEQ]).then_inc(A2_ACT.sem, A2_ACT.step(f"ot{g}"))

            def b_columns(i):
                act.wait_ge(B1_PE.sem, B1_PE.at(i, "xT"))
                columns(B1_ACT, tB1, x2Ta[:, :], x2Tb[0:DIM - P, :], ("xTa", "xTb"))

            def b_operands(i, n):
                act.wait_ge(B1_PE.sem, B1_PE.at(i, f"qk{n}"))
                for m in (2 * n, 2 * n + 1):
                    src = tB1[:, (m % 2) * SEQ:(m % 2 + 1) * SEQ]
                    if m < GROUPS:
                        act.activation(q2_full[:, m, :], src, ACT.Identity, bias=bias_q[:, m:m + 1], scale=SCALE)\
                            .then_inc(B1_ACT.sem, B1_ACT.step(f"q{m}"))
                    else:
                        g = m - GROUPS
                        act.activation(k2_full[:, g, :], src, ACT.Identity, bias=bias[:, 3, g:g + 1])\
                            .then_inc(B1_ACT.sem, B1_ACT.step(f"k{g}"))

            def b_values(i):
                act.wait_ge(B1_PE.sem, B1_PE.at(i, "v"))
                for c in range(2):
                    r = ROWS[c]
                    act.copy(v2[0:r, :, c, :], tB1[0:r, c * DIM:(c + 1) * DIM].rearrange("p (h d) -> p h d", h=HEADS))\
                        .then_inc(B1_ACT.sem, B1_ACT.step(f"v{c}"))

            def b_exp(i, u):
                p, c = divmod(u, 2)
                g, r = group_of(p), ROWS[c]
                act.wait_ge(B1_DVE.sem, B1_DVE.at(i, f"max{u}"))
                if u == 8:
                    act.wait_ge(B1_PE.sem, B1_PE.at(i, "c0"))
                for a in range(2):
                    h = 2 * p + a
                    e = act.activation(PB[0:r, g % 2, c, h % 4, :], ps[0:r, 4 + c, a * SEQ:(a + 1) * SEQ], ACT.Exp,
                                       bias=nmax2[0:r, c, h:h + 1], accum_out=Z2[0:r, h, c:c + 1])
                e.then_inc(B1_ACT.sem, B1_ACT.step(f"exp{u}"))

            def b_ct(i, g):
                act.wait_ge(B1_PE.sem, B1_PE.at(i, f"c{g}"))
                act.copy(CT[:, g, :], tB1[:, 0:SEQ]).then_inc(B1_ACT.sem, B1_ACT.step(f"ct{g}"))

            def b_x3(i):
                act.wait_ge(B2_PE.sem, B2_PE.at(i, "x3T"))
                columns(B2_ACT, tB2, x3Ta[:, :], x3Tb[:, :], ("x3Ta", "x3Tb"))

            def b_router(i):
                act.wait_ge(B2_DVE.sem, B2_DVE.at(i, "lgm"))
                act.activation(ex[:, :, :], lgm[:, :, :], ACT.Exp).then_inc(B2_ACT.sem, B2_ACT.step("ex"))

            def body(i, a1, a2, b1, b2):
                a1(a_xt, 0)
                b1(b_columns)
                b1(b_operands, 0)
                b1(b_operands, 1)
                b1(b_operands, 2)
                a1(a_xt, 2)
                b2(b_x3)
                a2(a_exp, 0)
                a2(a_exp, 1)
                b1(b_exp, 0)
                a2(a_exp, 2)
                b1(b_exp, 1)
                b1(b_values)
                a2(a_exp, 3)
                a1(a_squares)
                a2(a_exp, 4)
                b1(b_exp, 2)
                a2(a_exp, 5)
                b1(b_exp, 3)
                a2(a_exp, 6)
                a2(a_ot, 0)
                a2(a_exp, 7)
                b1(b_exp, 4)
                a1(a_normal)
                a2(a_exp, 8)
                b1(b_exp, 5)
                a2(a_exp, 9)
                b1(b_exp, 6)
                b2(b_router)
                a2(a_exp, 10)
                b1(b_exp, 7)
                a2(a_exp, 11)
                b1(b_ct, 0)
                a2(a_ot, 1)
                b1(b_exp, 8)
                a2(a_ot, 2)
                a1(a_columns)
                b1(b_exp, 9)
                a1(a_keys, 0)
                b1(b_exp, 10)
                a1(a_keys, 1)
                a1(a_key_parts)
                b1(b_exp, 11)
                b1(b_ct, 1)
                a1(a_queries)
                a1(a_values)
                b1(b_ct, 2)

            turns(act, body)

        @block.vector
        def _(dve):
            for steps in (A1_DVE, A2_DVE, B1_DVE, B2_DVE):
                dve.sem_inc(steps.sem, len(steps.names))
            dve.sem_inc(h2_out, 32)
            dve.wait_ge(zeroed, 1)
            dve.memset(xTb[DIM - P:, :], 1.0).then_inc(set_up, 1)
            dve.memset(x2Tb[DIM - P:, :], 1.0).then_inc(set_up, 1)
            for c in range(2):
                dve.memset(va[0:ROWS[c], :, c, DH:DH + 1], 1.0).then_inc(set_up, 1)
            dve.wait_ge(loads, 16 * len(n_loads))
            dve.tensor_tensor(addend[:, :, :], addend[:, :, :], pos_emb[:, :, :], ALU.add).then_inc(set_up, 1)
            dve.tensor_copy(ident_b[:, :], ident[:, :]).then_inc(set_up, 1)
            dve.tensor_copy(tri[:, :], tri_f[:, :]).then_inc(set_up, 1)
            dve.tensor_copy(sel[:, :, :], sel_f[:, :, :]).then_inc(set_up, 1)
            dve.tensor_scalar(bias_q[:, :], bias[:, 2, :], SCALE, None, ALU.mult).then_inc(set_up, 1)
            dve.wait_ge(set_up, 9)

            def after(steps, i, name):
                dve.wait_ge(steps.sem, steps.at(i, name))

            def hold():
                dve.memset(held[:, :], 0.0)

            def a_xt(i):
                dve.wait_ge(A1_PE.sem, A1_PE.at(i, "xt1"))
                dve.tensor_copy(XT[:, 2:4, :], tA1[:, 0:2 * SEQ].rearrange("p (a b) -> p a b", a=2))\
                    .then_inc(A1_DVE.sem, A1_DVE.step("xt1"))

            def a_tokens(i):
                dve.wait_ge(A2_POOL.sem, A2_POOL.at(i, "tok", before=1))
                dve.wait_ge(A1_PE.sem, A1_PE.at(i, "tok1"))
                for c in range(2):
                    r = ROWS[c]
                    dve.scalar_tensor_tensor(tok[0:r, c, :], tA1[0:r, c * DIM:(c + 1) * DIM], 1.0, addend[0:r, c, :],
                                             ALU.mult, ALU.add, accum_out=tok_sum[0:r, c:c + 1])\
                        .then_inc(A1_DVE.sem, A1_DVE.step(f"tok{c}"))

            def a_mean(i):
                dve.wait_ge(A1_PE.sem, A1_PE.at(i, "mean"))
                dve.tensor_reduce(neg_mean[:, :], tA1[:, 0:2], AX.X, ALU.add, negate=True)\
                    .then_inc(A1_DVE.sem, A1_DVE.step("nmean"))

            def a_var(i):
                dve.wait_ge(A1_PE.sem, A1_PE.at(i, "var"))
                dve.tensor_scalar(junk2[:, :], tA1[:, 0:2], 1.0, EPS, ALU.mult, ALU.add, accum_out=var_eps[:, :])\
                    .then_inc(A1_DVE.sem, A1_DVE.step("var"))

            def a_shift(i):
                dve.wait_ge(A1_POOL.sem, A1_POOL.at(i, "rstd"))
                dve.tensor_tensor(shift[:, :], neg_mean[:, :], rstd[:, :], ALU.mult)\
                    .then_inc(A1_DVE.sem, A1_DVE.step("shift"))

            def a_normal(i):
                dve.wait_ge(A1_ACT.sem, A1_ACT.at(i, "xn"))
                dve.tensor_tensor(xh[:, :, :], xh[:, :, :], ln_w[:, :, :], ALU.mult)\
                    .then_inc(A1_DVE.sem, A1_DVE.step("lnw"))
                after(A1_DVE, i, "lnw")
                dve.tensor_tensor(xh[:, :, :], xh[:, :, :], ln_b[:, :, :], ALU.add)\
                    .then_inc(A1_DVE.sem, A1_DVE.step("lnb"))

            def split_queries(steps, i, full, hi, lo):
                dve.tensor_copy(hi[:, :, :], full[:, :, :]).then_inc(steps.sem, steps.step("q_hi"))
                after(steps, i, "q_hi")
                dve.tensor_tensor(lo[:, :, :], full[:, :, :], hi[:, :, :].bitcast(F32), ALU.subtract)\
                    .then_inc(steps.sem, steps.step("q_lo"))

            def keys_left(steps, full, hi, st):
                dve.scalar_tensor_tensor(st[:, :, :], hi[:, :, :].bitcast(F32), neg_lo[:, 0:1], full[:, :, :],
                                         ALU.mult, ALU.add).then_inc(steps.sem, steps.step("k_st"))

            def a_query(i, g, at):
                dve.wait_ge(A1_ACT.sem, A1_ACT.at(i, f"q_hi{max(g, 2 * (g > 0))}"))
                dve.scalar_tensor_tensor(q_lo[:, g, :], A1_KQ[1 if g == 0 else 2][:, at * SEQ:(at + 1) * SEQ], bias[:, 0, g:g + 1],
                                         q_hi[:, g, :].bitcast(F32), ALU.add, ALU.subtract)\
                    .then_inc(A1_DVE.sem, A1_DVE.step(f"q_lo{g}"))

            def a_keys_and_query(i):
                a_query(i, 0, 1)
                dve.wait_ge(A1_ACT.sem, A1_ACT.at(i, "k_hi"))
                dve.wait_ge(A2_PE.sem, A2_PE.at(i, "sb11", before=1))
                keys_left(A1_DVE, k_full, k_hi, k_st)

            def a_queries(i):
                for g in (1, 2):
                    a_query(i, g, g - 1)

            def b_split_queries(i):
                dve.wait_ge(B1_ACT.sem, B1_ACT.at(i, "q2"))
                split_queries(B1_DVE, i, q2_full, q2_hi, q2_lo)

            def b_split_keys(i):
                dve.wait_ge(B1_ACT.sem, B1_ACT.at(i, "k2"))
                dve.tensor_copy(k2_hi[:, :, :], k2_full[:, :, :]).then_inc(B1_DVE.sem, B1_DVE.step("k_hi"))
                after(B1_DVE, i, "k_hi")
                keys_left(B1_DVE, k2_full, k2_hi, k2_st)

            def a_max(i, u):
                p, c = divmod(u, 2)
                dve.wait_ge(A2_PE.sem, A2_PE.at(i, f"sa{u}"))
                dve.tensor_reduce(nmax[0:ROWS[c], c, 2 * p:2 * p + 2],
                                  ps[0:ROWS[c], c, 0:2 * SEQ].rearrange("p (a b) -> p a b", a=2), AX.X, ALU.max,
                                  negate=True).then_inc(A2_DVE.sem, A2_DVE.step(f"max{u}"))

            def a_max_rows(i):
                after(A2_DVE, i, "max11")
                dve.tensor_copy(nm[:, :, 0:HEADS], nmax[:, :, :]).then_inc(A2_DVE.sem, A2_DVE.step("nmh"))
                after(A2_DVE, i, "nmh")
                dve.tensor_tensor(nm[:, :, HEADS:], nmax[:, :, :], nm[:, :, 0:HEADS], ALU.subtract)\
                    .then_inc(A2_DVE.sem, A2_DVE.step("nml"))
                dve.wait_ge(A2_PE.sem, A2_PE.at(i, "nmT"))
                dve.tensor_copy(nmT[0:2 * HEADS, :], tA2.bitcast(BF16)[0:2 * HEADS, 0:SEQ])\
                    .then_inc(A2_DVE.sem, A2_DVE.step("nmT"))

            def a_finish(i, c):
                if c == 0:
                    dve.wait_ge(A2_POOL.sem, A2_POOL.at(i, "tok"))
                    dve.wait_ge(B1_POOL.sem, B1_POOL.at(i, "h1b", before=1))
                r = ROWS[c]
                dve.wait_ge(A2_PE.sem, A2_PE.at(i, f"oT{c}"))
                o = tA2[0:r, 0:GROUPS * P].rearrange("p (h d) -> p h d", h=HEADS)
                dve.reciprocal(rzA[0:r, c, :], o[:, :, DH]).then_inc(A2_DVE.sem, A2_DVE.step(f"rz{c}"))
                after(A2_DVE, i, f"rz{c}")
                dve.tensor_tensor(on[0:r, c, :].rearrange("p (h d) -> p h d", h=HEADS), o[:, :, 0:DH],
                                  rzA[0:r, c, :].unsqueeze(2).to_broadcast([r, HEADS, DH]), ALU.mult)\
                    .then_inc(A2_DVE.sem, A2_DVE.step(f"on{c}"))
                after(A2_DVE, i, f"on{c}")
                dve.tensor_tensor(h1[0:r, c, :], on[0:r, c, :], tok2[0:r, c, :], ALU.add)\
                    .then_inc(A2_DVE.sem, A2_DVE.step(("h0", "h1")[c]))

            def moments(steps, i, src, st, mv, ve):
                for c in range(2):
                    dve.bn_stats(st[0:ROWS[c], c, :], src[0:ROWS[c], c, :]).then_inc(steps.sem, steps.step(f"bs{c}"))
                after(steps, i, "bs1")
                hold()
                for c in range(2):
                    dve.bn_aggr(mv[0:ROWS[c], c, :], st[0:ROWS[c], c, :]).then_inc(steps.sem, steps.step(f"ba{c}"))
                after(steps, i, "ba1")
                dve.tensor_scalar(ve[:, :], mv[:, :, 1], EPS, None, ALU.add).then_inc(steps.sem, steps.step("ve"))

            def normal(steps, pool_steps, i, src, dst, mv, rs, sh):
                dve.wait_ge(pool_steps.sem, pool_steps.at(i, "rstd"))
                dve.scalar_tensor_tensor(sh[:, :], mv[:, :, 0], -1.0, rs[:, :], ALU.mult, ALU.mult)\
                    .then_inc(steps.sem, steps.step("shift"))
                after(steps, i, "shift")
                for c in range(2):
                    dve.tensor_scalar(dst[:, c, :], src[:, c, :], rs[:, c:c + 1], sh[:, c:c + 1], ALU.mult, ALU.add)\
                        .then_inc(steps.sem, steps.step(f"x{c}"))

            def a_moments(i):
                after(A2_DVE, i, "h1")
                moments(A2_DVE, i, h1, st2, mv2, ve2)

            def a_normal2(i):
                normal(A2_DVE, A2_POOL, i, h1, x2, mv2, rstd2, shift2)

            def b_moments3(i):
                after(B2_DVE, i, "h21")
                moments(B2_DVE, i, h2, st3, mv3, ve3)

            def b_normal3(i):
                dve.wait_ge(rows_out, i * 64 + 16 * SPARE)
                normal(B2_DVE, B2_POOL, i, h2, x3, mv3, rstd3, shift3)

            def b_max(i, u):
                p, c = divmod(u, 2)
                dve.wait_ge(B1_PE.sem, B1_PE.at(i, f"s{u}"))
                dve.tensor_reduce(nmax2[0:ROWS[c], c, 2 * p:2 * p + 2],
                                  ps[0:ROWS[c], 4 + c, 0:2 * SEQ].rearrange("p (a b) -> p a b", a=2), AX.X, ALU.max,
                                  negate=True).then_inc(B1_DVE.sem, B1_DVE.step(f"max{u}"))

            def b_values(i, g):
                dve.wait_ge(B1_ACT.sem, B1_ACT.at(i, f"exp{4 * g + 3}"))
                h = slice(4 * g, 4 * g + 4)
                dve.reciprocal(rz2[:, h, :], Z2[:, h, :]).then_inc(B1_DVE.sem, B1_DVE.step(f"rz{g}"))
                after(B1_DVE, i, f"rz{g}")
                dve.tensor_tensor(v2s[:, h, :, 0:DH], v2[:, h, :, :],
                                  rz2[:, h, :].unsqueeze(3).to_broadcast([P, 4, 2, DH]), ALU.mult)\
                    .then_inc(B1_DVE.sem, B1_DVE.step(f"vs{g}"))

            def b_residual(i):
                dve.wait_ge(B2_PE.sem, B2_PE.at(i, "wo"))
                dve.wait_ge(B1_POOL.sem, B1_POOL.at(i, "h1b"))
                dve.wait_ge(h2_out, i * 32 + 32)
                for c in range(2):
                    r = ROWS[c]
                    dve.tensor_tensor(h2[0:r, c, :], tB2[0:r, c * DIM:(c + 1) * DIM], h1b[0:r, c, :], ALU.add)\
                        .then_inc(B2_DVE.sem, B2_DVE.step(f"h2{c}"))

            def b_choose(i):
                dve.wait_ge(B2_PE.sem, B2_PE.at(i, "logits"))
                for c in range(2):
                    dve.tensor_copy(lg[0:ROWS[c], c, :], tB2[0:ROWS[c], c * EXPERTS:(c + 1) * EXPERTS])\
                        .then_inc(B2_DVE.sem, B2_DVE.step(f"lg{c}"))
                after(B2_DVE, i, "lg1")
                hold()
                for c in range(2):
                    dve.max(top8[:, c, :], lg[:, c, :]).then_inc(B2_DVE.sem, B2_DVE.step(f"top{c}"))
                after(B2_DVE, i, "top1")
                hold()
                for c in range(2):
                    dve.max_index(top_i[:, c, :], top8[:, c, :], lg[:, c, :]).then_inc(B2_DVE.sem, B2_DVE.step(f"ti{c}"))
                after(B2_DVE, i, "ti1")
                dve.tensor_copy(top_f[:, :, :], top_i[:, :, 0:2]).then_inc(B2_DVE.sem, B2_DVE.step("topf"))
                dve.tensor_tensor(rec[:, 8:10], top8[:, :, 1], top8[:, :, 0], ALU.subtract)\
                    .then_inc(B2_DVE.sem, B2_DVE.step("diff"))
                after(B2_DVE, i, "topf")
                for k in range(2):
                    dve.tensor_tensor(hot[:, k, :, :], iota_e[:, :, :],
                                      top_f[:, :, k].unsqueeze(2).to_broadcast([P, 2, EXPERTS]), ALU.is_equal)\
                        .then_inc(B2_DVE.sem, B2_DVE.step(f"hot{k}"))
                after(B2_DVE, i, "hot1")
                dve.tensor_tensor(hots[:, :, :], hot[:, 0, :, :], hot[:, 1, :, :], ALU.add)\
                    .then_inc(B2_DVE.sem, B2_DVE.step("hots"))
                dve.tensor_tensor(lgm[:, :, :], lg[:, :, :], top8[:, :, 0:1].to_broadcast([P, 2, EXPERTS]),
                                  ALU.subtract).then_inc(B2_DVE.sem, B2_DVE.step("lgm"))

            def b_slots(i):
                dve.wait_ge(B2_PE.sem, B2_PE.at(i, "rank"))
                t = tB2
                dve.tensor_tensor(slot[:, :, :], t[:, 0:2 * EXPERTS].rearrange("p (a b) -> p a b", a=2),
                                  base[:, :].unsqueeze(1).to_broadcast([P, 2, EXPERTS]), ALU.add)\
                    .then_inc(B2_DVE.sem, B2_DVE.step("slot"))
                after(B2_DVE, i, "slot")
                for k in range(2):
                    dve.tensor_tensor(picked[:, k, :, :], hot[:, k, :, :], slot[:, :, :], ALU.mult)\
                        .then_inc(B2_DVE.sem, B2_DVE.step(f"pick{k}"))
                    after(B2_DVE, i, f"pick{k}")
                    dve.tensor_reduce(rec[:, 2 * k:2 * k + 2], picked[:, k, :, :], AX.X, ALU.add)\
                        .then_inc(B2_DVE.sem, B2_DVE.step(f"pos{k}"))
                dve.tensor_tensor(base[:, :], base[:, :], t[:, 2 * EXPERTS:3 * EXPERTS], ALU.add)\
                    .then_inc(B2_DVE.sem, B2_DVE.step("base"))
                after(B2_DVE, i, "pos1")
                dve.tensor_copy(slot_u[:, :], rec[:, 0:4]).then_inc(B2_DVE.sem, B2_DVE.step("slotu"))
                dve.tensor_copy(rec[:, 4:8].rearrange("p (k c) -> p c k", k=2), top_f[:, :, :])\
                    .then_inc(B2_DVE.sem, B2_DVE.step("recf"))
                after(B2_DVE, i, "recf")
                dve.tensor_copy(rec_all[:, bass.ds(i, 1), :].rearrange("p a r -> p (a r)"), rec[:, :])\
                    .then_inc(B2_DVE.sem, B2_DVE.step("rec"))

            def b_probs(i):
                dve.wait_ge(B2_ACT.sem, B2_ACT.at(i, "ex"))
                dve.tensor_reduce(exs[:, :], ex[:, :, :], AX.X, ALU.add).then_inc(B2_DVE.sem, B2_DVE.step("exs"))
                after(B2_DVE, i, "exs")
                dve.reciprocal(exr[:, :], exs[:, :]).then_inc(B2_DVE.sem, B2_DVE.step("exr"))
                after(B2_DVE, i, "exr")
                dve.tensor_tensor(prob[:, :, :], ex[:, :, :], exr[:, :].unsqueeze(2).to_broadcast([P, 2, EXPERTS]),
                                  ALU.mult).then_inc(B2_DVE.sem, B2_DVE.step("prob"))
                after(B2_DVE, i, "prob")
                dve.tensor_tensor(prob_sum[:, :, :], prob_sum[:, :, :], prob[:, :, :], ALU.add)\
                    .then_inc(B2_DVE.sem, B2_DVE.step("sum"))

            def body(i, a1, a2, b1, b2):
                a2(a_max, 0)
                a2(a_max, 1)
                b2(b_residual)
                a2(a_max, 2)
                a2(a_max, 3)
                b2(b_moments3)
                a2(a_max, 4)
                a2(a_max, 5)
                a1(a_xt)
                b2(b_normal3)
                a2(a_max, 6)
                a2(a_max, 7)
                b1(b_split_queries)
                a2(a_max, 8)
                a2(a_max, 9)
                b1(b_split_keys)
                a2(a_max, 10)
                a2(a_max, 11)
                a2(a_max_rows)
                a1(a_tokens)
                b1(b_max, 0)
                b1(b_max, 1)
                b2(b_choose)
                a1(a_mean)
                b1(b_max, 2)
                b1(b_max, 3)
                a1(a_var)
                a1(a_shift)
                b1(b_max, 4)
                b1(b_max, 5)
                b1(b_values, 0)
                a1(a_normal)
                b1(b_max, 6)
                b1(b_max, 7)
                b2(b_slots)
                b1(b_max, 8)
                b2(b_probs)
                b1(b_max, 9)
                a2(a_finish, 0)
                b1(b_max, 10)
                a2(a_finish, 1)
                b1(b_values, 1)
                b1(b_max, 11)
                a2(a_moments)
                a1(a_keys_and_query)
                b1(b_values, 2)
                a1(a_queries)
                a2(a_normal2)

            turns(dve, body)


def phase234(nc, ins, ps, xs, ys, h2d, out_rows, sb_top, sem, rec_all, base, prob_sum, valid, ones):
    ctx = ExitStack()
    with ctx:
        def sb(name, shape, dt=F32):
            return sb_top(name, shape, dt, ctx)

        w1_hi = sb("w1_hi", [P, EXPERTS, FFN], F32R)
        w1_lo = sb("w1_lo", [P, EXPERTS, FFN], F32R)
        w1_st = sb("w1_st", [P, EXPERTS, FFN], F32R)
        w2_hi = sb("w2_hi", [P, EXPERTS, FCH * DIM], F32R)
        w2_lo = sb("w2_lo", [P, EXPERTS, FCH * DIM], F32R)
        tile_expert = sb("tile_expert", [1, TILES], I32)
        tile_start = sb("tile_start", [1, TILES], I32)
        gate = sb("gate", [P, 2, IMAGES, 2])
        ident = sb("ident2", [P, P])

        phase2(nc, ins, ps, xs, sb_top, sem, rec_all, base, prob_sum, valid, ones, w1_hi, w1_lo, w1_st, w2_hi, w2_lo,
               tile_expert, tile_start, gate, ident)
        phase3(nc, ps, xs, ys, sb_top, sem, w1_hi, w1_lo, w1_st, w2_hi, w2_lo, tile_expert, tile_start, ident)
        phase4(nc, ys, h2d, out_rows, sb_top, sem, rec_all, gate)


def phase2(nc, ins, ps, xs, sb_top, sem, rec_all, base, prob_sum, valid, ones, w1_hi, w1_lo, w1_st, w2_hi, w2_lo,
           tile_expert, tile_start, gate, ident):
    ctx = ExitStack()
    with ctx:
        def sb(name, shape, dt=F32):
            return sb_top(name, shape, dt, ctx)

        raw1 = sb("raw1", [P, 2, FFN])
        raw1s = sb("raw1s", [P, 2, FFN])
        raw1h = sb("raw1h", [P, 2, FFN])
        raw2 = sb("raw2", [P, 2, FCH * DIM])
        neg_low_half = sb("neg_low_half", [P, 1])
        first_slot = sb("first_slot2", [P, EXPERTS])
        row_of = sb("row_of", [P, EXPERTS])
        tile_i = sb("tile_i", [1, TILES])
        zeros = sb("zeros", [P, DIM])
        pad_slot = sb("pad_slot", [P, EXPERTS], U32)
        importance = sb("importance", [P, EXPERTS])
        inv = sb("inv", [P, EXPERTS])
        count_i = sb("count_i", [P, EXPERTS], I32)
        tiles_of = sb("tiles_of", [P, EXPERTS])
        tiles_to = sb("tiles_to", [P, EXPERTS])
        no_e = sb("no_e", [P, EXPERTS])
        past = sb("past", [1, TILES, EXPERTS])
        past_n = sb("past_n", [1, TILES, EXPERTS])
        te = sb("te", [1, TILES])
        tu = sb("tu", [1, TILES])
        share = sb("share", [P, 2, IMAGES, 2])
        to_row = sb("to_row", [P, EXPERTS])
        one_e = sb("one_e", [P, IMAGES, 2])
        e2 = sb("e2", [P, IMAGES, 2])
        total = sb("total", [P, IMAGES, 2])

        const_in = sem("const_in")
        raw_in = [sem("raw_in_even"), sem("raw_in_odd")]
        hi_done = sem("hi_done")
        lo_done = sem("lo_done")
        sums_ready = sem("sums_ready")
        probs_ready = sem("probs_ready")
        chain = sem("dve_chain")
        pads_known = sem("pads_known")
        exp_ready = sem("exp_ready")
        zero_ready = sem("zero_ready")
        pads_out = sem("pads_out")

        block = ctx.enter_context(nc.Block())

        @block.sync
        def _(sp):
            for dst, name in ((neg_low_half, "neg_low_half"), (first_slot, "first_slot"), (row_of, "row_of"),
                              (tile_i, "tile_i"), (ident, "ident")):
                sp.dma_start(dst[:], ins[name][:]).then_inc(const_in, 16)
            for e in range(EXPERTS):
                if e >= 2:
                    sp.wait_ge(lo_done, 3 * (e - 1))
                s = raw_in[e % 2]
                sp.dma_start(raw1[:, e % 2, :], ins["w1"][0:P, e, :]).then_inc(s, 16)
                for half in range(2):
                    sp.dma_start(raw1s[64 * half:64 * half + 64, e % 2, :], ins["w1"][P:DIM, e, :]).then_inc(s, 16)
                sp.dma_start(raw2[:, e % 2, :], ins["w2"][:, e, :]).then_inc(s, 16)
            sp.wait_ge(raw_in[1], 64 * (EXPERTS // 2))

        @block.gpsimd
        def _(pool):
            pool.memset(zeros[:], 0.0).then_inc(zero_ready, 1)
            pool.wait_ge(zero_ready, 1)
            pool.wait_ge(pads_known, 1)
            for e in range(EXPERTS):
                pool.indirect_dma_start(out=xs[:, :],
                                        out_offset=bass.IndirectOffsetOnAxis(ap=pad_slot[:, e:e + 1], axis=0),
                                        in_=zeros[:, :], in_offset=None).then_inc(pads_out, 16)
            pool.wait_ge(pads_out, 16 * EXPERTS)

        @block.tensor
        def _(pe):
            pe.wait_ge(probs_ready, 1)
            pe.matmul(ps[:, 0, 0:2 * EXPERTS], ones[:, :], prob_sum[:, :, :].rearrange("p a b -> p (a b)"),
                      start=True, stop=True).then_inc(sums_ready, 1)

        @block.scalar
        def _(act):
            for e in range(EXPERTS):
                act.wait_ge(raw_in[e % 2], 64 * (e // 2 + 1))
                if e >= 2:
                    act.wait_ge(lo_done, 3 * (e - 1))
                act.copy(w1_hi[:, e, :], raw1[:, e % 2, :]).then_inc(hi_done, 1)
                act.copy(raw1h[:, e % 2, :].bitcast(F32R), raw1s[:, e % 2, :]).then_inc(hi_done, 1)
                act.copy(w2_hi[:, e, :], raw2[:, e % 2, :]).then_inc(hi_done, 1)
            act.activation(e2[:, :, :], rec_all[:, :, 8:10], ACT.Exp).then_inc(exp_ready, 1)

        @block.vector
        def _(dve):
            links = [0]

            def link(instruction):
                links[0] += 1
                instruction.then_inc(chain, 1)
                dve.wait_ge(chain, links[0])

            dve.wait_ge(const_in, 16 * 5)
            dve.tensor_tensor(pad_slot[:, :], base[:, :], row_of[:, :], ALU.add).then_inc(pads_known, 1)
            link(dve.tensor_tensor(no_e[:, :], base[:, :], first_slot[:, :], ALU.subtract))
            link(dve.tensor_scalar(count_i[:, :], no_e[:, :], float(P - 1), None, ALU.add))
            link(dve.tensor_scalar(count_i[:, :], count_i[:, :], P.bit_length() - 1, None, ALU.logical_shift_right))
            link(dve.tensor_copy(tiles_of[:, :], count_i[:, :]))
            link(dve.memset(no_e[:, :], 0.0))
            link(dve.tensor_tensor_scan(tiles_to[:, :], tiles_of[:, :], no_e[:, :], 0.0, ALU.add, ALU.add))
            link(dve.tensor_tensor(past[:, :, :], tile_i[:, :].unsqueeze(2).to_broadcast([1, TILES, EXPERTS]),
                                   tiles_to[0:1, :].unsqueeze(1).to_broadcast([1, TILES, EXPERTS]), ALU.is_ge))
            link(dve.tensor_reduce(te[:, :], past[:, :, :], AX.X, ALU.add))
            link(dve.tensor_tensor(past_n[:, :, :], past[:, :, :],
                                   tiles_of[0:1, :].unsqueeze(1).to_broadcast([1, TILES, EXPERTS]), ALU.mult))
            link(dve.tensor_reduce(tu[:, :], past_n[:, :, :], AX.X, ALU.add))
            link(dve.tensor_tensor(tu[:, :], tile_i[:, :], tu[:, :], ALU.subtract))
            link(dve.tensor_scalar(tu[:, :], tu[:, :], float(P), None, ALU.mult))
            link(dve.scalar_tensor_tensor(tile_start[:, :], te[:, :], float(CAP), tu[:, :], ALU.mult, ALU.add))
            link(dve.tensor_scalar(tile_expert[:, :], te[:, :], float(EXPERTS - 1), None, ALU.min))
            link(dve.tensor_tensor(no_e[:, :], tiles_to[:, :], tiles_of[:, :], ALU.subtract))
            link(dve.scalar_tensor_tensor(to_row[:, :], no_e[:, :], float(P), first_slot[:, :], ALU.mult, ALU.subtract))
            dve.tensor_tensor(prob_sum[:, :, :], prob_sum[:, :, :], valid[:, :, :], ALU.mult).then_inc(probs_ready, 1)
            dve.wait_ge(sums_ready, 1)
            link(dve.tensor_copy(importance[:, :], ps[:, 0, 0:EXPERTS]))
            link(dve.tensor_tensor(importance[:, :], ps[:, 0, EXPERTS:2 * EXPERTS], importance[:, :], ALU.add))
            link(dve.tensor_scalar(importance[:, :], importance[:, :], -1.0, float(np.float32(1.0 - 0.9)),
                                   ALU.add, ALU.mult))
            link(dve.tensor_scalar(importance[:, :], importance[:, :], 1.0, 0.01, ALU.add, ALU.add))
            link(dve.reciprocal(inv[:, :], importance[:, :]))
            link(dve.memset(share[:, :, :, :], 0.0))
            for e in range(EXPERTS):
                h = raw1h[:, e % 2, :]
                dve.wait_ge(hi_done, 3 * e + 1)
                dve.tensor_tensor(w1_lo[:, e, :], raw1[:, e % 2, :], w1_hi[:, e, :].bitcast(F32), ALU.subtract)\
                    .then_inc(lo_done, 1)
                dve.wait_ge(hi_done, 3 * e + 2)
                dve.scalar_tensor_tensor(w1_st[:, e, :], h, neg_low_half[:, 0:1], raw1s[:, e % 2, :],
                                         ALU.mult, ALU.add).then_inc(lo_done, 1)
                dve.wait_ge(hi_done, 3 * e + 3)
                dve.tensor_tensor(w2_lo[:, e, :], raw2[:, e % 2, :], w2_hi[:, e, :].bitcast(F32), ALU.subtract)\
                    .then_inc(lo_done, 1)
                for k in range(2):
                    link(dve.tensor_scalar(one_e[:, :, :], rec_all[:, :, 4 + 2 * k:6 + 2 * k], float(e),
                                           inv[:, e:e + 1], ALU.is_equal, ALU.mult))
                    link(dve.tensor_tensor(share[:, k, :, :], share[:, k, :, :], one_e[:, :, :], ALU.add))
                    link(dve.tensor_scalar(one_e[:, :, :], rec_all[:, :, 4 + 2 * k:6 + 2 * k], float(e),
                                           to_row[:, e:e + 1], ALU.is_equal, ALU.mult))
                    link(dve.tensor_tensor(rec_all[:, :, 2 * k:2 * k + 2], rec_all[:, :, 2 * k:2 * k + 2],
                                           one_e[:, :, :], ALU.add))
            dve.wait_ge(exp_ready, 1)
            link(dve.tensor_tensor(share[:, 1, :, :], share[:, 1, :, :], e2[:, :, :], ALU.mult))
            link(dve.tensor_tensor(total[:, :, :], share[:, 0, :, :], share[:, 1, :, :], ALU.add))
            link(dve.reciprocal(total[:, :, :], total[:, :, :]))
            for k in range(2):
                link(dve.tensor_tensor(gate[:, k, :, :], share[:, k, :, :], total[:, :, :], ALU.mult))


def phase3(nc, ps, xs, ys, sb_top, sem, w1_hi, w1_lo, w1_st, w2_hi, w2_lo, tile_expert, tile_start, ident):
    ctx = ExitStack()
    with ctx:
        def sb(name, shape, dt=F32):
            return sb_top(name, shape, dt, ctx)

        xt = sb("xt", [P, 2, 2 * P])
        x_hi = sb("x_hi", [P, 2, 2 * P], F32R)
        x_lo = sb("x_lo", [P, 2, 2 * P], F32R)
        hid = sb("hid", [P, 2, FFN])
        h_hi = sb("h_hi", [P, 2, FFN], F32R)
        h_lo = sb("h_lo", [P, 2, FFN], F32R)
        yt = sb("yt", [P, 2, DIM])

        xt_in = [sem("xt_in_even"), sem("xt_in_odd")]
        y_out = [sem("y_out_even"), sem("y_out_odd")]
        x_turned, up_done, h_turned, down_done = (sem(s) for s in ("x_turned", "up_done", "h_turned", "down_done"))
        x_hi_done, silu_done, h_hi_done = (sem(s) for s in ("x_hi_done", "silu_done", "h_hi_done"))
        x_lo_done, y_done, h_lo_done = (sem(s) for s in ("x_lo_done", "y_done", "h_lo_done"))

        def through(tile):
            return tile + 2

        def bank(kind, par):
            return ps[:, 2 * kind + par, :]

        def tiles(eng, slot):
            for n in range(3):
                slot(n, n % 2, n // 2)
            with eng.Fori(1, (TILES - 2) // 2) as i:
                known = slot(2 * i + 1, 1, i)
                if known is None:
                    slot(2 * i + 2, 0, i + 1)
                else:
                    slot(2 * i + 2, 0, i + 1, known)
            slot(TILES - 1, 1, TILES // 2 - 1)

        def first(n):
            return isinstance(n, int) and n == 0

        def last(n):
            return isinstance(n, int) and n == TILES - 1

        block = ctx.enter_context(nc.Block())

        @block.sync
        def _(sp):
            def load(n, par, turned=None):
                r = sp.value_load(tile_start[0:1, bass.ds(n, 1)], min_val=0, max_val=SLOTS - P)
                if turned is not None:
                    sp.wait_ge(x_turned, through(turned))
                sp.dma_start(xt[:, par, 0:DIM], xs[bass.ds(r, P), :]).then_inc(xt_in[par], 16)
                sp.dma_start(xt[:, par, DIM:2 * P], xs[bass.ds(r, P), P:DIM]).then_inc(xt_in[par], 16)

            load(0, 0)
            load(1, 1)
            with sp.Fori(0, (TILES - 2) // 2) as i:
                for par in range(2):
                    load(2 * i + 2 + par, par, turned=2 * i + par)

        @block.gpsimd
        def _(pool):
            for s in (x_turned, up_done, h_turned, down_done, x_hi_done, silu_done, h_hi_done, x_lo_done, y_done,
                      h_lo_done):
                pool.sem_inc(s, 1)
            with pool.Fori(0, TILES // 2) as i:
                for par in range(2):
                    n = 2 * i + par
                    pool.wait_ge(y_done, through(n))
                    pool.dma_start(ys[bass.ds(n * P, P), :], yt[:, par, :]).then_inc(y_out[par], 16)
            for s in y_out:
                pool.wait_ge(s, 16 * (TILES // 2))

        @block.tensor
        def _(pe):
            def turn_x(n, par, loads):
                pe.wait_ge(xt_in[par], 32 * loads + 32)
                if not first(n):
                    pe.wait_ge(x_lo_done, through(n - 2))
                pe.transpose(bank(0, par)[:, 0:P], xt[:, par, 0:P], ident[:, :])
                pe.transpose(bank(0, par)[:, P:2 * P], xt[:, par, P:2 * P], ident[:, :]).then_inc(x_turned, 1)

            def expert_of(n):
                return pe.value_load(tile_expert[0:1, bass.ds(n, 1)], min_val=0, max_val=EXPERTS - 1)

            def up(n, par, e):
                pe.wait_ge(x_lo_done, through(n))
                if not first(n):
                    pe.wait_ge(silu_done, through(n - 2))
                o = bank(1, par)[:, 0:FFN]

                def w(t, rows=P):
                    return t[0:rows, bass.ds(e, 1), :].rearrange("p a b -> p (a b)")

                pe.matmul(o, x_hi[:, par, 0:P], w(w1_hi), start=True, stop=False)
                pe.matmul(o, x_hi[:, par, 0:P], w(w1_lo), start=False, stop=False)
                pe.matmul(o, x_lo[:, par, 0:P], w(w1_hi), start=False, stop=False)
                pe.matmul(o, x_hi[:, par, P:2 * P], w(w1_st), start=False, stop=False)
                pe.matmul(o, x_lo[:, par, P:2 * P], w(w1_st), start=False, stop=True).then_inc(up_done, 1)

            def turn_h(n, par):
                pe.wait_ge(silu_done, through(n))
                if not first(n):
                    pe.wait_ge(h_lo_done, through(n - 2))
                for f in range(FCH):
                    mm = pe.transpose(bank(2, par)[:, f * P:(f + 1) * P], hid[:, par, f * P:(f + 1) * P], ident[:, :])
                mm.then_inc(h_turned, 1)

            def down(n, par, e):
                pe.wait_ge(h_lo_done, through(n))
                if not first(n):
                    pe.wait_ge(y_done, through(n - 2))
                o = bank(3, par)[:, 0:DIM]
                parts = [(h, w, f) for f in range(FCH) for h, w in ((h_hi, w2_hi), (h_hi, w2_lo), (h_lo, w2_hi))]
                for m, (h, w, f) in enumerate(parts):
                    mm = pe.matmul(o, h[:, par, f * P:(f + 1) * P],
                                   w[:, bass.ds(e, 1), f * DIM:(f + 1) * DIM].rearrange("p a b -> p (a b)"),
                                   start=(m == 0), stop=(m == len(parts) - 1))
                mm.then_inc(down_done, 1)

            def slot(n, par, pair, before=None):
                e = expert_of(n)
                up(n, par, e)
                if not last(n):
                    turn_x(n + 1, 1 - par, pair + 1 if par else pair)
                if not first(n):
                    down(n - 1, 1 - par, before if before is not None else expert_of(n - 1))
                turn_h(n, par)
                return e

            turn_x(0, 0, 0)
            tiles(pe, slot)
            down(TILES - 1, 1, expert_of(TILES - 1))

        @block.scalar
        def _(act):
            def high_x(n, par):
                act.wait_ge(x_turned, through(n))
                if not first(n):
                    act.wait_ge(up_done, through(n - 2))
                act.copy(x_hi[:, par, :], bank(0, par)[:, 0:2 * P]).then_inc(x_hi_done, 1)

            def slot(n, par, pair):
                act.wait_ge(up_done, through(n))
                if not first(n):
                    act.wait_ge(h_turned, through(n - 2))
                act.activation(hid[:, par, :], bank(1, par)[:, 0:FFN], ACT.Silu).then_inc(silu_done, 1)
                if not last(n):
                    high_x(n + 1, 1 - par)
                act.wait_ge(h_turned, through(n))
                if not first(n):
                    act.wait_ge(down_done, through(n - 2))
                act.copy(h_hi[:, par, :], bank(2, par)[:, 0:FFN]).then_inc(h_hi_done, 1)

            high_x(0, 0)
            tiles(act, slot)

        @block.vector
        def _(dve):
            def low_x(n, par):
                dve.wait_ge(x_hi_done, through(n))
                if not first(n):
                    dve.wait_ge(up_done, through(n - 2))
                dve.tensor_tensor(x_lo[:, par, :], bank(0, par)[:, 0:2 * P], x_hi[:, par, :].bitcast(F32), ALU.subtract)\
                    .then_inc(x_lo_done, 1)

            def output(n, par, stores):
                dve.wait_ge(down_done, through(n))
                if not (isinstance(stores, int) and stores <= 0):
                    dve.wait_ge(y_out[par], 16 * stores)
                dve.tensor_copy(yt[:, par, :], bank(3, par)[:, 0:DIM]).then_inc(y_done, 1)

            def slot(n, par, pair):
                if not last(n):
                    low_x(n + 1, 1 - par)
                if not first(n):
                    output(n - 1, 1 - par, pair if par else pair - 1)
                dve.wait_ge(h_hi_done, through(n))
                if not first(n):
                    dve.wait_ge(down_done, through(n - 2))
                dve.tensor_tensor(h_lo[:, par, :], bank(2, par)[:, 0:FFN], h_hi[:, par, :].bitcast(F32), ALU.subtract)\
                    .then_inc(h_lo_done, 1)

            low_x(0, 0)
            tiles(dve, slot)
            output(TILES - 1, 1, TILES // 2 - 1)


def phase4(nc, ys, h2d, out_rows, sb_top, sem, rec_all, gate):
    ctx = ExitStack()
    with ctx:
        def sb(name, shape, dt=F32):
            return sb_top(name, shape, dt, ctx)

        BUFS = 2
        held = sb("held4", [P, 1])
        slot_u = sb("slot_u4", [P, BUFS, 4], U32)
        y = sb("y4", [P, BUFS, 4, DIM])
        res = sb("res4", [P, BUFS, 2, DIM])
        o = sb("o4", [P, BUFS, 2, DIM])
        rows_in = [sem("rows_in_even"), sem("rows_in_odd")]
        res_in = [sem("res_in_even"), sem("res_in_odd")]
        out_done = [sem("out_done_even"), sem("out_done_odd")]
        slots_ready = sem("slots_ready")
        mixed = sem("mixed")
        MIX = 4

        block = ctx.enter_context(nc.Block())
        PAIRS_OF = IMAGES // 2

        @block.sync
        def _(sp):
            for s in out_done:
                sp.sem_inc(s, 32)

            def load(i, par):
                for c in range(2):
                    sp.dma_start(res[0:ROWS[c], par, c, :], h2d[bass.ds(i * SEQ + START[c], ROWS[c]), :])\
                        .then_inc(res_in[par], 16)

            load(0, 0)
            load(1, 1)
            with sp.Fori(0, PAIRS_OF - 1) as i:
                for par in range(2):
                    sp.wait_ge(mixed, MIX * (2 * i + par) + 3 * MIX)
                    load(2 * i + 2 + par, par)

        @block.scalar
        def _(act):
            with act.Fori(0, PAIRS_OF) as i:
                for par in range(2):
                    n = 2 * i + par
                    act.wait_ge(mixed, MIX * n + 3 * MIX)
                    for c in range(2):
                        act.dma_start(out_rows[bass.ds(n * SEQ + START[c], ROWS[c]), :], o[0:ROWS[c], par, c, :])\
                            .then_inc(out_done[par], 16)
            for s in out_done:
                act.wait_ge(s, 32 + 32 * PAIRS_OF)

        @block.gpsimd
        def _(pool):
            pool.sem_inc(mixed, 2 * MIX)
            with pool.Fori(0, PAIRS_OF) as i:
                for par in range(2):
                    n = 2 * i + par
                    pool.wait_ge(mixed, MIX * n + MIX)
                    pool.tensor_copy(slot_u[:, par, :],
                                     rec_all[:, bass.ds(n, 1), 0:4].rearrange("p a r -> p (a r)"))\
                        .then_inc(slots_ready, 1)
                    pool.wait_ge(slots_ready, n + 1)
                    pool.tensor_tensor(held[:, :], rec_all[:, 0, 8:9], rec_all[:, 0, 8:9], ALU.add)
                    for k in range(2):
                        for c in range(2):
                            m, r = 2 * k + c, ROWS[c]
                            pool.indirect_dma_start(
                                out=y[0:r, par, m, :], out_offset=None, in_=ys[:, :],
                                in_offset=bass.IndirectOffsetOnAxis(ap=slot_u[0:r, par, m:m + 1], axis=0))\
                                .then_inc(rows_in[par], 16)

        @block.vector
        def _(dve):
            with dve.Fori(0, PAIRS_OF) as i:
                for par in range(2):
                    n = 2 * i + par
                    dve.wait_ge(rows_in[par], 64 * i + 64)
                    dve.wait_ge(res_in[par], 32 * i + 32)
                    dve.wait_ge(out_done[par], 32 * i + 32)
                    for k in range(2):
                        for c in range(2):
                            r = ROWS[c]
                            if k:
                                dve.wait_ge(mixed, MIX * n + 2 * MIX + 1 + c)
                            dve.scalar_tensor_tensor(
                                o[0:r, par, c, :], y[0:r, par, 2 * k + c, :],
                                gate[0:r, k, bass.ds(n, 1), c:c + 1].rearrange("p a b -> p (a b)"),
                                o[0:r, par, c, :] if k else res[0:r, par, c, :], ALU.mult, ALU.add)\
                                .then_inc(mixed, 1)




def _layout(x):
    a = {k.replace("L0_", ""): np.asarray(v) for k, v in x.items()}
    f = np.float32
    o = {}
    o["x"] = np.ascontiguousarray(a["x"]).reshape(IMAGES, PATCHES, IN_DIM)
    o["wm"] = a["tok_W_map"].T.reshape(KCH, P, DIM).transpose(1, 0, 2)
    o["b_map"] = a["tok_b_map"][None]
    o["cls"] = a["tok_class_token"]
    o["ln_w"], o["ln_b"] = a["tok_ln_w"], a["tok_ln_b"]

    def columns(w):
        full = np.zeros((DIM, GROUPS, P), f)
        for h in range(HEADS):
            rows = slice(None) if w.shape[1] == DIM else slice(h * DH, (h + 1) * DH)
            for twice in range(2):
                at = 32 * (h % 4) + twice * DH
                full[rows, h // 4, at:at + DH] = w[h]
        return full

    for n, w in (("wq1", a["tok_Wq"]), ("wk1", a["tok_Wk"])):
        full = columns(w.transpose(0, 2, 1))
        both = full[:P].copy()
        both[0:DIM - P, 2, :] = full[P:, 2, :]
        o[n] = both
    for n, w in (("wq2", a["attn_Wq"]), ("wk2", a["attn_Wk"])):
        full = columns(w)
        o[n + "a"], o[n + "b"] = full[:P], full[P:]
    bd = np.zeros((DIM + 1, DIM), f)
    for h in range(HEADS):
        bd[h * DH:(h + 1) * DH, h * DH:(h + 1) * DH] = a["tok_Wv"][h].T
    bd[DIM] = a["tok_bv"].reshape(DIM)
    o["wv1a"], o["wv1b"] = bd[:P], bd[P:]
    wv = np.zeros((DIM + 1, DIM), f)
    wv[:DIM] = a["attn_Wv"].transpose(1, 0, 2).reshape(DIM, DIM)
    wv[DIM] = a["attn_bv"].reshape(DIM)
    o["wv2a"], o["wv2b"] = wv[:P], wv[P:]
    bias = np.zeros((P, 4, GROUPS), f)
    for j, n in enumerate(("tok_bq", "tok_bk", "attn_bq", "attn_bk")):
        for h in range(HEADS):
            for twice in range(2):
                at = 32 * (h % 4) + twice * DH
                bias[at:at + DH, j, h // 4] = a[n][h]
    o["bias"] = bias
    wo = np.zeros((P, GROUPS, DIM), f)
    for h in range(HEADS):
        wo[32 * (h % 4):32 * (h % 4) + DH, h // 4] = a["attn_Wo"][h * DH:(h + 1) * DH]
    o["wo"] = wo
    o["bo"] = a["attn_bo"][None]
    o["rw_a"], o["rw_b"] = a["ffn_router_w"].T[:P], a["ffn_router_w"].T[P:]
    o["w1"] = a["ffn_w1"].transpose(2, 0, 1)
    o["w2"] = a["ffn_w2"].transpose(0, 2, 1).reshape(EXPERTS, FCH, P, DIM).transpose(2, 0, 1, 3)\
        .reshape(P, EXPERTS, FCH * DIM)

    part, row = np.arange(P), np.arange(SEQ, dtype=f)[:, None]
    col = np.arange(DIM, dtype=f)[None]
    even = np.arange(DIM) % 2 == 0
    o["pos_emb"] = np.where(even, np.sin(row / np.power(f(10000), col / f(DIM))),
                            np.cos(row / np.power(f(10000), (col - f(1)) / f(DIM)))).astype(f)
    o["ident"] = np.eye(P, dtype=f)
    o["tri"] = (part[:, None] < part[None]).astype(f)
    sel = np.zeros((P, HEADS, P), f)
    for h in range(HEADS):
        sel[[h, HEADS + h], h] = 1
    o["sel"] = sel
    o["neg_lo"] = -(part[:, None] % 32 >= DH).astype(f)
    o["neg_low_half"] = -(part[:, None] >= DIM - P).astype(f)
    real = np.stack([part < ROWS[0], part < ROWS[1]], 1)[:, :, None]
    o["iota_e"] = np.where(real, np.arange(EXPERTS), -1).astype(f)
    o["valid"] = np.broadcast_to(real, (P, 2, EXPERTS)).astype(f)
    o["first_slot"] = np.broadcast_to(np.arange(EXPERTS) * CAP, (P, EXPERTS)).astype(f)
    o["row_of"] = np.broadcast_to(part[:, None], (P, EXPERTS)).astype(f)
    o["tile_i"] = np.arange(TILES, dtype=f)[None]
    return {k: np.ascontiguousarray(v) for k, v in o.items()}


def kernel(**inputs):
    import concourse.bacc as _bacc
    from concourse import mybir as _mybir
    from concourse.bass_utils import run_bass_kernel_spmd as _run

    nc = _bacc.Bacc("TRN2", target_bir_lowering=False, num_devices=1)
    arrays, ins = {}, {}
    for name, a in _layout(inputs).items():
        arrays[f"in_{name}"] = a
        ins[name] = nc.dram_tensor(f"in_{name}", a.shape, _mybir.dt.from_np(a.dtype), kind="ExternalInput").ap()
    out = nc.dram_tensor("out", (IMAGES, SEQ, DIM), F32, kind="ExternalOutput").ap()
    build(nc, ins, out)
    r = _run(nc, [arrays], core_ids=[0])
    return r.results[0]["out"]
```
